# Optimizing a Trainium2 kernel written in Bass

```python
import numpy as np
import jax
import jax.numpy as jnp

def _softmax(x, axis=-1):
    return jax.nn.softmax(x, axis=axis)

def _gelu(x):
    return jax.nn.gelu(x, approximate=True)

def _silu(x):
    return jax.nn.silu(x)

def _sigmoid(x):
    return jax.nn.sigmoid(x)

def _layernorm(x, axis=-1, eps=1e-05):
    m = jnp.mean(x, axis=axis, keepdims=True)
    v = jnp.var(x, axis=axis, keepdims=True)
    return (x - m) / jnp.sqrt(v + eps)

def _scatter_add(tgt, idx, src, axis=0):
    return tgt.at[idx].add(src)

def _segment_sum(src, seg, n):
    return jax.ops.segment_sum(src, seg, n)
kernel_name = 'mk_early_fusion_d2_tok_img768_r4_f39c64'

def setup_inputs(seed: int=0):
    np.random.seed(seed)
    _w = jnp.asarray

    def _rec_inputs():
        import jax
        import jax.numpy as jnp
        _rk = jax.random.key(seed)
        x = -0.000596345 + 1.00056 * jax.random.normal(jax.random.fold_in(_rk, 1), (2, 3, 64, 64), jnp.float32)
        txt = -0.000190561 + 0.886117 * jax.random.normal(jax.random.fold_in(_rk, 2), (2, 32, 192), jnp.float32)
        return (x, txt)
    x, txt = _rec_inputs()

    def _L0_tok_setup():
        import jax, jax.numpy as jnp
        import numpy as np
        B = 16
        IMG = 64
        CH = 3
        EMBED = 64
        GP = 16
        PRE = [1, 2, 4]
        N_LEVELS = 3
        FUSED = EMBED * N_LEVELS

        def hilbert_flat_indices(n):
            t = np.arange(n * n, dtype=np.int64)
            x = np.zeros(n * n, dtype=np.int64)
            y = np.zeros(n * n, dtype=np.int64)
            s = 1
            while s < n:
                rx = 1 & t // 2
                ry = 1 & (t ^ rx)
                swap = ry == 0
                flip = swap & (rx == 1)
                x = np.where(flip, s - 1 - x, x)
                y = np.where(flip, s - 1 - y, y)
                x2 = np.where(swap, y, x)
                y2 = np.where(swap, x, y)
                x, y = (x2, y2)
                x = x + s * rx
                y = y + s * ry
                t = t // 4
                s *= 2
            return y * n + x

        def _level(x, idx, W, b, p, gp):
            Bsz, C, H, _ = x.shape
            h = H // p
            t = x.reshape(Bsz, C, h, p, h, p).transpose(0, 2, 4, 3, 5, 1).reshape(Bsz, h * h, p * p * C)
            t = t[:, idx]
            t = t.reshape(Bsz, h * h // gp, gp * p * p * C)
            return t @ W.T + b

        def _interp_linear(x, n_out):
            L = x.shape[1]
            pos = (jnp.arange(n_out, dtype=jnp.float32) + 0.5) * (L / n_out) - 0.5
            pos = jnp.clip(pos, 0.0, L - 1)
            i0 = jnp.floor(pos).astype(jnp.int32)
            i1 = jnp.minimum(i0 + 1, L - 1)
            w = (pos - i0).astype(x.dtype)
            return x[:, i0] * (1.0 - w)[None, :, None] + x[:, i1] * w[None, :, None]
        key = jax.random.key(seed)
        ks = jax.random.split(key, 9)
        inp = {'x': jax.random.normal(ks[0], (B, CH, IMG, IMG), jnp.float32)}
        for i, p in enumerate(PRE):
            din = CH * p * p * GP
            inp[f'W{i}'] = jax.random.normal(ks[1 + 2 * i], (EMBED, din), jnp.float32) * din ** (-0.5)
            inp[f'b{i}'] = jax.random.normal(ks[2 + 2 * i], (EMBED,), jnp.float32) * 0.02
        inp['Wf'] = jax.random.normal(ks[7], (FUSED, FUSED), jnp.float32) * FUSED ** (-0.5)
        inp['bf'] = jax.random.normal(ks[8], (FUSED,), jnp.float32) * 0.02
        for i, p in enumerate(PRE):
            inp[f'idx{i}'] = jnp.asarray(hilbert_flat_indices(IMG // p), jnp.int32)
        return inp
    _L0_tok_all = _L0_tok_setup()
    _L0_tok_in = {k: v for k, v in _L0_tok_all.items() if k in ('W0', 'b0', 'W1', 'b1', 'W2', 'b2', 'Wf', 'bf', 'idx0', 'idx1', 'idx2')}
    del _L0_tok_all

    def _L0_attn_setup():
        import math
        import jax, jax.numpy as jnp
        import numpy as np
        D_MODEL = 192
        NUM_HEADS = 12
        NUM_KV_HEADS = 12
        FEATURE_DIM = 16
        HEAD_DIM = D_MODEL // NUM_KV_HEADS
        EPS = 1e-12
        R2 = math.sqrt(2.0)
        RD = math.sqrt(FEATURE_DIM)
        RRD = math.sqrt(RD)

        def taylor_exp(x):
            b, h, l, f = x.shape
            x2 = (x[..., :, None] * x[..., None, :]).reshape(b, h, l, f * f) / R2
            ones = jnp.ones((b, h, l, 1), dtype=x.dtype)
            return jnp.concatenate([ones, x / RRD, x2 / RD], axis=-1)
        key = jax.random.key(seed)
        k0, k1, k2, k3, k4 = jax.random.split(key, 5)
        B, L = (1, 128)
        hidden_states = jax.random.normal(k0, (B, L, D_MODEL), dtype=jnp.float32)
        s = 0.02
        Wq = jax.random.normal(k1, (FEATURE_DIM * NUM_HEADS, D_MODEL), dtype=jnp.float32) * s
        Wk = jax.random.normal(k2, (FEATURE_DIM * NUM_KV_HEADS, D_MODEL), dtype=jnp.float32) * s
        Wv = jax.random.normal(k3, (NUM_KV_HEADS * HEAD_DIM, D_MODEL), dtype=jnp.float32) * s
        Wo = jax.random.normal(k4, (D_MODEL, NUM_HEADS * HEAD_DIM), dtype=jnp.float32) * s
        return {'hidden_states': hidden_states, 'Wq': Wq, 'Wk': Wk, 'Wv': Wv, 'Wo': Wo}
    _L0_attn_all = _L0_attn_setup()
    _L0_attn_in = {k: v for k, v in _L0_attn_all.items() if k in ('Wq', 'Wk', 'Wv', 'Wo')}
    del _L0_attn_all

    def _L0_ffn_setup():
        import jax, jax.numpy as jnp
        import numpy as np
        B, T, H, F, E = (128, 32, 192, 768, 3)
        key = jax.random.key(seed)
        ks = jax.random.split(key, 4)
        s = 0.02
        return {'x': jax.random.normal(ks[0], (B, T, H), jnp.float32), 'Wg': jax.random.normal(ks[1], (E, H), jnp.float32) * s, 'W1': jax.random.normal(ks[2], (E, H, F), jnp.float32) * s, 'b1': jnp.zeros((E, F), jnp.float32), 'W2': jax.random.normal(ks[3], (E, F, H), jnp.float32) * s, 'b2': jnp.zeros((E, H), jnp.float32)}
    _L0_ffn_all = _L0_ffn_setup()
    _L0_ffn_in = {k: v for k, v in _L0_ffn_all.items() if k in ('Wg', 'W1', 'b1', 'W2', 'b2')}
    del _L0_ffn_all

    def _L1_attn_setup():
        import jax, jax.numpy as jnp
        import numpy as np
        B, S, E, H = (8, 256, 192, 12)
        SPARSITY = 0.4
        key = jax.random.key(seed)
        ks = jax.random.split(key, 5)
        return {'hidden_states': jax.random.normal(ks[0], (B, S, E), dtype=jnp.float32), 'W_qkv': jax.random.normal(ks[1], (E, 3 * E), dtype=jnp.float32) * E ** (-0.5), 'b_qkv': jax.random.normal(ks[2], (3 * E,), dtype=jnp.float32) * 0.02, 'W_proj': jax.random.normal(ks[3], (E, E), dtype=jnp.float32) * E ** (-0.5), 'b_proj': jax.random.normal(ks[4], (E,), dtype=jnp.float32) * 0.02}
    _L1_attn_all = _L1_attn_setup()
    _L1_attn_in = {k: v for k, v in _L1_attn_all.items() if k in ('W_qkv', 'b_qkv', 'W_proj', 'b_proj')}
    del _L1_attn_all

    def _L1_ffn_setup():
        import jax, jax.numpy as jnp
        import numpy as np
        B, S, H, D, E = (4, 512, 192, 256, 8)
        TOP_K = 2
        EPS = 1e-08
        LN_EPS = 1e-05

        def _gelu(t):
            return jax.nn.gelu(t, approximate=False)

        def _layer_norm(t, gamma, beta):
            mu = jnp.mean(t, axis=-1, keepdims=True)
            var = jnp.mean(jnp.square(t - mu), axis=-1, keepdims=True)
            return (t - mu) * jax.lax.rsqrt(var + LN_EPS) * gamma + beta
        key = jax.random.key(seed)
        ks = jax.random.split(key, 8)
        x = jax.random.normal(ks[0], (B, S, H), dtype=jnp.float32)
        w1 = jax.random.normal(ks[1], (H, H // 2), dtype=jnp.float32) * 0.02
        b1 = jnp.zeros((H // 2,), dtype=jnp.float32)
        w2 = jax.random.normal(ks[2], (H // 2, E), dtype=jnp.float32) * 0.02
        b2 = jnp.zeros((E,), dtype=jnp.float32)
        a_dn = float(np.sqrt(6.0 / (H + D)))
        a_up = float(np.sqrt(6.0 / (D + H)))
        down_w = jax.random.uniform(ks[3], (E, H, D), dtype=jnp.float32, minval=-a_dn, maxval=a_dn)
        down_b = jnp.zeros((E, D), dtype=jnp.float32)
        up_w = jax.random.uniform(ks[4], (E, D, H), dtype=jnp.float32, minval=-a_up, maxval=a_up)
        gamma = jnp.ones((H,), dtype=jnp.float32)
        beta = jnp.zeros((H,), dtype=jnp.float32)
        return {'x': x, 'w1': w1, 'b1': b1, 'w2': w2, 'b2': b2, 'down_w': down_w, 'down_b': down_b, 'up_w': up_w, 'gamma': gamma, 'beta': beta}
    _L1_ffn_all = _L1_ffn_setup()
    _L1_ffn_in = {k: v for k, v in _L1_ffn_all.items() if k in ('w1', 'b1', 'w2', 'b2', 'down_w', 'down_b', 'up_w', 'gamma', 'beta')}
    del _L1_ffn_all
    return {'x': x, 'txt': txt, 'L0_tok_W0': _L0_tok_in['W0'], 'L0_tok_b0': _L0_tok_in['b0'], 'L0_tok_W1': _L0_tok_in['W1'], 'L0_tok_b1': _L0_tok_in['b1'], 'L0_tok_W2': _L0_tok_in['W2'], 'L0_tok_b2': _L0_tok_in['b2'], 'L0_tok_Wf': _L0_tok_in['Wf'], 'L0_tok_bf': _L0_tok_in['bf'], 'L0_tok_idx0': _L0_tok_in['idx0'], 'L0_tok_idx1': _L0_tok_in['idx1'], 'L0_tok_idx2': _L0_tok_in['idx2'], 'L0_attn_Wq': _L0_attn_in['Wq'], 'L0_attn_Wk': _L0_attn_in['Wk'], 'L0_attn_Wv': _L0_attn_in['Wv'], 'L0_attn_Wo': _L0_attn_in['Wo'], 'L0_ffn_Wg': _L0_ffn_in['Wg'], 'L0_ffn_W1': _L0_ffn_in['W1'], 'L0_ffn_b1': _L0_ffn_in['b1'], 'L0_ffn_W2': _L0_ffn_in['W2'], 'L0_ffn_b2': _L0_ffn_in['b2'], 'L1_attn_W_qkv': _L1_attn_in['W_qkv'], 'L1_attn_b_qkv': _L1_attn_in['b_qkv'], 'L1_attn_W_proj': _L1_attn_in['W_proj'], 'L1_attn_b_proj': _L1_attn_in['b_proj'], 'L1_ffn_w1': _L1_ffn_in['w1'], 'L1_ffn_b1': _L1_ffn_in['b1'], 'L1_ffn_w2': _L1_ffn_in['w2'], 'L1_ffn_b2': _L1_ffn_in['b2'], 'L1_ffn_down_w': _L1_ffn_in['down_w'], 'L1_ffn_down_b': _L1_ffn_in['down_b'], 'L1_ffn_up_w': _L1_ffn_in['up_w'], 'L1_ffn_gamma': _L1_ffn_in['gamma'], 'L1_ffn_beta': _L1_ffn_in['beta']}

def reference(x, txt, L0_tok_W0, L0_tok_b0, L0_tok_W1, L0_tok_b1, L0_tok_W2, L0_tok_b2, L0_tok_Wf, L0_tok_bf, L0_tok_idx0, L0_tok_idx1, L0_tok_idx2, L0_attn_Wq, L0_attn_Wk, L0_attn_Wv, L0_attn_Wo, L0_ffn_Wg, L0_ffn_W1, L0_ffn_b1, L0_ffn_W2, L0_ffn_b2, L1_attn_W_qkv, L1_attn_b_qkv, L1_attn_W_proj, L1_attn_b_proj, L1_ffn_w1, L1_ffn_b1, L1_ffn_w2, L1_ffn_b2, L1_ffn_down_w, L1_ffn_down_b, L1_ffn_up_w, L1_ffn_gamma, L1_ffn_beta):
    import jax
    import jax.numpy as jnp

    def _L0_tok_ref(x, W0, b0, W1, b1, W2, b2, Wf, bf, idx0, idx1, idx2):
        import jax, jax.numpy as jnp
        import numpy as np
        B = 16
        IMG = 64
        CH = 3
        EMBED = 64
        GP = 16
        PRE = [1, 2, 4]
        N_LEVELS = 3
        FUSED = EMBED * N_LEVELS

        def hilbert_flat_indices(n):
            t = np.arange(n * n, dtype=np.int64)
            x = np.zeros(n * n, dtype=np.int64)
            y = np.zeros(n * n, dtype=np.int64)
            s = 1
            while s < n:
                rx = 1 & t // 2
                ry = 1 & (t ^ rx)
                swap = ry == 0
                flip = swap & (rx == 1)
                x = np.where(flip, s - 1 - x, x)
                y = np.where(flip, s - 1 - y, y)
                x2 = np.where(swap, y, x)
                y2 = np.where(swap, x, y)
                x, y = (x2, y2)
                x = x + s * rx
                y = y + s * ry
                t = t // 4
                s *= 2
            return y * n + x

        def _level(x, idx, W, b, p, gp):
            Bsz, C, H, _ = x.shape
            h = H // p
            t = x.reshape(Bsz, C, h, p, h, p).transpose(0, 2, 4, 3, 5, 1).reshape(Bsz, h * h, p * p * C)
            t = t[:, idx]
            t = t.reshape(Bsz, h * h // gp, gp * p * p * C)
            return t @ W.T + b

        def _interp_linear(x, n_out):
            L = x.shape[1]
            pos = (jnp.arange(n_out, dtype=jnp.float32) + 0.5) * (L / n_out) - 0.5
            pos = jnp.clip(pos, 0.0, L - 1)
            i0 = jnp.floor(pos).astype(jnp.int32)
            i1 = jnp.minimum(i0 + 1, L - 1)
            w = (pos - i0).astype(x.dtype)
            return x[:, i0] * (1.0 - w)[None, :, None] + x[:, i1] * w[None, :, None]
        Ws = [(idx0, W0, b0, PRE[0]), (idx1, W1, b1, PRE[1]), (idx2, W2, b2, PRE[2])]
        outs = [_level(x, idx, W, b, p, GP) for idx, W, b, p in Ws]
        n_tokens = outs[0].shape[1]
        outs = [outs[0]] + [_interp_linear(o, n_tokens) for o in outs[1:]]
        y = jnp.concatenate(outs, axis=-1)
        return y @ Wf.T + bf

    def _L0_attn_ref(hidden_states, Wq, Wk, Wv, Wo):
        import math
        import jax, jax.numpy as jnp
        import numpy as np
        D_MODEL = 192
        NUM_HEADS = 12
        NUM_KV_HEADS = 12
        FEATURE_DIM = 16
        HEAD_DIM = D_MODEL // NUM_KV_HEADS
        EPS = 1e-12
        R2 = math.sqrt(2.0)
        RD = math.sqrt(FEATURE_DIM)
        RRD = math.sqrt(RD)

        def taylor_exp(x):
            b, h, l, f = x.shape
            x2 = (x[..., :, None] * x[..., None, :]).reshape(b, h, l, f * f) / R2
            ones = jnp.ones((b, h, l, 1), dtype=x.dtype)
            return jnp.concatenate([ones, x / RRD, x2 / RD], axis=-1)
        b, l, _ = hidden_states.shape
        q = (hidden_states @ Wq.T).reshape(b, l, NUM_HEADS, FEATURE_DIM).transpose(0, 2, 1, 3)
        k = (hidden_states @ Wk.T).reshape(b, l, NUM_KV_HEADS, FEATURE_DIM).transpose(0, 2, 1, 3)
        v = (hidden_states @ Wv.T).reshape(b, l, NUM_KV_HEADS, HEAD_DIM).transpose(0, 2, 1, 3)
        q = taylor_exp(q)
        k = taylor_exp(k)
        kv = k[..., None, :] * v[..., :, None]
        kv = jnp.cumsum(kv, axis=2)
        num = jnp.einsum('bhlD,bhldD->bhld', q, kv)
        den = jnp.einsum('bhlD,bhlD->bhl', q, jnp.cumsum(k, axis=2)) + EPS
        y = num / den[..., None]
        y = y.transpose(0, 2, 1, 3).reshape(b, l, NUM_HEADS * HEAD_DIM)
        return y @ Wo.T

    def _L0_ffn_ref(x, Wg, W1, b1, W2, b2):
        import jax, jax.numpy as jnp
        import numpy as np
        B, T, H, F, E = (128, 32, 192, 768, 3)
        scores = jax.nn.softmax(jnp.mean(x, axis=1) @ Wg.T, axis=-1)
        _, idx = jax.lax.top_k(scores, 1)
        sel = idx[:, 0]
        h = jax.nn.gelu(jnp.einsum('bth,ehf->betf', x, W1) + b1[None, :, None, :], approximate=False)
        y = jnp.einsum('betf,efh->beth', h, W2) + b2[None, :, None, :]
        w = scores * jax.nn.one_hot(sel, E, dtype=scores.dtype)
        out = jnp.einsum('beth,be->bth', y, w)
        return out

    def _L1_attn_ref(hidden_states, W_qkv, b_qkv, W_proj, b_proj):
        import jax, jax.numpy as jnp
        import numpy as np
        B, S, E, H = (8, 256, 192, 12)
        SPARSITY = 0.4
        bsz, tgt_len, embed_dim = hidden_states.shape
        head_dim = embed_dim // H
        scale = head_dim ** (-0.5)
        qkv = (hidden_states @ W_qkv + b_qkv).reshape(bsz, tgt_len, 3, H, head_dim)
        qkv = qkv.transpose(2, 0, 3, 1, 4)
        q, k, v = (qkv[0], qkv[1], qkv[2])
        attn_weights = jnp.einsum('bhqd,bhkd->bhqk', q, k) * scale
        top_k = max(1, int(SPARSITY * tgt_len))
        top_k = min(top_k, tgt_len)
        kth = jax.lax.top_k(attn_weights, top_k)[0][..., -1:]
        min_val = jnp.finfo(attn_weights.dtype).min
        sparse_weights = jnp.where(attn_weights >= kth, attn_weights, min_val)
        attn = jax.nn.softmax(sparse_weights.astype(jnp.float32), axis=-1)
        attn = attn.astype(v.dtype)
        out = jnp.einsum('bhqk,bhkd->bqhd', attn, v).reshape(bsz, tgt_len, embed_dim)
        return out @ W_proj + b_proj

    def _L1_ffn_ref(x, w1, b1, w2, b2, down_w, down_b, up_w, gamma, beta):
        import jax, jax.numpy as jnp
        import numpy as np
        B, S, H, D, E = (4, 512, 192, 256, 8)
        TOP_K = 2
        EPS = 1e-08
        LN_EPS = 1e-05

        def _gelu(t):
            return jax.nn.gelu(t, approximate=False)

        def _layer_norm(t, gamma, beta):
            mu = jnp.mean(t, axis=-1, keepdims=True)
            var = jnp.mean(jnp.square(t - mu), axis=-1, keepdims=True)
            return (t - mu) * jax.lax.rsqrt(var + LN_EPS) * gamma + beta
        logits = _gelu(x @ w1 + b1) @ w2 + b2
        routing = jax.nn.softmax(logits, axis=-1)
        topv, topi = jax.lax.top_k(routing, TOP_K)
        sparse = jnp.sum(jax.nn.one_hot(topi, E, dtype=routing.dtype) * topv[..., None], axis=-2)
        sparse = sparse / (jnp.sum(sparse, axis=-1, keepdims=True) + EPS)
        z = _gelu(jnp.einsum('bsh,ehd->bsed', x, down_w) + down_b)
        expert_out = jnp.einsum('bsed,edh->bseh', z, up_w)
        moe_out = jnp.einsum('bseh,bse->bsh', expert_out, sparse)
        return _layer_norm(x + moe_out, gamma, beta)
    h = _L0_tok_ref(x, L0_tok_W0, L0_tok_b0, L0_tok_W1, L0_tok_b1, L0_tok_W2, L0_tok_b2, L0_tok_Wf, L0_tok_bf, L0_tok_idx0, L0_tok_idx1, L0_tok_idx2)
    h = jnp.concatenate([h, txt], axis=1)
    h = h + _L0_attn_ref(_layernorm(h, axis=-1), L0_attn_Wq, L0_attn_Wk, L0_attn_Wv, L0_attn_Wo)
    h = h + _L0_ffn_ref(_layernorm(h, axis=-1), L0_ffn_Wg, L0_ffn_W1, L0_ffn_b1, L0_ffn_W2, L0_ffn_b2)
    h = h + _L1_attn_ref(_layernorm(h, axis=-1), L1_attn_W_qkv, L1_attn_b_qkv, L1_attn_W_proj, L1_attn_b_proj)
    h = h + _L1_ffn_ref(_layernorm(h, axis=-1), L1_ffn_w1, L1_ffn_b1, L1_ffn_w2, L1_ffn_b2, L1_ffn_down_w, L1_ffn_down_b, L1_ffn_up_w, L1_ffn_gamma, L1_ffn_beta)
    return h

_drawn_inputs = setup_inputs


def setup_inputs(seed=0):
    import zlib

    import numpy as np

    out = dict(_drawn_inputs(seed))
    spreads = {'L0_ffn_b1': (0.0, 0.294),
     'L0_ffn_b2': (0.0, 0.1),
     'L1_ffn_b1': (0.0, 0.1),
     'L1_ffn_b2': (0.0, 0.1),
     'L1_ffn_down_b': (0.0, 0.299),
     'L1_ffn_gamma': (1.0, 0.2),
     'L1_ffn_beta': (0.0, 0.1)}
    factors = {'L0_attn_Wq': 8.0, 'L0_attn_Wk': 15.432, 'L0_ffn_Wg': 22.909, 'L0_tok_b1': 2.95}
    for name, (base, spread) in spreads.items():
        noise = np.random.default_rng([zlib.crc32(name.encode()), seed]).standard_normal(out[name].shape)
        drawn = base * np.exp(spread * noise) if base else spread * noise
        out[name] = jnp.asarray(drawn.astype(out[name].dtype))
    for name, factor in factors.items():
        out[name] = (out[name] * factor).astype(out[name].dtype)
    return out
```

```python
from contextlib import ExitStack

import concourse.bass as bass
from concourse import mybir

F32 = mybir.dt.float32
I32 = mybir.dt.int32
U32 = mybir.dt.uint32
ALU = mybir.AluOpType
ACT = mybir.ActivationFunctionType
AX = mybir.AxisListType

NB = 2
P = 128
IMG, TXT = 256, 32
T = IMG + TXT
TP = 3 * P
SIZES = (P, P, TXT)
D = 192
HF = D // 2
NH, HD = 12, 16
HPG = 4
NG = NH // HPG
VW = HD + 1
F0 = 768
NF = F0 // P
E0 = 3
E1, D1 = 8, 256
G1 = 96
TOPK = 115
KEYW = (T, T - P, TXT)
KEYAT = (0, T, 2 * T - P)
CAUSAL = sum(KEYW)
TILES = 2 * NH + NG
SW = T + 2
TINY = 2.0 ** -40
RING = 6
PMR = 3


def tile_heads():
    out = []
    for g in range(NG):
        for hh in range(HPG):
            out += [(g, hh, 0), (g, hh, 1)]
        out.append((g, None, 2))
    return out


class Ring:

    def __init__(self):
        self.uses = {}

    def add(self, *key):
        n = len(self.uses)
        self.uses[key] = (n % RING, n // RING)


def plan_banks():
    r = Ring()
    r.add("t1")
    r.add("t2")
    r.add("o1")
    r.add("o2")
    for gh in range(2):
        r.add("t0", gh)
        for b in range(NB):
            r.add("y", gh, b)
        for b in range(NB):
            r.add("h", gh, b)

    def norm_in(i, b):
        r.add("xt", i, b, 0)
        r.add("xt", i, b, 1)

    def qkv(i, b):
        for j in range(2 * NG):
            r.add("qk", i, b, j)
        r.add("v", i, b, 0)
        r.add("v", i, b, 1)

    def proj(i, b):
        for n in range(2):
            r.add("yt", i, b, n)
        for n in range(2):
            r.add("o", i, b, n)

    for b in range(NB):
        norm_in(0, b)
    for b in range(NB):
        qkv(0, b)
        for h in range(NH):
            r.add("s0", b, h)
        proj(0, b)
    for b in range(NB):
        norm_in(1, b)
        r.add("xsum", 1, b)
        r.add("logits0", b)
    for b in range(NB):
        r.add("gate0", b)
    for b in range(NB):
        for f in range(NF):
            r.add("up0", b, f)
        r.add("down0", b, 0)
        r.add("down0", b, 1)
    for b in range(NB):
        norm_in(2, b)
        r.add("xsum", 2, b)
        qkv(1, b)
        for t in range(TILES):
            r.add("s1", b, t)
    for b in range(NB):
        for t in range(TILES):
            r.add("pt", b, t)
        proj(1, b)
    for b in range(NB):
        norm_in(3, b)
        r.add("g1", b)
        r.add("logits1", b)
    for b in range(NB):
        for e in range(E1):
            r.add("z", b, e, 0)
            r.add("z", b, e, 1)
            r.add("up1", b, e, 0)
            r.add("up1", b, e, 1)
    return r.uses


def fusion_program(nc, a, out):
    USES = plan_banks()
    ctx = ExitStack()
    with ctx:
        def sb(name, shape, dt=F32):
            return ctx.enter_context(nc.sbuf_tensor(name, shape, dt))

        sems = {}

        def sem(*name):
            if name not in sems:
                sems[name] = ctx.enter_context(nc.semaphore("_".join(map(str, name))))
            return sems[name]

        ident = sb("ident", [P, P])
        ones_row = sb("ones_row", [1, P])
        ones_col = sb("ones_col", [P, 1])
        eps_col = sb("eps_col", [P, 1])
        mask = sb("mask", [P, CAUSAL])
        iota8 = sb("iota8", [P, E1])
        idx = sb("idx", [P, 42], I32)
        w_tok0 = sb("w_tok0", [48, 64])
        w_tok1 = sb("w_tok1", [96, 2, 64])
        w_tok2 = sb("w_tok2", [96, 8, 64])
        b_tok01 = sb("b_tok01", [P, 1])
        b_tok2 = sb("b_tok2", [64, 1])
        wf_a = sb("wf_a", [P, D])
        wf_b = sb("wf_b", [64, D])
        bf_row = sb("bf_row", [1, D])
        interp1 = sb("interp1", [64, IMG])
        interp2 = sb("interp2", [16, IMG])
        w_qk = [sb(f"w_qk{i}", [HF, 2, 2 * NG, P]) for i in range(2)]
        w_v = [sb(f"w_v{i}", [HF, 2, D]) for i in range(2)]
        w_o = [sb(f"w_o{i}", [HF, 2, D]) for i in range(2)]
        b_qk = sb("b_qk", [P, 2 * NG])
        b_q = sb("b_q", [P, NG])
        b_v = sb("b_v", [1, D])
        b_o = sb("b_o", [1, D])
        w_g0 = sb("w_g0", [HF, 2, E0])
        b_up0 = sb("b_up0", [P, NB, NF])
        b_dn0 = sb("b_dn0", [1, NB, D])
        w_g1 = sb("w_g1", [HF, 2, G1])
        b_g1 = sb("b_g1", [G1, 1])
        w_l1 = sb("w_l1", [G1, E1])
        b_l1 = sb("b_l1", [1, E1])
        w_z = sb("w_z", [HF, E1, 2, D1])
        b_z = sb("b_z", [P, E1, 2])
        w_u = sb("w_u", [P, E1, 2, D])
        gamma = sb("gamma", [P, D])
        beta = sb("beta", [P, D])

        pool_sb = sb("score_store", [P, NB, TILES * SW])
        scores = pool_sb[:].rearrange("p b (t n) -> p b t n", t=TILES)
        used = [0, 0]

        def share(b, parts, *shape):
            n = 1
            for k in shape:
                n *= k
            at = used[b]
            used[b] += n
            assert used[b] <= TILES * SW
            letters = "abc"[0:len(shape)]
            return pool_sb[0:parts, b, at:at + n].rearrange(
                f"p ({' '.join(letters)}) -> p {' '.join(letters)}", **dict(zip(letters, shape)))

        w_up0 = [share(1, HF, 2, F0) for _ in range(NB)]
        hid0 = [share(1, P, NF, T) for _ in range(NB)]
        w_dn0 = [share(0, P, NF, D) for _ in range(NB)]
        sq = share(0, P, PMR, CAUSAL)
        pm = share(0, P, PMR, CAUSAL)
        patch0 = sb("patch0", [P, 2, 16, NB * 3])
        patch1 = sb("patch1", [P, 8, NB * 12])
        patch2 = sb("patch2", [P, 2, NB * 48])
        seq0 = sb("seq0", [P, 2, NB, 48])
        seq1 = sb("seq1", [P, NB, 96])
        seq2 = sb("seq2", [P, NB, 96])
        t0 = sb("t0", [48, 2, NB, P])
        t1 = sb("t1", [96, NB, 2, 64])
        t2 = sb("t2", [96, NB, 8, 16])
        o1 = sb("o1", [64, NB, 64])
        o2 = sb("o2", [16, NB, 64])
        y_a = sb("y_a", [P, NB, P])
        y_b = sb("y_b", [64, NB, P])
        resid = sb("resid", [P, NB, 3, D])
        stats = sb("stats", [P, NB, 3, 6])
        moments = sb("moments", [P, NB, 3, 2])
        std = sb("std", [P, NB, 3])
        rstd = sb("rstd", [P, NB, 3])
        xhat = sb("xhat", [P, NB, 3, D])
        xT = sb("xT", [HF, NB, 2, TP])
        qk = sb("qk", [P, NB, 2 * NG, TP])
        vals = sb("vals", [P, NB, 3, NH, VW])
        den = sb("den", [P, 3, NH])
        rden = sb("rden", [P, 3, NH])
        att = sb("att", [P, NB, 3, D])
        attT = sb("attT", [HF, NB, 2, TP])
        lg0 = sb("lg0", [1, NB, 8])
        top0 = sb("top0", [1, NB, 8])
        arg0 = sb("arg0", [1, NB, 8], U32)
        neg0 = sb("neg0", [1, NB])
        exp0 = sb("exp0", [1, NB, E0])
        sum0 = sb("sum0", [1, NB])
        wt0 = sb("wt0", [1, NB])
        wcol0 = sb("wcol0", [P, NB])
        xmean = sb("xmean", [HF, NB, 2])
        smax = sb("smax", [P, NB, TILES])
        nbias = sb("nbias", [P, NB, TILES])
        thr = sb("thr", [P, NB, TILES])
        work = sb("work", [P, 2, T])
        top8 = sb("top8", [P, 8])
        es = sb("es", [P, PMR, T])
        ps = sb("ps", [P, PMR, TP])
        psT = sb("psT", [P, PMR, TP])
        gT = sb("gT", [G1, NB, TP])
        lg1 = sb("lg1", [P, NB, 3, E1])
        max1 = sb("max1", [P, NB, 3])
        e1 = sb("e1", [P, NB, 3, E1])
        z1 = sb("z1", [P, NB, 3])
        top1 = sb("top1", [P, NB, 3, 8])
        arg1 = sb("arg1", [P, NB, 3, 8], U32)
        arg1f = sb("arg1f", [P, NB, 3, 2])
        hit = sb("hit", [P, NB, 2, 3, E1])
        w1 = sb("w1", [P, NB, 3, E1])
        s1 = sb("s1", [P, NB, 3])
        zT = psT[:].rearrange("p r n -> p (r n)")[:, 0:4 * T].rearrange("p (r c n) -> p r c n", r=2, c=2)
        acc = xhat
        fin = att

        banks = ctx.enter_context(nc.psum_tensor("banks", [P, 8, 512], F32))
        y01 = banks[:, 6, 0:2 * NH * VW].rearrange("p (c h w) -> p c h w", c=2, h=NH)
        y2 = banks[0:TXT, 7, 0:NH * VW].rearrange("p (h w) -> p h w", h=NH)
        bank_full = [sem("bank_full", k) for k in range(RING)]
        bank_free = [sem("bank_free", k) for k in range(RING)]

        def filled(eng, *key):
            k, n = USES[key]
            eng.wait_ge(bank_full[k], n + 1)
            return banks[:, k, :]

        def emptied(eng, *key):
            k, n = USES[key]
            eng.wait_ge(bank_free[k], n + 1)

        def free_of(*key):
            return bank_free[USES[key][0]]

        block = ctx.enter_context(nc.Block())

        LOADS = [
            ("idx", [(idx, "idx")]),
            ("tok", [(w_tok1, "w_tok1"), (w_tok2, "w_tok2"), (w_tok0, "w_tok0"), (interp1, "interp1"),
                     (interp2, "interp2"), (b_tok01, "b_tok01"), (b_tok2, "b_tok2"), (wf_a, "wf_a"),
                     (wf_b, "wf_b"), (bf_row, "bf_row")]),
            ("att0", [(w_qk[0], "w_qk0"), (w_v[0], "w_v0"), (w_o[0], "w_o0"), (mask, "mask")]),
            ("ffn0", [(w_g0, "w_g0")]),
            ("att1", [(w_qk[1], "w_qk1"), (w_v[1], "w_v1"), (w_o[1], "w_o1"), (b_qk, "b_qk"),
                      (b_v, "b_v"), (b_o, "b_o")]),
            ("ffn1", [(w_g1, "w_g1"), (b_g1, "b_g1"), (w_l1, "w_l1"), (b_l1, "b_l1"), (w_z, "w_z"),
                      (b_z, "b_z"), (w_u, "w_u"), (gamma, "gamma"), (beta, "beta"), (iota8, "iota8")]),
        ]
        N_LOADS = {k: 16 * len(v) for k, v in LOADS}

        def loaded(eng, group):
            eng.wait_ge(sem("loaded", group), N_LOADS[group])

        @block.sync
        def _(sp):
            for group, items in LOADS:
                for dst, name in items:
                    sp.dma_start(dst[:], a[name]).then_inc(sem("loaded", group), 16)
                if group == "idx":
                    sp.wait_ge(sem("resid_zero"), 1)
                    for b in range(NB):
                        sp.dma_start(resid[0:TXT, b, 2, :], a["txt"][b]).then_inc(sem("text_in"), 16)
            for b in range(NB):
                sp.wait_ge(sem("expert_known", b), 1)
                e = sp.value_load(arg0[0:1, b, 0:1], min_val=0, max_val=E0 - 1)
                one = bass.ds(e, 1)
                done = sem("expert_in", b)
                sp.dma_start(w_up0[b], a["w_up0"][one, :, :, :].rearrange("e p c n -> (e p) c n")).then_inc(done, 16)
                sp.dma_start(b_up0[:, b, :], a["b_up0"][one, :, :].rearrange("e p n -> (e p) n")).then_inc(done, 16)
                sp.dma_start(w_dn0[b], a["w_dn0"][one, :, :, :].rearrange("e p c n -> (e p) c n")).then_inc(done, 16)
                sp.dma_start(b_dn0[:, b, :], a["b_dn0"][one, :]).then_inc(done, 16)
            for b in range(NB):
                sp.wait_ge(sem("fin_ready", b), 1)
                sp.dma_start(out[b, 0:IMG, :].rearrange("(c p) d -> p c d", p=P), fin[:, b, 0:2, :]).then_inc(sem("stored"), 16)
                sp.dma_start(out[b, IMG:T, :], fin[0:TXT, b, 2, :]).then_inc(sem("stored"), 16)
            sp.wait_ge(sem("stored"), 64)

        @block.gpsimd
        def _(pool):
            pool.memset(resid[:, :, 2, :], 0.0).then_inc(sem("resid_zero"), 1)
            pool.memset(ident[:], 0.0).then_inc(sem("ident"), 1)
            pool.wait_ge(sem("ident"), 1)
            pool.affine_select(out=ident[:], in_=ident[:], compare_op=ALU.not_equal, fill=1.0, base=0,
                               pattern=[[-1, P]], channel_multiplier=1).then_inc(sem("ident"), 1)
            loaded(pool, "idx")

            def gather(dst, src, col, done):
                pool.indirect_dma_start(out=dst, out_offset=None, in_=src,
                                        in_offset=bass.IndirectOffsetOnAxis(ap=idx[:, col:col + 1], axis=0)).then_inc(done, 16)

            for k in range(8):
                gather(patch1[:, k, :], a["x1"], 32 + k, sem("patch1_in"))
            for k in range(2):
                gather(patch2[:, k, :], a["x2"], 40 + k, sem("patch2_in"))
            for gh in range(2):
                for s in range(16):
                    gather(patch0[:, gh, s, :], a["x0"], 16 * gh + s, sem("patch0_in", gh))

        @block.scalar
        def _(act):
            def out_of(ins, *key):
                ins.then_inc(free_of(*key), 1)

            emptied_o2 = filled(act, "o2")
            out_of(act.activation(o2[:].rearrange("p b n -> p (b n)"), emptied_o2[0:16, 0:NB * 64], ACT.Copy), "o2")
            for gh in range(2):
                pt = filled(act, "t0", gh)
                out_of(act.activation(t0[:, gh, :, :].rearrange("p b n -> p (b n)"), pt[0:48, 0:NB * P], ACT.Copy), "t0", gh)
                for b in range(NB):
                    py = filled(act, "y", gh, b)
                    if gh:
                        act.wait_ge(sem("y_used"), b + 1)
                    act.activation(y_a[:, b, :], py[:, 0:P], ACT.Identity, bias=b_tok01[:, 0:1]).then_inc(sem("y_a_ready"), 1)
                    out_of(act.activation(y_b[:, b, :], py[0:64, P:2 * P], ACT.Identity, bias=b_tok2[:, 0:1]), "y", gh, b)

            def norm_std(i, b):
                act.wait_ge(sem("moments_ready", i, b), 3)
                act.activation(std[:, b, :], moments[:, b, :, 1], ACT.Sqrt, bias=eps_col[:, 0:1]).then_inc(sem("std_ready", i, b), 1)

            def norm_out(i, b):
                px = filled(act, "xt", i, b, 0)
                out_of(act.activation(xT[:, b, 0, :], px[0:HF, 0:TP], ACT.Copy), "xt", i, b, 0)

            def att_out(i, b):
                px = filled(act, "yt", i, b, 0)
                out_of(act.activation(attT[:, b, 0, :], px[0:HF, 0:TP], ACT.Copy), "yt", i, b, 0)

            act.wait_ge(sem("eps_set"), 1)
            for b in range(NB):
                norm_std(0, b)
            for b in range(NB):
                norm_out(0, b)
            for b in range(NB):
                for j in range(0, 2 * NG, 2):
                    p = filled(act, "qk", 0, b, j)
                    out_of(act.activation(qk[:, b, j, 0:T], p[:, 0:T], ACT.Copy), "qk", 0, b, j)
                for h in range(NH):
                    n = b * NH + h
                    p = filled(act, "s0", b, h)
                    if n >= PMR:
                        act.wait_ge(sem("pm_ready"), n - PMR + 1)
                    out_of(act.activation(sq[:, n % PMR, :], p[:, 0:CAUSAL], ACT.Square, scale=0.25, bias=ones_col[:, 0:1]), "s0", b, h)
                att_out(0, b)
            for b in range(NB):
                norm_std(1, b)
            for b in range(NB):
                norm_out(1, b)
            for b in range(NB):
                act.wait_ge(sem("expert_known", b), 1)
                act.activation(exp0[:, b, :], lg0[:, b, 0:E0], ACT.Exp, bias=neg0[:, b:b + 1],
                               accum_out=sum0[:, b:b + 1]).then_inc(sem("sum0_ready", b), 1)
            for b in range(NB):
                act.wait_ge(sem("expert_in", b), 64)
                for f in range(NF):
                    p = filled(act, "up0", b, f)
                    out_of(act.activation(hid0[b][:, f, :], p[:, 0:T], ACT.Gelu, bias=b_up0[:, b, f:f + 1]), "up0", b, f)
            for b in range(NB):
                norm_std(2, b)
            act.wait_ge(sem("b_q_ready"), 1)
            for b in range(NB):
                norm_out(2, b)
                for j in range(NG):
                    p = filled(act, "qk", 1, b, j)
                    out_of(act.activation(qk[:, b, j, 0:T], p[:, 0:T], ACT.Identity, scale=0.25 * TINY,
                                          bias=b_q[:, j:j + 1]), "qk", 1, b, j)
                for t in range(TILES):
                    p = filled(act, "s1", b, t)
                    out_of(act.activation(scores[:, b, t, 0:T + 1], p[:, 0:T + 1], ACT.Copy), "s1", b, t)
            for b in range(NB):
                act.wait_ge(sem("nbias_ready", b), 1)

                def exp_tile(t):
                    n = b * TILES + t
                    if n >= PMR:
                        act.wait_ge(sem("ps_ready"), n - PMR + 1)
                    act.activation(es[:, n % PMR, :], scores[:, b, t, 0:T], ACT.Exp, scale=1.0 / TINY,
                                   bias=nbias[:, b, t:t + 1]).then_inc(sem("es_ready"), 1)

                def turn_tile(t):
                    n = b * TILES + t
                    p = filled(act, "pt", b, t)
                    if n >= PMR:
                        act.wait_ge(sem("psT_used"), n - PMR + 1)
                    out_of(act.activation(psT[:, n % PMR, :], p[:, 0:TP], ACT.Copy), "pt", b, t)

                for t in range(TILES + 2):
                    if t < TILES:
                        exp_tile(t)
                    if t >= 2:
                        turn_tile(t - 2)
                att_out(1, b)
            for b in range(NB):
                norm_std(3, b)
            for b in range(NB):
                norm_out(3, b)
                p = filled(act, "g1", b)
                out_of(act.activation(gT[:, b, 0:T], p[0:G1, 0:T], ACT.Gelu, bias=b_g1[:, 0:1]), "g1", b)
            for b in range(NB):
                emptied(act, "logits1", b)
                act.activation(e1[:, b, :, :], lg1[:, b, :, :], ACT.Exp).then_inc(sem("e1_ready", b), 1)
            for b in range(NB):
                for e in range(E1):
                    n = b * E1 + e
                    for c in range(2):
                        p = filled(act, "z", b, e, c)
                        if n >= 2:
                            filled(act, "up1", *divmod(n - 2, E1), 1)
                        out_of(act.activation(zT[:, n % 2, c, :], p[:, 0:T], ACT.Gelu, bias=b_z[:, e, c:c + 1]), "z", b, e, c)
            for b in range(NB):
                norm_std(4, b)

        @block.tensor
        def _(pe):
            def bank(*key):
                k, n = USES[key]
                if n:
                    pe.wait_ge(bank_free[k], n)
                return banks[:, k, :]

            def full(mm, *key):
                mm.then_inc(bank_full[USES[key][0]], 1)

            pe.wait_ge(sem("ident"), 2)
            pe.wait_ge(sem("seq1_ready"), 1)
            p = bank("t1")
            for b in range(NB):
                mm = pe.transpose(p[0:96, b * P:(b + 1) * P], seq1[:, b, :], ident[:])
            full(mm, "t1")
            pe.wait_ge(sem("seq2_ready"), 1)
            p = bank("t2")
            for b in range(NB):
                mm = pe.transpose(p[0:96, b * P:(b + 1) * P], seq2[:, b, :], ident[:])
            full(mm, "t2")
            loaded(pe, "tok")
            emptied(pe, "t1")
            p = bank("o1")
            for b in range(NB):
                for k in range(2):
                    mm = pe.matmul(p[0:64, b * 64:b * 64 + 64], t1[:, b, k, :], w_tok1[:, k, :], start=(k == 0), stop=(k == 1))
            full(mm, "o1")
            emptied(pe, "t2")
            p = bank("o2")
            for b in range(NB):
                for k in range(8):
                    mm = pe.matmul(p[0:16, b * 64:b * 64 + 64], t2[:, b, k, :], w_tok2[:, k, :], start=(k == 0), stop=(k == 7))
            full(mm, "o2")
            emptied(pe, "o1")
            emptied(pe, "o2")
            pe.wait_ge(sem("ones_set"), 1)
            for gh in range(2):
                half = slice(gh * P, gh * P + P)
                pe.wait_ge(sem("seq0_ready"), gh + 1)
                p = bank("t0", gh)
                for b in range(NB):
                    mm = pe.transpose(p[0:48, b * P:(b + 1) * P], seq0[:, gh, b, :], ident[:])
                full(mm, "t0", gh)
                emptied(pe, "t0", gh)
                for b in range(NB):
                    p = bank("y", gh, b)
                    pe.matmul(p[0:64, 0:P], w_tok0[:], t0[:, gh, b, :], start=True, stop=True)
                    pe.matmul(p[64:128, 0:P], o1[:, b, :], interp1[:, half], start=True, stop=True)
                    full(pe.matmul(p[0:64, P:2 * P], o2[:, b, :], interp2[:, half], start=True, stop=True), "y", gh, b)
                for b in range(NB):
                    p = bank("h", gh, b)
                    emptied(pe, "y", gh, b)
                    pe.matmul(p[:, 0:D], y_a[:, b, :], wf_a[:], start=True, stop=False)
                    pe.matmul(p[:, 0:D], y_b[:, b, :], wf_b[:], start=False, stop=False).then_inc(sem("y_used"), 1)
                    full(pe.matmul(p[:, 0:D], ones_row[:], bf_row[:], start=False, stop=True), "h", gh, b)

            def turn(src, name, ready, i, b):
                pe.wait_ge(ready, 3)
                for kc in range(2):
                    p = bank(name, i, b, kc)
                    for c in range(3):
                        mm = pe.transpose(p[0:HF, c * P:(c + 1) * P], src[:, b, c, kc * HF:(kc + 1) * HF], ident[:])
                    full(mm, name, i, b, kc)

            def token_sum(i, b):
                p = bank("xsum", i, b)
                for kc in range(2):
                    for c in range(3):
                        n = SIZES[c]
                        mm = pe.matmul(p[0:HF, kc:kc + 1], xhat[0:n, b, c, kc * HF:(kc + 1) * HF], ones_col[0:n, :],
                                       start=(c == 0), stop=(c == 2))
                full(mm, "xsum", i, b)

            def turned(i, b):
                for kc in range(2):
                    emptied(pe, "xt", i, b, kc)

            def qkv(i, b):
                turned(2 * i, b)
                n = T + i
                for j in range(2 * NG):
                    w = n if j >= NG else T
                    p = bank("qk", i, b, j)
                    if i and j == NG:
                        emptied(pe, "xsum", 2, b)
                    for kc in range(2):
                        mm = pe.matmul(p[:, 0:w], w_qk[i][:, kc, j, :], xT[:, b, kc, 0:w], start=(kc == 0), stop=(kc == 1))
                    full(mm, "qk", i, b, j)
                for part in range(2):
                    p = bank("v", i, b, part)
                    for c in ((0, 1), (2,))[part]:
                        m = SIZES[c]
                        at = D * (c % 2)
                        for kc in range(2):
                            mm = pe.matmul(p[0:m, at:at + D], xT[:, b, kc, c * P:c * P + m], w_v[i][:, kc, :],
                                           start=(kc == 0), stop=(kc == 1 and not i))
                        if i:
                            mm = pe.matmul(p[0:m, at:at + D], ones_row[:, 0:m], b_v[:], start=False, stop=True)
                    full(mm, "v", i, b, part)

            def proj(i, b):
                turn(att, "yt", sem("att_ready", i, b), i, b)
                for kc in range(2):
                    emptied(pe, "yt", i, b, kc)
                for part in range(2):
                    p = bank("o", i, b, part)
                    for c in ((0, 1), (2,))[part]:
                        m = SIZES[c]
                        at = D * (c % 2)
                        for kc in range(2):
                            mm = pe.matmul(p[0:m, at:at + D], attT[:, b, kc, c * P:c * P + m], w_o[i][:, kc, :],
                                           start=(kc == 0), stop=(kc == 1 and not i))
                        if i:
                            mm = pe.matmul(p[0:m, at:at + D], ones_row[:, 0:m], b_o[:], start=False, stop=True)
                    full(mm, "o", i, b, part)

            for b in range(NB):
                turn(xhat, "xt", sem("xhat_ready", 0, b), 0, b)
            loaded(pe, "att0")
            pe.wait_ge(sem("pads_set"), 1)
            for b in range(NB):
                qkv(0, b)
                for j in range(2 * NG):
                    emptied(pe, "qk", 0, b, j)

                def scores0(h):
                    g, r = h // HPG, 32 * (h % HPG)
                    p = bank("s0", b, h)
                    for c in range(3):
                        mm = pe.matmul(p[:, KEYAT[c]:KEYAT[c] + KEYW[c]], qk[r:r + HD, b, NG + g, c * P:(c + 1) * P],
                                       qk[r:r + HD, b, g, c * P:T], start=True, stop=True, tile_position=(r, 0))
                    full(mm, "s0", b, h)

                def values0(h):
                    n = b * NH + h
                    pe.wait_ge(sem("pm_ready"), n + 1)
                    w = pm[:, n % PMR, :]
                    for qc in range(3):
                        m = SIZES[qc]
                        dst = y01[:, qc, h, :] if qc < 2 else y2[:, h, :]
                        for kc in range(qc + 1):
                            at = KEYAT[kc] + (qc - kc) * P
                            k = SIZES[kc]
                            mm = pe.matmul(dst, w[0:k, at:at + m], vals[0:k, b, kc, h, :], start=(kc == 0), stop=(kc == qc))
                    mm.then_inc(sem("pm_used"), 1)

                for part in range(2):
                    emptied(pe, "v", 0, b, part)
                if b:
                    pe.wait_ge(sem("att_ready", 0, b - 1), 3)
                for h in range(NH + 2):
                    if h < NH:
                        scores0(h)
                    if h >= 2:
                        values0(h - 2)
                proj(0, b)
            loaded(pe, "ffn0")
            for b in range(NB):
                turn(xhat, "xt", sem("xhat_ready", 1, b), 1, b)
                token_sum(1, b)
                p = bank("logits0", b)
                emptied(pe, "xsum", 1, b)
                for kc in range(2):
                    mm = pe.matmul(p[0:1, 0:E0], xmean[:, b, kc:kc + 1], w_g0[:, kc, :], start=(kc == 0), stop=(kc == 1))
                full(mm, "logits0", b)
            for b in range(NB):
                p = bank("gate0", b)
                pe.wait_ge(sem("wt0_ready", b), 1)
                full(pe.matmul(p[:, 0:1], ones_row[:], wt0[:, b:b + 1], start=True, stop=True), "gate0", b)
            for b in range(NB):
                turned(1, b)
                pe.wait_ge(sem("expert_in", b), 64)
                for f in range(NF):
                    p = bank("up0", b, f)
                    for kc in range(2):
                        mm = pe.matmul(p[:, 0:T], w_up0[b][:, kc, f * P:(f + 1) * P], xT[:, b, kc, 0:T], start=(kc == 0), stop=(kc == 1))
                    full(mm, "up0", b, f)
                for f in range(NF):
                    emptied(pe, "up0", b, f)
                for part in range(2):
                    p = bank("down0", b, part)
                    for c in ((0, 1), (2,))[part]:
                        m = SIZES[c]
                        at = D * (c % 2)
                        for f in range(NF):
                            pe.matmul(p[0:m, at:at + D], hid0[b][:, f, c * P:c * P + m], w_dn0[b][:, f, :], start=(f == 0), stop=False)
                        mm = pe.matmul(p[0:m, at:at + D], ones_row[:, 0:m], b_dn0[:, b, :], start=False, stop=True)
                    full(mm, "down0", b, part)
            loaded(pe, "att1")
            for b in range(NB):
                turn(xhat, "xt", sem("xhat_ready", 2, b), 2, b)
                token_sum(2, b)
                qkv(1, b)
                for j in range(2 * NG):
                    emptied(pe, "qk", 1, b, j)
                for t, (g, hh, c) in enumerate(tile_heads()):
                    p = bank("s1", b, t)
                    for one in ([hh] if hh is not None else range(HPG)):
                        r = 32 * one
                        m = SIZES[c]
                        to = 0 if hh is not None else r
                        mm = pe.matmul(p[to:to + m, 0:T + 1], qk[r:r + HD, b, g, c * P:c * P + m],
                                       qk[r:r + HD, b, NG + g, 0:T + 1], start=True, stop=True, tile_position=(r, to))
                    full(mm, "s1", b, t)
            for b in range(NB):
                for part in range(2):
                    emptied(pe, "v", 1, b, part)
                pe.wait_ge(sem("att_ready", *((1, b - 1) if b else (0, NB - 1))), 3)

                def turn_probs(t):
                    n = b * TILES + t
                    pe.wait_ge(sem("ps_ready"), n + 1)
                    p = bank("pt", b, t)
                    for kc in range(3):
                        mm = pe.transpose(p[:, kc * P:(kc + 1) * P], ps[:, n % PMR, kc * P:(kc + 1) * P], ident[:])
                    full(mm, "pt", b, t)

                def values1(t):
                    n = b * TILES + t
                    g, hh, c = tile_heads()[t]
                    emptied(pe, "pt", b, t)
                    for one in ([hh] if hh is not None else range(HPG)):
                        h = g * HPG + one
                        m = SIZES[c]
                        at = 0 if hh is not None else 32 * one
                        dst = y01[:, c, h, :] if hh is not None else y2[:, h, :]
                        for kc in range(3):
                            k = SIZES[kc]
                            mm = pe.matmul(dst, psT[0:k, n % PMR, kc * P + at:kc * P + at + m], vals[0:k, b, kc, h, :],
                                           start=(kc == 0), stop=(kc == 2))
                    mm.then_inc(sem("psT_used"), 1)

                for t in range(TILES + 2):
                    if t < TILES:
                        turn_probs(t)
                    if t >= 2:
                        values1(t - 2)
                proj(1, b)
            loaded(pe, "ffn1")
            for b in range(NB):
                turn(xhat, "xt", sem("xhat_ready", 3, b), 3, b)
                turned(3, b)
                p = bank("g1", b)
                for kc in range(2):
                    mm = pe.matmul(p[0:G1, 0:T], w_g1[:, kc, :], xT[:, b, kc, 0:T], start=(kc == 0), stop=(kc == 1))
                full(mm, "g1", b)
                p = bank("logits1", b)
                emptied(pe, "g1", b)
                for c in range(3):
                    pe.matmul(p[:, c * E1:(c + 1) * E1], gT[:, b, c * P:(c + 1) * P], w_l1[:], start=True, stop=False)
                    mm = pe.matmul(p[:, c * E1:(c + 1) * E1], ones_row[:], b_l1[:], start=False, stop=True)
                full(mm, "logits1", b)
            for b in range(NB):
                for e in range(E1):
                    n = b * E1 + e
                    for f in range(2):
                        p = bank("z", b, e, f)
                        for kc in range(2):
                            mm = pe.matmul(p[:, 0:T], w_z[:, e, kc, f * P:(f + 1) * P], xT[:, b, kc, 0:T], start=(kc == 0), stop=(kc == 1))
                        full(mm, "z", b, e, f)
                    for part in range(2):
                        p = bank("up1", b, e, part)
                        for f in range(2):
                            emptied(pe, "z", b, e, f)
                        for c in ((0, 1), (2,))[part]:
                            m = SIZES[c]
                            at = D * (c % 2)
                            for f in range(2):
                                mm = pe.matmul(p[0:m, at:at + D], zT[:, n % 2, f, c * P:c * P + m], w_u[:, e, f, :],
                                               start=(f == 0), stop=(f == 1))
                        full(mm, "up1", b, e, part)

        @block.vector
        def _(dve):
            steps = [0]

            def step(ins):
                steps[0] += 1
                ins.then_inc(sem("dve_step"), 1)

            def settle():
                dve.wait_ge(sem("dve_step"), steps[0])

            def out_of(ins, *key):
                ins.then_inc(free_of(*key), 1)

            dve.memset(ones_row[:], 1.0).then_inc(sem("ones_set"), 1)
            dve.memset(ones_col[:], 1.0)
            dve.memset(eps_col[:], 1e-5).then_inc(sem("eps_set"), 1)
            dve.memset(vals[:], 1.0).then_inc(sem("vals_set"), 1)
            dve.memset(att[:, :, 2, :], 0.0).then_inc(sem("att_zero"), 1)
            dve.memset(ps[:, :, T:TP], 0.0)
            dve.memset(gT[:, :, T:TP], 0.0)
            dve.memset(lg0[:], -3e38).then_inc(sem("lg0_set"), 1)
            dve.memset(qk[:, :, :, T:TP], 0.0).then_inc(sem("pads_set"), 1)

            def by_sequence(dst, src, f, done):
                dve.tensor_copy(dst.rearrange("p b (k f) -> p k b f", f=f), src.rearrange("p k (b f) -> p k b f", b=NB)).then_inc(done, 1)

            dve.wait_ge(sem("patch1_in"), 128)
            by_sequence(seq1[:], patch1[:], 12, sem("seq1_ready"))
            p = filled(dve, "t1")
            out_of(dve.tensor_copy(t1[:].rearrange("p b k n -> p (b k n)"), p[0:96, 0:NB * P]), "t1")
            dve.wait_ge(sem("patch2_in"), 32)
            by_sequence(seq2[:], patch2[:], 48, sem("seq2_ready"))
            p = filled(dve, "t2")
            out_of(dve.tensor_copy(t2[:].rearrange("p b k n -> p (b k n)"), p[0:96, 0:NB * P]), "t2")
            p = filled(dve, "o1")
            out_of(dve.tensor_copy(o1[:].rearrange("p b n -> p (b n)"), p[0:64, 0:NB * 64]), "o1")
            for gh in range(2):
                dve.wait_ge(sem("patch0_in", gh), 256)
                by_sequence(seq0[:, gh, :, :], patch0[:, gh, :, :], 3, sem("seq0_ready"))
                for b in range(NB):
                    p = filled(dve, "h", gh, b)
                    out_of(dve.tensor_copy(resid[:, b, gh, :], p[:, 0:D]), "h", gh, b)

            def layernorm(i, b, src, dst):
                for c in range(3):
                    step(dve.bn_stats(stats[:, b, c, :], src[:, b, c, :]))
                settle()
                for c in range(3):
                    dve.bn_aggr(moments[:, b, c, :], stats[:, b, c, :]).then_inc(sem("moments_ready", i, b), 1)
                dve.wait_ge(sem("std_ready", i, b), 1)
                step(dve.reciprocal(rstd[:, b, :], std[:, b, :]))
                settle()
                for c in range(3):
                    dve.tensor_scalar(dst[:, b, c, :], src[:, b, c, :], moments[:, b, c, 0:1], rstd[:, b, c:c + 1],
                                      ALU.subtract, ALU.mult).then_inc(sem("xhat_ready", i, b), 1)

            def turned_half(i, b):
                p = filled(dve, "xt", i, b, 1)
                out_of(dve.tensor_copy(xT[:, b, 1, :], p[0:HF, 0:TP]), "xt", i, b, 1)

            def values(i, b):
                p = filled(dve, "v", i, b, 0)
                out_of(dve.tensor_copy(vals[:, b, 0:2, :, 0:HD], p[:, 0:2 * D].rearrange("p (c h w) -> p c h w", c=2, h=NH)), "v", i, b, 0)
                p = filled(dve, "v", i, b, 1)
                out_of(dve.tensor_copy(vals[0:TXT, b, 2, :, 0:HD], p[0:TXT, 0:D].rearrange("p (h w) -> p h w", h=NH)), "v", i, b, 1)

            def normalize(i, b, last_used, eps):
                dve.wait_ge(*last_used)
                if eps:
                    step(dve.tensor_scalar(den[:, 0:2, :], y01[:, :, :, HD], eps, None, ALU.add))
                    step(dve.tensor_scalar(den[0:TXT, 2, :], y2[:, :, HD], eps, None, ALU.add))
                else:
                    step(dve.tensor_copy(den[:, 0:2, :], y01[:, :, :, HD]))
                    step(dve.tensor_copy(den[0:TXT, 2, :], y2[:, :, HD]))
                settle()
                step(dve.reciprocal(rden[:, 0:2, :], den[:, 0:2, :]))
                step(dve.reciprocal(rden[0:TXT, 2, :], den[0:TXT, 2, :]))
                settle()
                ready = sem("att_ready", i, b)
                for c in range(3):
                    m = SIZES[c]
                    src = y01[:, c, :, 0:HD] if c < 2 else y2[:, :, 0:HD]
                    dve.tensor_tensor(att[0:m, b, c, :].rearrange("p (h w) -> p h w", h=NH), src,
                                      rden[0:m, c, :].unsqueeze(2).to_broadcast([m, NH, HD]), ALU.mult).then_inc(ready, 1)

            def add_projection(i, b):
                p = filled(dve, "yt", i, b, 1)
                out_of(dve.tensor_copy(attT[:, b, 1, :], p[0:HF, 0:TP]), "yt", i, b, 1)
                add_chunks("o", i, b)

            def add_chunks(*key):
                b = key[-1]
                p = filled(dve, *key, 0)
                r = resid[:, b, 0:2, :].rearrange("p c n -> p (c n)")
                dve.tensor_tensor(r, p[:, 0:2 * D], r, ALU.add).then_inc(free_of(*key, 0), 1)
                p = filled(dve, *key, 1)
                r = resid[0:TXT, b, 2, :]
                dve.tensor_tensor(r, p[0:TXT, 0:D], r, ALU.add).then_inc(free_of(*key, 1), 1)
                for n in range(2):
                    emptied(dve, *key, n)

            for gh in range(2):
                for b in range(NB):
                    emptied(dve, "h", gh, b)
            dve.wait_ge(sem("text_in"), 32)
            for b in range(NB):
                layernorm(0, b, resid, xhat)
            for b in range(NB):
                turned_half(0, b)
            dve.wait_ge(sem("vals_set"), 1)
            loaded(dve, "att0")
            for b in range(NB):
                for j in range(1, 2 * NG, 2):
                    p = filled(dve, "qk", 0, b, j)
                    out_of(dve.tensor_copy(qk[:, b, j, 0:T], p[:, 0:T]), "qk", 0, b, j)
                values(0, b)
                for h in range(NH):
                    n = b * NH + h
                    emptied(dve, "s0", b, h)
                    if n >= PMR:
                        dve.wait_ge(sem("pm_used"), n - PMR + 1)
                    dve.scalar_tensor_tensor(pm[:, n % PMR, :], sq[:, n % PMR, :], 1.0, mask[:], ALU.add, ALU.mult).then_inc(sem("pm_ready"), 1)
                normalize(0, b, (sem("pm_used"), (b + 1) * NH), 2e-12)
                add_projection(0, b)
            for b in range(NB):
                layernorm(1, b, resid, xhat)
            dve.wait_ge(sem("lg0_set"), 1)
            for b in range(NB):
                turned_half(1, b)
                p = filled(dve, "xsum", 1, b)
                out_of(dve.tensor_scalar(xmean[:, b, :], p[0:HF, 0:2], 1.0 / T, None, ALU.mult), "xsum", 1, b)
                p = filled(dve, "logits0", b)
                out_of(dve.tensor_copy(lg0[:, b, 0:E0], p[0:1, 0:E0]), "logits0", b)
                emptied(dve, "logits0", b)
                step(dve.max(top0[:, b, :], lg0[:, b, :]))
                settle()
                step(dve.max_index(arg0[:, b, :], top0[:, b, :], lg0[:, b, :]))
                settle()
                dve.tensor_scalar(neg0[:, b:b + 1], top0[:, b, 0:1], -1.0, None, ALU.mult).then_inc(sem("expert_known", b), 1)
            for b in range(NB):
                dve.wait_ge(sem("sum0_ready", b), 1)
                dve.reciprocal(wt0[:, b:b + 1], sum0[:, b:b + 1]).then_inc(sem("wt0_ready", b), 1)
                p = filled(dve, "gate0", b)
                out_of(dve.tensor_copy(wcol0[:, b:b + 1], p[:, 0:1]), "gate0", b)
            for b in range(NB):
                emptied(dve, "gate0", b)
                for part in range(2):
                    m = SIZES[2 * part]
                    p = filled(dve, "down0", b, part)
                    r = resid[0:m, b, 0:2, :] if part == 0 else resid[0:m, b, 2:3, :]
                    r = r.rearrange("p c n -> p (c n)")
                    out_of(dve.scalar_tensor_tensor(r, p[0:m, 0:D * (2 - part)], wcol0[0:m, b:b + 1], r, ALU.mult, ALU.add), "down0", b, part)
                for part in range(2):
                    emptied(dve, "down0", b, part)
            loaded(dve, "att1")
            dve.tensor_scalar(b_q[:], b_qk[:, 0:NG], 0.25 * TINY, None, ALU.mult).then_inc(sem("b_q_ready"), 1)
            for b in range(NB):
                layernorm(2, b, resid, xhat)
            for b in range(NB):
                turned_half(2, b)
                p = filled(dve, "xsum", 2, b)
                emptied(dve, "xt", 2, b, 0)
                emptied(dve, "xt", 2, b, 1)
                dve.tensor_scalar(xT[:, b, :, T], p[0:HF, 0:2], 1.0 / T, None, ALU.mult).then_inc(free_of("xsum", 2, b), 1)
                for j in range(NG, 2 * NG):
                    p = filled(dve, "qk", 1, b, j)
                    out_of(dve.tensor_scalar(qk[:, b, j, 0:T + 1], p[:, 0:T + 1], b_qk[:, j:j + 1], None, ALU.add), "qk", 1, b, j)
                values(1, b)
            for b in range(NB):
                for t in range(TILES):
                    emptied(dve, "s1", b, t)
                    step(dve.tensor_reduce(smax[:, b, t:t + 1], scores[:, b, t, 0:T], AX.X, ALU.max))
                settle()
                dve.tensor_scalar(nbias[:, b, :], smax[:, b, :], -1.0 / TINY, None, ALU.mult).then_inc(sem("nbias_ready", b), 1)
                rounds = (TOPK + 7) // 8
                with dve.Fori(0, TILES) as i:
                    dve.sem_clear(sem("pick_step"))
                    dve.tensor_copy(work[:, 0, :], scores[:, b, bass.ds(i, 1), 0:T].rearrange("p a n -> p (a n)")).then_inc(sem("pick_step"), 1)
                    n = 1
                    for r in range(rounds):
                        dve.wait_ge(sem("pick_step"), n)
                        dve.max(top8[:], work[:, r % 2, :]).then_inc(sem("pick_step"), 1)
                        n += 1
                        dve.wait_ge(sem("pick_step"), n)
                        if r < rounds - 1:
                            dve.match_replace(work[:, (r + 1) % 2, :], top8[:], work[:, r % 2, :], -3e38).then_inc(sem("pick_step"), 1)
                            n += 1
                    at = (TOPK - 1) % 8
                    dve.tensor_copy(thr[:, b, bass.ds(i, 1)], top8[:, at:at + 1]).then_inc(sem("pick_step"), 1)
                    dve.wait_ge(sem("pick_step"), n + 1)
            for b in range(NB):
                for t in range(TILES):
                    n = b * TILES + t
                    dve.wait_ge(sem("es_ready"), n + 1)
                    if n >= PMR:
                        filled(dve, "pt", *divmod(n - PMR, TILES))
                    dve.scalar_tensor_tensor(ps[:, n % PMR, 0:T], scores[:, b, t, 0:T], thr[:, b, t:t + 1], es[:, n % PMR, :],
                                             ALU.is_ge, ALU.mult).then_inc(sem("ps_ready"), 1)
                normalize(1, b, (sem("psT_used"), (b + 1) * TILES), 0.0)
                add_projection(1, b)
            for b in range(NB):
                layernorm(3, b, resid, xhat)
            loaded(dve, "ffn1")
            for b in range(NB):
                turned_half(3, b)
            for b in range(NB):
                p = filled(dve, "logits1", b)
                pl = p[:, 0:3 * E1].rearrange("p (c e) -> p c e", c=3)
                step(dve.tensor_reduce(max1[:, b, :], pl, AX.X, ALU.max))
                settle()
                dve.tensor_tensor(lg1[:, b, :, :], pl, max1[:, b, :].unsqueeze(2).to_broadcast([P, 3, E1]), ALU.subtract).then_inc(free_of("logits1", b), 1)
                emptied(dve, "logits1", b)
                for c in range(3):
                    step(dve.max(top1[:, b, c, :], lg1[:, b, c, :]))
                settle()
                for c in range(3):
                    step(dve.max_index(arg1[:, b, c, :], top1[:, b, c, :], lg1[:, b, c, :]))
                settle()
                step(dve.tensor_copy(arg1f[:, b, :, :], arg1[:, b, :, 0:2]))
                settle()
                for k in range(2):
                    step(dve.tensor_tensor(hit[:, b, k, :, :], iota8[:].unsqueeze(1).to_broadcast([P, 3, E1]),
                                           arg1f[:, b, :, k:k + 1].to_broadcast([P, 3, E1]), ALU.is_equal))
                settle()
                step(dve.tensor_tensor(hit[:, b, 0, :, :], hit[:, b, 0, :, :], hit[:, b, 1, :, :], ALU.add))
                settle()
                dve.wait_ge(sem("e1_ready", b), 1)
                step(dve.tensor_tensor(w1[:, b, :, :], e1[:, b, :, :], hit[:, b, 0, :, :], ALU.mult))
                step(dve.tensor_reduce(z1[:, b, :], e1[:, b, :, :], AX.X, ALU.add))
                settle()
                step(dve.tensor_reduce(s1[:, b, :], w1[:, b, :, :], AX.X, ALU.add))
                settle()
                step(dve.scalar_tensor_tensor(s1[:, b, :], z1[:, b, :], 1e-8, s1[:, b, :], ALU.mult, ALU.add))
                settle()
                step(dve.reciprocal(s1[:, b, :], s1[:, b, :]))
                settle()
                step(dve.tensor_tensor(w1[:, b, :, :], w1[:, b, :, :], s1[:, b, :].unsqueeze(2).to_broadcast([P, 3, E1]), ALU.mult))
                settle()
            for b in range(NB):
                for e in range(E1):
                    if e:
                        emptied(dve, "up1", b, e - 1, 0)
                        emptied(dve, "up1", b, e - 1, 1)

                    def add_expert(c, p):
                        m, at = SIZES[c], D * (c % 2)
                        return dve.scalar_tensor_tensor(acc[0:m, b, c, :], p[0:m, at:at + D], w1[0:m, b, c, e:e + 1],
                                                        acc[0:m, b, c, :], ALU.mult, ALU.add)

                    p = filled(dve, "up1", b, e, 0)
                    add_expert(0, p)
                    out_of(add_expert(1, p), "up1", b, e, 0)
                    p = filled(dve, "up1", b, e, 1)
                    out_of(add_expert(2, p), "up1", b, e, 1)
            for b in range(NB):
                for part in range(2):
                    emptied(dve, "up1", b, E1 - 1, part)
                layernorm(4, b, acc, fin)
                dve.wait_ge(sem("xhat_ready", 4, b), 3)
                f, r = fin[:, b, :, :], resid[:, b, :, :]
                step(dve.tensor_tensor(f, f, gamma[:].unsqueeze(1).to_broadcast([P, 3, D]), ALU.mult))
                step(dve.tensor_tensor(r, r, beta[:].unsqueeze(1).to_broadcast([P, 3, D]), ALU.add))
                settle()
                dve.tensor_tensor(f, f, r, ALU.add).then_inc(sem("fin_ready", b), 1)


def kernel(x, txt, L0_tok_W0, L0_tok_b0, L0_tok_W1, L0_tok_b1, L0_tok_W2, L0_tok_b2, L0_tok_Wf, L0_tok_bf,
           L0_tok_idx0, L0_tok_idx1, L0_tok_idx2, L0_attn_Wq, L0_attn_Wk, L0_attn_Wv, L0_attn_Wo,
           L0_ffn_Wg, L0_ffn_W1, L0_ffn_b1, L0_ffn_W2, L0_ffn_b2, L1_attn_W_qkv, L1_attn_b_qkv,
           L1_attn_W_proj, L1_attn_b_proj, L1_ffn_w1, L1_ffn_b1, L1_ffn_w2, L1_ffn_b2, L1_ffn_down_w,
           L1_ffn_down_b, L1_ffn_up_w, L1_ffn_gamma, L1_ffn_beta):
    import numpy as np
    import concourse.bacc as bacc
    from concourse.bass_utils import run_bass_kernel_spmd as run

    def patches(p):
        h = 64 // p
        return x.reshape(NB, 3, h, p, h, p).transpose(2, 4, 0, 3, 5, 1).reshape(h * h, NB * p * p * 3)

    def halves(w):
        return w.reshape(2, HF, -1).transpose(1, 0, 2)

    def heads(w):
        o = np.zeros(w.shape[:-1] + (NH, 32), w.dtype)
        o[..., 0:HD] = w.reshape(w.shape[:-1] + (NH, HD))
        return o.reshape(w.shape[:-1] + (NH * 32,))

    def interp(n):
        pos = np.clip((np.arange(IMG, dtype=np.float32) + 0.5) * (n / IMG) - 0.5, 0.0, n - 1)
        i0 = np.floor(pos).astype(np.int32)
        i1 = np.minimum(i0 + 1, n - 1)
        w = (pos - i0).astype(np.float32)
        m = np.zeros((n, IMG), np.float32)
        m[i0, np.arange(IMG)] += 1.0 - w
        m[i1, np.arange(IMG)] += w
        return m

    def qk_weights(wq, wk):
        return np.concatenate([halves(heads(wq)), halves(heads(wk))], axis=2).reshape(HF, 2, 2 * NG, P)

    tri = (np.arange(T)[None, :] >= np.arange(P)[:, None]).astype(np.float32)
    qkv_w, qkv_b = L1_attn_W_qkv, L1_attn_b_qkv
    arrays = {
        "x0": patches(1), "x1": patches(2), "x2": patches(4), "txt": txt,
        "idx": np.concatenate([
            L0_tok_idx0.reshape(2, P, 16).transpose(1, 0, 2).reshape(P, 32),
            L0_tok_idx1.reshape(64, 2, 8).transpose(1, 0, 2).reshape(P, 8),
            L0_tok_idx2.reshape(16, 8, 2).transpose(1, 0, 2).reshape(P, 2)], axis=1),
        "w_tok0": L0_tok_W0.T, "w_tok1": L0_tok_W1.T.reshape(2, 96, 64).transpose(1, 0, 2),
        "w_tok2": L0_tok_W2.T.reshape(8, 96, 64).transpose(1, 0, 2),
        "b_tok01": np.concatenate([L0_tok_b0, L0_tok_b1])[:, None], "b_tok2": L0_tok_b2[:, None],
        "wf_a": L0_tok_Wf.T[0:P], "wf_b": L0_tok_Wf.T[P:D], "bf_row": L0_tok_bf[None, :],
        "interp1": interp(64), "interp2": interp(16),
        "mask": np.concatenate([tri[:, 0:w] for w in KEYW], axis=1),
        "iota8": np.tile(np.arange(E1, dtype=np.float32), (P, 1)),
        "w_qk0": qk_weights(L0_attn_Wq.T, L0_attn_Wk.T), "w_v0": halves(L0_attn_Wv.T), "w_o0": halves(L0_attn_Wo.T),
        "w_qk1": qk_weights(qkv_w[:, 0:D], qkv_w[:, D:2 * D]), "w_v1": halves(qkv_w[:, 2 * D:]),
        "w_o1": halves(L1_attn_W_proj),
        "b_qk": np.concatenate([heads(qkv_b[0:D]), heads(qkv_b[D:2 * D])]).reshape(2 * NG, P).T,
        "b_v": qkv_b[None, 2 * D:], "b_o": L1_attn_b_proj[None, :],
        "w_g0": halves(L0_ffn_Wg.T),
        "w_up0": L0_ffn_W1.reshape(E0, 2, HF, F0).transpose(0, 2, 1, 3),
        "b_up0": L0_ffn_b1.reshape(E0, NF, P).transpose(0, 2, 1),
        "w_dn0": L0_ffn_W2.reshape(E0, NF, P, D).transpose(0, 2, 1, 3), "b_dn0": L0_ffn_b2,
        "w_g1": halves(L1_ffn_w1), "b_g1": L1_ffn_b1[:, None], "w_l1": L1_ffn_w2, "b_l1": L1_ffn_b2[None, :],
        "w_z": L1_ffn_down_w.reshape(E1, 2, HF, D1).transpose(2, 0, 1, 3),
        "b_z": L1_ffn_down_b.reshape(E1, 2, P).transpose(2, 0, 1),
        "w_u": L1_ffn_up_w.reshape(E1, 2, P, D).transpose(2, 0, 1, 3),
        "gamma": np.broadcast_to(L1_ffn_gamma, (P, D)), "beta": np.broadcast_to(L1_ffn_beta, (P, D)),
    }
    nc = bacc.Bacc("TRN2", target_bir_lowering=False, num_devices=1)
    arrays = {f"in_{k}": np.ascontiguousarray(v) for k, v in arrays.items()}
    aps = {k[3:]: nc.dram_tensor(k, v.shape, mybir.dt.from_np(v.dtype), kind="ExternalInput").ap() for k, v in arrays.items()}
    out = nc.dram_tensor("out_0", (NB, T, D), F32, kind="ExternalOutput").ap()
    fusion_program(nc, aps, out)
    r = run(nc, [arrays], core_ids=[0])
    return r.results[0]["out_0"]
```

```python
from contextlib import ExitStack

import concourse.bass as bass
from concourse import mybir

F32 = mybir.dt.float32
I32 = mybir.dt.int32
U32 = mybir.dt.uint32
ALU = mybir.AluOpType
ACT = mybir.ActivationFunctionType
AX = mybir.AxisListType

NB = 2
P = 128
IMG, TXT = 256, 32
T = IMG + TXT
TP = 3 * P
SIZES = (P, P, TXT)
D = 192
HF = D // 2
NH, HD = 12, 16
HPG = 4
NG = NH // HPG
VW = HD + 1
F0 = 768
NF = F0 // P
E0 = 3
E1, D1 = 8, 256
G1 = 96
TOPK = 115
KEYW = (T, T - P, TXT)
KEYAT = (0, T, 2 * T - P)
CAUSAL = sum(KEYW)
TILES = 2 * NH + NG
SW = T + 2
TINY = 2.0 ** -40
RING = 6
PMR = 3

GT = TILES // NG
BATCHES = NB * NG
STAGES = 7
BLOCKS = (((6, 4), (2, 0)), ((5, 3), (1,)))
ACT_COUNTS = {1: 9, 2: 7, 3: 9, 4: 3}
POOL_SUBS = (1, 3, 5, 7)
AIM = TOPK - 4.5
HITS = 3.5
SPREAD = 1 / 2.75
START = 0.28
REACH = 120
SLOPE = 111
WORK = 4


def schedule():
    out = []
    for s in range(2 * (BATCHES - 1) + STAGES):
        out.append([[((s - k) // 2, k) for k in block if s >= k and (s - k) // 2 < BATCHES] for block in BLOCKS[s % 2]])
    return out


def counted_by():
    out, act, dve = {}, 0, 0
    for slot in schedule():
        for block in slot:
            for i, k in block:
                if k in ACT_COUNTS:
                    act += ACT_COUNTS[k]
                    dve += GT - ACT_COUNTS[k]
                    out[i, k] = (act, dve)
    return out


def tile_heads():
    out = []
    for g in range(NG):
        for hh in range(HPG):
            out += [(g, hh, 0), (g, hh, 1)]
        out.append((g, None, 2))
    return out


class Ring:

    def __init__(self):
        self.uses = {}

    def add(self, *key):
        n = len(self.uses)
        self.uses[key] = (n % RING, n // RING)


def plan_banks():
    r = Ring()
    r.add("t1")
    r.add("t2")
    r.add("o1")
    r.add("o2")
    for gh in range(2):
        r.add("t0", gh)
        for b in range(NB):
            r.add("y", gh, b)
        for b in range(NB):
            r.add("h", gh, b)

    def norm_in(i, b):
        r.add("xt", i, b, 0)
        r.add("xt", i, b, 1)

    def qkv(i, b):
        for j in range(2 * NG):
            r.add("qk", i, b, j)
        r.add("v", i, b, 0)
        r.add("v", i, b, 1)

    def proj(i, b):
        for n in range(2):
            r.add("yt", i, b, n)
        for n in range(2):
            r.add("o", i, b, n)

    for b in range(NB):
        norm_in(0, b)
    for b in range(NB):
        qkv(0, b)
        for h in range(NH):
            r.add("s0", b, h)
        proj(0, b)
    for b in range(NB):
        norm_in(1, b)
        r.add("xsum", 1, b)
        r.add("logits0", b)
    for b in range(NB):
        r.add("gate0", b)
    for b in range(NB):
        for f in range(NF):
            r.add("up0", b, f)
        r.add("down0", b, 0)
        r.add("down0", b, 1)
    for b in range(NB):
        norm_in(2, b)
        r.add("xsum", 2, b)
        qkv(1, b)
    for slot in schedule():
        for block in slot:
            if any(k == 6 for _, k in block):
                r.add("hits", block[0][0])
            for t in range(GT):
                for i, k in block:
                    if k == 6:
                        r.add("pt", *divmod(i * GT + t, TILES))
                    if k == 0:
                        r.add("s1", *divmod(i * GT + t, TILES))
            for i, k in block:
                if k == 6 and i % NG == NG - 1:
                    proj(1, i // NG)
    for b in range(NB):
        norm_in(3, b)
        r.add("g1", b)
        r.add("logits1", b)
    for b in range(NB):
        for e in range(E1):
            r.add("z", b, e, 0)
            r.add("z", b, e, 1)
            r.add("up1", b, e, 0)
            r.add("up1", b, e, 1)
    return r.uses


def fusion_program(nc, a, out):
    USES = plan_banks()
    COUNTED = counted_by()
    ctx = ExitStack()
    with ctx:
        def sb(name, shape, dt=F32):
            return ctx.enter_context(nc.sbuf_tensor(name, shape, dt))

        sems = {}

        def sem(*name):
            if name not in sems:
                sems[name] = ctx.enter_context(nc.semaphore("_".join(map(str, name))))
            return sems[name]

        ident = sb("ident", [P, P])
        ones_row = sb("ones_row", [1, P])
        ones_col = sb("ones_col", [P, 1])
        eps_col = sb("eps_col", [P, 1])
        mask = sb("mask", [P, CAUSAL])
        iota8 = sb("iota8", [P, E1])
        idx = sb("idx", [P, 42], I32)
        w_tok0 = sb("w_tok0", [48, 64])
        w_tok1 = sb("w_tok1", [96, 2, 64])
        w_tok2 = sb("w_tok2", [96, 8, 64])
        b_tok01 = sb("b_tok01", [P, 1])
        b_tok2 = sb("b_tok2", [64, 1])
        wf_a = sb("wf_a", [P, D])
        wf_b = sb("wf_b", [64, D])
        bf_row = sb("bf_row", [1, D])
        interp1 = sb("interp1", [64, IMG])
        interp2 = sb("interp2", [16, IMG])
        w_qk = [sb(f"w_qk{i}", [HF, 2, 2 * NG, P]) for i in range(2)]
        w_v = [sb(f"w_v{i}", [HF, 2, D]) for i in range(2)]
        w_o = [sb(f"w_o{i}", [HF, 2, D]) for i in range(2)]
        b_qk = sb("b_qk", [P, 2 * NG])
        b_q = sb("b_q", [P, NG])
        b_v = sb("b_v", [1, D])
        b_o = sb("b_o", [1, D])
        w_g0 = sb("w_g0", [HF, 2, E0])
        b_up0 = sb("b_up0", [P, NB, NF])
        b_dn0 = sb("b_dn0", [1, NB, D])
        w_g1 = sb("w_g1", [HF, 2, G1])
        b_g1 = sb("b_g1", [G1, 1])
        w_l1 = sb("w_l1", [G1, E1])
        b_l1 = sb("b_l1", [1, E1])
        w_z = sb("w_z", [HF, E1, 2, D1])
        b_z = sb("b_z", [P, E1, 2])
        w_u = sb("w_u", [P, E1, 2, D])
        gamma = sb("gamma", [P, D])
        beta = sb("beta", [P, D])

        pool_sb = sb("score_store", [P, NB, TILES * SW])
        scores = pool_sb[:].rearrange("p b (t n) -> p b t n", t=TILES)
        used = [0, 0]

        def share(b, parts, *shape):
            n = 1
            for k in shape:
                n *= k
            at = used[b]
            used[b] += n
            assert used[b] <= TILES * SW
            letters = "abcd"[0:len(shape)]
            return pool_sb[0:parts, b, at:at + n].rearrange(
                f"p ({' '.join(letters)}) -> p {' '.join(letters)}", **dict(zip(letters, shape)))

        w_up0 = [share(1, HF, 2, F0) for _ in range(NB)]
        hid0 = [share(1, P, NF, T) for _ in range(NB)]
        w_dn0 = [share(0, P, NF, D) for _ in range(NB)]
        sq = share(0, P, PMR, CAUSAL)
        pm = share(0, P, PMR, CAUSAL)
        patch0 = share(1, P, 2, 16, NB * 3)
        patch1 = share(1, P, 8, NB * 12)
        patch2 = share(1, P, 2, NB * 48)
        seq0 = share(1, P, 2, NB, 48)
        seq1 = share(1, P, NB, 96)
        seq2 = share(1, P, NB, 96)
        t0 = share(0, 48, 2, NB, P)
        t1 = share(0, 96, NB, 2, 64)
        t2 = share(0, 96, NB, 8, 16)
        o1 = share(0, 64, NB, 64)
        o2 = share(0, 16, NB, 64)
        y_a = share(0, P, NB, P)
        y_b = share(0, 64, NB, P)
        resid = sb("resid", [P, NB, 3, D])
        stats = sb("stats", [P, NB, 3, 6])
        moments = sb("moments", [P, NB, 3, 2])
        std = sb("std", [P, NB, 3])
        rstd = sb("rstd", [P, NB, 3])
        xhat = sb("xhat", [P, NB, 3, D])
        xT = sb("xT", [HF, NB, 2, TP])
        qk = sb("qk", [P, NB, 2 * NG, TP])
        vals = sb("vals", [P, NB, 3, NH, VW])
        den = sb("den", [P, 3, NH])
        rden = sb("rden", [P, 3, NH])
        att = sb("att", [P, NB, 3, D])
        attT = sb("attT", [HF, NB, 2, TP])
        lg0 = sb("lg0", [1, NB, 8])
        top0 = sb("top0", [1, NB, 8])
        arg0 = sb("arg0", [1, NB, 8], U32)
        neg0 = sb("neg0", [1, NB])
        exp0 = sb("exp0", [1, NB, E0])
        sum0 = sb("sum0", [1, NB])
        wt0 = sb("wt0", [1, NB])
        wcol0 = sb("wcol0", [P, NB])
        xmean = sb("xmean", [HF, NB, 2])
        smax = sb("smax", [P, NB, TILES])
        nbias = sb("nbias", [P, NB, TILES])
        thr = sb("thr", [P, NB, TILES])
        bracket = sb("bracket", [P, NB, 3, 2, TILES])
        side = sb("side", [P, 2, TILES])
        diff = sb("diff", [P, NB, 2, 2, TILES])
        factor = sb("factor", [P, 3])
        spread = sb("spread", [P, TILES])
        signs = sb("signs", [P, 2, T])
        marks = sb("marks", [P, 2, T])
        work = sb("work", [P, WORK, T])
        below8 = sb("below8", [P, TILES, 8])
        count_of = sb("count_of", [P, 8])
        hit8 = sb("hit8", [P, GT, 8])
        hits = sb("hits", [P, NB, NG])
        all_hits = sb("all_hits", [1, 1], I32)
        top8 = sb("top8", [P, 8])
        es = sb("es", [P, PMR, T])
        ps = sb("ps", [P, PMR, TP])
        psT = sb("psT", [P, PMR, TP])
        gT = sb("gT", [G1, NB, TP])
        lg1 = sb("lg1", [P, NB, 3, E1])
        max1 = sb("max1", [P, NB, 3])
        e1 = sb("e1", [P, NB, 3, E1])
        z1 = sb("z1", [P, NB, 3])
        top1 = sb("top1", [P, NB, 3, 8])
        arg1 = sb("arg1", [P, NB, 3, 8], U32)
        arg1f = sb("arg1f", [P, NB, 3, 2])
        hit = sb("hit", [P, NB, 2, 3, E1])
        w1 = sb("w1", [P, NB, 3, E1])
        s1 = sb("s1", [P, NB, 3])
        zT = psT[:].rearrange("p r n -> p (r n)")[:, 0:4 * T].rearrange("p (r c n) -> p r c n", r=2, c=2)
        acc = xhat
        fin = att

        banks = ctx.enter_context(nc.psum_tensor("banks", [P, 8, 512], F32))
        y01 = banks[:, 6, 0:2 * NH * VW].rearrange("p (c h w) -> p c h w", c=2, h=NH)
        y2 = banks[0:TXT, 7, 0:NH * VW].rearrange("p (h w) -> p h w", h=NH)
        bank_full = [sem("bank_full", k) for k in range(RING)]
        bank_free = [sem("bank_free", k) for k in range(RING)]

        def filled(eng, *key):
            k, n = USES[key]
            eng.wait_ge(bank_full[k], n + 1)
            return banks[:, k, :]

        def emptied(eng, *key):
            k, n = USES[key]
            eng.wait_ge(bank_free[k], n + 1)

        def free_of(*key):
            return bank_free[USES[key][0]]

        block = ctx.enter_context(nc.Block())

        LOADS = [
            ("idx", [(idx, "idx")]),
            ("tok", [(w_tok1, "w_tok1"), (w_tok2, "w_tok2"), (w_tok0, "w_tok0"), (interp1, "interp1"),
                     (interp2, "interp2"), (b_tok01, "b_tok01"), (b_tok2, "b_tok2"), (wf_a, "wf_a"),
                     (wf_b, "wf_b"), (bf_row, "bf_row")]),
            ("att0", [(w_qk[0], "w_qk0"), (w_v[0], "w_v0"), (w_o[0], "w_o0"), (mask, "mask")]),
            ("ffn0", [(w_g0, "w_g0")]),
            ("att1", [(w_qk[1], "w_qk1"), (w_v[1], "w_v1"), (w_o[1], "w_o1"), (b_qk, "b_qk"),
                      (b_v, "b_v"), (b_o, "b_o"), (iota8, "iota8")]),
            ("ffn1", [(w_g1, "w_g1"), (b_g1, "b_g1"), (w_l1, "w_l1"), (b_l1, "b_l1"), (w_z, "w_z"),
                      (b_z, "b_z"), (w_u, "w_u"), (gamma, "gamma"), (beta, "beta")]),
        ]
        N_LOADS = {k: 16 * len(v) for k, v in LOADS}

        def loaded(eng, group):
            eng.wait_ge(sem("loaded", group), N_LOADS[group])

        @block.sync
        def _(sp):
            for group, items in LOADS:
                for dst, name in items:
                    sp.dma_start(dst[:], a[name]).then_inc(sem("loaded", group), 16)
                if group == "idx":
                    sp.wait_ge(sem("resid_zero"), 1)
                    for b in range(NB):
                        sp.dma_start(resid[0:TXT, b, 2, :], a["txt"][b]).then_inc(sem("text_in"), 16)
            for b in range(NB):
                sp.wait_ge(sem("expert_known", b), 1)
                e = sp.value_load(arg0[0:1, b, 0:1], min_val=0, max_val=E0 - 1)
                one = bass.ds(e, 1)
                done = sem("expert_in", b)
                sp.dma_start(w_up0[b], a["w_up0"][one, :, :, :].rearrange("e p c n -> (e p) c n")).then_inc(done, 16)
                sp.dma_start(b_up0[:, b, :], a["b_up0"][one, :, :].rearrange("e p n -> (e p) n")).then_inc(done, 16)
                sp.dma_start(w_dn0[b], a["w_dn0"][one, :, :, :].rearrange("e p c n -> (e p) c n")).then_inc(done, 16)
                sp.dma_start(b_dn0[:, b, :], a["b_dn0"][one, :]).then_inc(done, 16)
            for b in range(NB):
                sp.wait_ge(sem("fin_ready", b), 1)
                sp.dma_start(out[b, 0:IMG, :].rearrange("(c p) d -> p c d", p=P), fin[:, b, 0:2, :]).then_inc(sem("stored"), 16)
                sp.dma_start(out[b, IMG:T, :], fin[0:TXT, b, 2, :]).then_inc(sem("stored"), 16)
            sp.wait_ge(sem("stored"), 64)

        @block.gpsimd
        def _(pool):
            pool.memset(resid[:, :, 2, :], 0.0).then_inc(sem("resid_zero"), 1)
            pool.memset(ident[:], 0.0).then_inc(sem("ident"), 1)
            pool.wait_ge(sem("ident"), 1)
            pool.affine_select(out=ident[:], in_=ident[:], compare_op=ALU.not_equal, fill=1.0, base=0,
                               pattern=[[-1, P]], channel_multiplier=1).then_inc(sem("ident"), 1)
            loaded(pool, "idx")

            def gather(dst, src, col, done):
                pool.indirect_dma_start(out=dst, out_offset=None, in_=src,
                                        in_offset=bass.IndirectOffsetOnAxis(ap=idx[:, col:col + 1], axis=0)).then_inc(done, 16)

            for k in range(8):
                gather(patch1[:, k, :], a["x1"], 32 + k, sem("patch1_in"))
            for k in range(2):
                gather(patch2[:, k, :], a["x2"], 40 + k, sem("patch2_in"))
            for gh in range(2):
                for s in range(16):
                    gather(patch0[:, gh, s, :], a["x0"], 16 * gh + s, sem("patch0_in", gh))

            pool_steps = [0]

            def step(ins):
                pool_steps[0] += 1
                ins.then_inc(sem("pool_step"), 1)

            def settle():
                pool.wait_ge(sem("pool_step"), pool_steps[0])

            for n, z in enumerate((0.0, -REACH / SLOPE, REACH / SLOPE)):
                step(pool.memset(factor[:, n:n + 1], (START + z) * SPREAD))
            step(pool.memset(bracket[:, :, 1, 1, :], float(REACH)))
            step(pool.memset(bracket[:, :, 2, 1, :], -float(REACH)))
            settle()

            def first_guess(i):
                b, g = divmod(i, NG)
                cs = slice(g * GT, (g + 1) * GT)
                for t in range(cs.start, cs.stop):
                    if t >= cs.stop - RING:
                        emptied(pool, "s1", b, t)
                mean = scores[:, b, cs, T]
                step(pool.tensor_tensor(spread[:, cs], smax[:, b, cs], mean, ALU.subtract))
                pool.tensor_scalar(nbias[:, b, cs], smax[:, b, cs], -1.0 / TINY, None, ALU.mult).then_inc(sem("nbias_ready", i), 1)
                settle()
                w = bracket[:, b, :, 0, cs]
                step(pool.tensor_tensor(w, spread[:, cs].unsqueeze(1).to_broadcast([P, 3, GT]),
                                        factor[:].unsqueeze(2).to_broadcast([P, 3, GT]), ALU.mult))
                settle()
                pool.tensor_tensor(w, w, mean.unsqueeze(1).to_broadcast([P, 3, GT]), ALU.add).then_inc(sem("guess_ready", i), 1)

            def draw_in(i, r):
                b, g = divmod(i, NG)
                cs = slice(g * GT, (g + 1) * GT)
                by_act, by_dve = COUNTED[i, r + 1]
                if by_act:
                    pool.wait_ge(sem("act_counted"), by_act)
                if by_dve:
                    pool.wait_ge(sem("dve_counted"), by_dve)
                n = ACT_COUNTS[r + 1]
                if n:
                    c = bracket[:, b, 0, 1, g * GT:g * GT + n]
                    step(pool.tensor_scalar(c, c, -0.5, T / 2 - AIM, ALU.mult, ALU.add))
                    settle()
                now = bracket[:, b, 0, :, cs]
                step(pool.tensor_scalar(side[:, 0, cs], now[:, 1, :], 0.0, None, ALU.is_gt))
                step(pool.tensor_scalar(side[:, 1, cs], now[:, 1, :], 0.0, None, ALU.is_le))
                ends = bracket[:, b, 1:3, :, cs]
                move = diff[:, b, :, :, cs]
                step(pool.tensor_tensor(move, now.unsqueeze(1).to_broadcast([P, 2, 2, GT]), ends, ALU.subtract))
                settle()
                step(pool.tensor_tensor(move, move, side[:, :, cs].unsqueeze(2).to_broadcast([P, 2, 2, GT]), ALU.mult))
                settle()
                step(pool.tensor_tensor(ends, move, ends, ALU.add))
                settle()
                pool.tensor_tensor(diff[:, b, 0, :, cs], bracket[:, b, 1, :, cs], bracket[:, b, 2, :, cs],
                                   ALU.subtract).then_inc(sem("bracket_ready", i), 1)

            for slot in schedule():
                for block in slot:
                    for i, k in block:
                        if k == 5:
                            for t in POOL_SUBS:
                                n = i * GT + t
                                pool.wait_ge(sem("marked"), n + 1)
                                w = work[:, n % WORK, :]
                                pool.tensor_tensor(w, scores[:, i // NG, (i % NG) * GT + t, 0:T], w, ALU.subtract).then_inc(sem("pool_subs"), 1)
                    for i, k in block:
                        if k == 0:
                            first_guess(i)
                        if k in ACT_COUNTS:
                            draw_in(i, k - 1)

        @block.scalar
        def _(act):
            def out_of(ins, *key):
                ins.then_inc(free_of(*key), 1)

            emptied_o2 = filled(act, "o2")
            out_of(act.activation(o2.rearrange("p b n -> p (b n)"), emptied_o2[0:16, 0:NB * 64], ACT.Copy), "o2")
            for gh in range(2):
                pt = filled(act, "t0", gh)
                out_of(act.activation(t0[:, gh, :, :].rearrange("p b n -> p (b n)"), pt[0:48, 0:NB * P], ACT.Copy), "t0", gh)
                for b in range(NB):
                    py = filled(act, "y", gh, b)
                    if gh:
                        act.wait_ge(sem("y_used"), b + 1)
                    act.activation(y_a[:, b, :], py[:, 0:P], ACT.Identity, bias=b_tok01[:, 0:1]).then_inc(sem("y_a_ready"), 1)
                    out_of(act.activation(y_b[:, b, :], py[0:64, P:2 * P], ACT.Identity, bias=b_tok2[:, 0:1]), "y", gh, b)

            def norm_std(i, b):
                act.wait_ge(sem("moments_ready", i, b), 3)
                act.activation(std[:, b, :], moments[:, b, :, 1], ACT.Sqrt, bias=eps_col[:, 0:1]).then_inc(sem("std_ready", i, b), 1)

            def norm_out(i, b):
                px = filled(act, "xt", i, b, 0)
                out_of(act.activation(xT[:, b, 0, :], px[0:HF, 0:TP], ACT.Copy), "xt", i, b, 0)

            def att_out(i, b):
                px = filled(act, "yt", i, b, 0)
                out_of(act.activation(attT[:, b, 0, :], px[0:HF, 0:TP], ACT.Copy), "yt", i, b, 0)

            act.wait_ge(sem("eps_set"), 1)
            for b in range(NB):
                norm_std(0, b)
            for b in range(NB):
                norm_out(0, b)
            for b in range(NB):
                for j in range(0, 2 * NG, 2):
                    p = filled(act, "qk", 0, b, j)
                    out_of(act.activation(qk[:, b, j, 0:T], p[:, 0:T], ACT.Copy), "qk", 0, b, j)
                for h in range(NH):
                    n = b * NH + h
                    p = filled(act, "s0", b, h)
                    if n >= PMR:
                        act.wait_ge(sem("pm_ready"), n - PMR + 1)
                    out_of(act.activation(sq[:, n % PMR, :], p[:, 0:CAUSAL], ACT.Square, scale=0.25, bias=ones_col[:, 0:1]), "s0", b, h)
                att_out(0, b)
            for b in range(NB):
                norm_std(1, b)
            for b in range(NB):
                norm_out(1, b)
            for b in range(NB):
                act.wait_ge(sem("expert_known", b), 1)
                act.activation(exp0[:, b, :], lg0[:, b, 0:E0], ACT.Exp, bias=neg0[:, b:b + 1],
                               accum_out=sum0[:, b:b + 1]).then_inc(sem("sum0_ready", b), 1)
            for b in range(NB):
                act.wait_ge(sem("expert_in", b), 64)
                for f in range(NF):
                    p = filled(act, "up0", b, f)
                    out_of(act.activation(hid0[b][:, f, :], p[:, 0:T], ACT.Gelu, bias=b_up0[:, b, f:f + 1]), "up0", b, f)
            for b in range(NB):
                norm_std(2, b)
            act.wait_ge(sem("b_q_ready"), 1)
            for b in range(NB):
                norm_out(2, b)
                for j in range(NG):
                    p = filled(act, "qk", 1, b, j)
                    out_of(act.activation(qk[:, b, j, 0:T], p[:, 0:T], ACT.Identity, scale=0.25 * TINY,
                                          bias=b_q[:, j:j + 1]), "qk", 1, b, j)

            def exp_tile(i, t):
                b, n = i // NG, i * GT + t
                if n >= PMR:
                    act.wait_ge(sem("ps_ready"), n - PMR + 1)
                at = (i % NG) * GT + t
                act.activation(es[:, n % PMR, :], scores[:, b, at, 0:T], ACT.Exp, scale=1.0 / TINY,
                               bias=nbias[:, b, at:at + 1]).then_inc(sem("es_ready"), 1)

            def turn_tile(i, t):
                n = i * GT + t
                p = filled(act, "pt", *divmod(n, TILES))
                if n >= PMR:
                    act.wait_ge(sem("psT_used"), n - PMR + 1)
                out_of(act.activation(psT[:, n % PMR, :], p[:, 0:TP], ACT.Copy), "pt", *divmod(n, TILES))

            sign_count = 0
            for slot in schedule():
                for block in slot:
                    for i, k in block:
                        if k == 6:
                            act.wait_ge(sem("nbias_ready", i), 1)
                        if k in ACT_COUNTS and ACT_COUNTS[k]:
                            act.wait_ge(sem("guess_ready", i), k)
                    for t in range(GT):
                        for i, k in block:
                            b, at = i // NG, (i % NG) * GT + t
                            if k == 6:
                                exp_tile(i, t)
                                if t >= 2:
                                    turn_tile(i, t - 2)
                            if k in ACT_COUNTS and t < ACT_COUNTS[k]:
                                if sign_count >= 2:
                                    act.wait_ge(sem("act_counted"), sign_count - 1)
                                act.activation(signs[:, sign_count % 2, :], scores[:, b, at, 0:T], ACT.Sign, scale=-1.0,
                                               bias=bracket[:, b, 0, 0, at:at + 1],
                                               accum_out=bracket[:, b, 0, 1, at:at + 1]).then_inc(sem("act_counted"), 1)
                                sign_count += 1
                    for i, k in block:
                        if k == 6:
                            turn_tile(i, GT - 2)
                            turn_tile(i, GT - 1)
                            if i % NG == NG - 1:
                                att_out(1, i // NG)
            for b in range(NB):
                norm_std(3, b)
            for b in range(NB):
                norm_out(3, b)
                p = filled(act, "g1", b)
                out_of(act.activation(gT[:, b, 0:T], p[0:G1, 0:T], ACT.Gelu, bias=b_g1[:, 0:1]), "g1", b)
            for b in range(NB):
                emptied(act, "logits1", b)
                act.activation(e1[:, b, :, :], lg1[:, b, :, :], ACT.Exp).then_inc(sem("e1_ready", b), 1)
            for b in range(NB):
                for e in range(E1):
                    n = b * E1 + e
                    for c in range(2):
                        p = filled(act, "z", b, e, c)
                        if n >= 2:
                            filled(act, "up1", *divmod(n - 2, E1), 1)
                        out_of(act.activation(zT[:, n % 2, c, :], p[:, 0:T], ACT.Gelu, bias=b_z[:, e, c:c + 1]), "z", b, e, c)
            for b in range(NB):
                norm_std(4, b)

        @block.tensor
        def _(pe):
            def bank(*key):
                k, n = USES[key]
                if n:
                    pe.wait_ge(bank_free[k], n)
                return banks[:, k, :]

            def full(mm, *key):
                mm.then_inc(bank_full[USES[key][0]], 1)

            pe.wait_ge(sem("ident"), 2)
            pe.wait_ge(sem("seq1_ready"), 1)
            p = bank("t1")
            for b in range(NB):
                mm = pe.transpose(p[0:96, b * P:(b + 1) * P], seq1[:, b, :], ident[:])
            full(mm, "t1")
            pe.wait_ge(sem("seq2_ready"), 1)
            p = bank("t2")
            for b in range(NB):
                mm = pe.transpose(p[0:96, b * P:(b + 1) * P], seq2[:, b, :], ident[:])
            full(mm, "t2")
            loaded(pe, "tok")
            emptied(pe, "t1")
            p = bank("o1")
            for b in range(NB):
                for k in range(2):
                    mm = pe.matmul(p[0:64, b * 64:b * 64 + 64], t1[:, b, k, :], w_tok1[:, k, :], start=(k == 0), stop=(k == 1))
            full(mm, "o1")
            emptied(pe, "t2")
            p = bank("o2")
            for b in range(NB):
                for k in range(8):
                    mm = pe.matmul(p[0:16, b * 64:b * 64 + 64], t2[:, b, k, :], w_tok2[:, k, :], start=(k == 0), stop=(k == 7))
            full(mm, "o2")
            emptied(pe, "o1")
            emptied(pe, "o2")
            pe.wait_ge(sem("ones_set"), 1)
            for gh in range(2):
                half = slice(gh * P, gh * P + P)
                pe.wait_ge(sem("seq0_ready"), gh + 1)
                p = bank("t0", gh)
                for b in range(NB):
                    mm = pe.transpose(p[0:48, b * P:(b + 1) * P], seq0[:, gh, b, :], ident[:])
                full(mm, "t0", gh)
                emptied(pe, "t0", gh)
                for b in range(NB):
                    p = bank("y", gh, b)
                    pe.matmul(p[0:64, 0:P], w_tok0[:], t0[:, gh, b, :], start=True, stop=True)
                    pe.matmul(p[64:128, 0:P], o1[:, b, :], interp1[:, half], start=True, stop=True)
                    full(pe.matmul(p[0:64, P:2 * P], o2[:, b, :], interp2[:, half], start=True, stop=True), "y", gh, b)
                for b in range(NB):
                    p = bank("h", gh, b)
                    emptied(pe, "y", gh, b)
                    pe.matmul(p[:, 0:D], y_a[:, b, :], wf_a[:], start=True, stop=False)
                    pe.matmul(p[:, 0:D], y_b[:, b, :], wf_b[:], start=False, stop=False).then_inc(sem("y_used"), 1)
                    full(pe.matmul(p[:, 0:D], ones_row[:], bf_row[:], start=False, stop=True), "h", gh, b)

            def turn(src, name, ready, i, b):
                pe.wait_ge(ready, 3)
                for kc in range(2):
                    p = bank(name, i, b, kc)
                    for c in range(3):
                        mm = pe.transpose(p[0:HF, c * P:(c + 1) * P], src[:, b, c, kc * HF:(kc + 1) * HF], ident[:])
                    full(mm, name, i, b, kc)

            def token_sum(i, b):
                p = bank("xsum", i, b)
                for kc in range(2):
                    for c in range(3):
                        n = SIZES[c]
                        mm = pe.matmul(p[0:HF, kc:kc + 1], xhat[0:n, b, c, kc * HF:(kc + 1) * HF], ones_col[0:n, :],
                                       start=(c == 0), stop=(c == 2))
                full(mm, "xsum", i, b)

            def turned(i, b):
                for kc in range(2):
                    emptied(pe, "xt", i, b, kc)

            def qkv(i, b):
                turned(2 * i, b)
                n = T + i
                for j in range(2 * NG):
                    w = n if j >= NG else T
                    p = bank("qk", i, b, j)
                    if i and j == NG:
                        emptied(pe, "xsum", 2, b)
                    for kc in range(2):
                        mm = pe.matmul(p[:, 0:w], w_qk[i][:, kc, j, :], xT[:, b, kc, 0:w], start=(kc == 0), stop=(kc == 1))
                    full(mm, "qk", i, b, j)
                for part in range(2):
                    p = bank("v", i, b, part)
                    for c in ((0, 1), (2,))[part]:
                        m = SIZES[c]
                        at = D * (c % 2)
                        for kc in range(2):
                            mm = pe.matmul(p[0:m, at:at + D], xT[:, b, kc, c * P:c * P + m], w_v[i][:, kc, :],
                                           start=(kc == 0), stop=(kc == 1 and not i))
                        if i:
                            mm = pe.matmul(p[0:m, at:at + D], ones_row[:, 0:m], b_v[:], start=False, stop=True)
                    full(mm, "v", i, b, part)

            def proj(i, b):
                turn(att, "yt", sem("att_ready", i, b), i, b)
                for kc in range(2):
                    emptied(pe, "yt", i, b, kc)
                for part in range(2):
                    p = bank("o", i, b, part)
                    for c in ((0, 1), (2,))[part]:
                        m = SIZES[c]
                        at = D * (c % 2)
                        for kc in range(2):
                            mm = pe.matmul(p[0:m, at:at + D], attT[:, b, kc, c * P:c * P + m], w_o[i][:, kc, :],
                                           start=(kc == 0), stop=(kc == 1 and not i))
                        if i:
                            mm = pe.matmul(p[0:m, at:at + D], ones_row[:, 0:m], b_o[:], start=False, stop=True)
                    full(mm, "o", i, b, part)

            for b in range(NB):
                turn(xhat, "xt", sem("xhat_ready", 0, b), 0, b)
            loaded(pe, "att0")
            pe.wait_ge(sem("pads_set"), 1)
            for b in range(NB):
                qkv(0, b)
                for j in range(2 * NG):
                    emptied(pe, "qk", 0, b, j)

                def scores0(h):
                    g, r = h // HPG, 32 * (h % HPG)
                    p = bank("s0", b, h)
                    for c in range(3):
                        mm = pe.matmul(p[:, KEYAT[c]:KEYAT[c] + KEYW[c]], qk[r:r + HD, b, NG + g, c * P:(c + 1) * P],
                                       qk[r:r + HD, b, g, c * P:T], start=True, stop=True, tile_position=(r, 0))
                    full(mm, "s0", b, h)

                def values0(h):
                    n = b * NH + h
                    pe.wait_ge(sem("pm_ready"), n + 1)
                    w = pm[:, n % PMR, :]
                    for qc in range(3):
                        m = SIZES[qc]
                        dst = y01[:, qc, h, :] if qc < 2 else y2[:, h, :]
                        for kc in range(qc + 1):
                            at = KEYAT[kc] + (qc - kc) * P
                            k = SIZES[kc]
                            mm = pe.matmul(dst, w[0:k, at:at + m], vals[0:k, b, kc, h, :], start=(kc == 0), stop=(kc == qc))
                    mm.then_inc(sem("pm_used"), 1)

                for part in range(2):
                    emptied(pe, "v", 0, b, part)
                if b:
                    pe.wait_ge(sem("att_ready", 0, b - 1), 3)
                for h in range(NH + 2):
                    if h < NH:
                        scores0(h)
                    if h >= 2:
                        values0(h - 2)
                proj(0, b)
            loaded(pe, "ffn0")
            for b in range(NB):
                turn(xhat, "xt", sem("xhat_ready", 1, b), 1, b)
                token_sum(1, b)
                p = bank("logits0", b)
                emptied(pe, "xsum", 1, b)
                for kc in range(2):
                    mm = pe.matmul(p[0:1, 0:E0], xmean[:, b, kc:kc + 1], w_g0[:, kc, :], start=(kc == 0), stop=(kc == 1))
                full(mm, "logits0", b)
            for b in range(NB):
                p = bank("gate0", b)
                pe.wait_ge(sem("wt0_ready", b), 1)
                full(pe.matmul(p[:, 0:1], ones_row[:], wt0[:, b:b + 1], start=True, stop=True), "gate0", b)
            for b in range(NB):
                turned(1, b)
                pe.wait_ge(sem("expert_in", b), 64)
                for f in range(NF):
                    p = bank("up0", b, f)
                    for kc in range(2):
                        mm = pe.matmul(p[:, 0:T], w_up0[b][:, kc, f * P:(f + 1) * P], xT[:, b, kc, 0:T], start=(kc == 0), stop=(kc == 1))
                    full(mm, "up0", b, f)
                for f in range(NF):
                    emptied(pe, "up0", b, f)
                for part in range(2):
                    p = bank("down0", b, part)
                    for c in ((0, 1), (2,))[part]:
                        m = SIZES[c]
                        at = D * (c % 2)
                        for f in range(NF):
                            pe.matmul(p[0:m, at:at + D], hid0[b][:, f, c * P:c * P + m], w_dn0[b][:, f, :], start=(f == 0), stop=False)
                        mm = pe.matmul(p[0:m, at:at + D], ones_row[:, 0:m], b_dn0[:, b, :], start=False, stop=True)
                    full(mm, "down0", b, part)
            loaded(pe, "att1")
            for b in range(NB):
                turn(xhat, "xt", sem("xhat_ready", 2, b), 2, b)
                token_sum(2, b)
                qkv(1, b)
                for j in range(2 * NG):
                    emptied(pe, "qk", 1, b, j)

            def scores1(i, t):
                b, t = divmod(i * GT + t, TILES)
                g, hh, c = tile_heads()[t]
                p = bank("s1", b, t)
                for one in ([hh] if hh is not None else range(HPG)):
                    r = 32 * one
                    m = SIZES[c]
                    to = 0 if hh is not None else r
                    mm = pe.matmul(p[to:to + m, 0:T + 1], qk[r:r + HD, b, g, c * P:c * P + m],
                                   qk[r:r + HD, b, NG + g, 0:T + 1], start=True, stop=True, tile_position=(r, to))
                full(mm, "s1", b, t)

            def turn_probs(i, t):
                n = i * GT + t
                pe.wait_ge(sem("ps_ready"), n + 1)
                p = bank("pt", *divmod(n, TILES))
                for kc in range(3):
                    mm = pe.transpose(p[:, kc * P:(kc + 1) * P], ps[:, n % PMR, kc * P:(kc + 1) * P], ident[:])
                full(mm, "pt", *divmod(n, TILES))

            def values1(i, t):
                n = i * GT + t
                b, t = divmod(n, TILES)
                g, hh, c = tile_heads()[t]
                emptied(pe, "pt", b, t)
                for one in ([hh] if hh is not None else range(HPG)):
                    h = g * HPG + one
                    m = SIZES[c]
                    at = 0 if hh is not None else 32 * one
                    dst = y01[:, c, h, :] if hh is not None else y2[:, h, :]
                    for kc in range(3):
                        k = SIZES[kc]
                        mm = pe.matmul(dst, psT[0:k, n % PMR, kc * P + at:kc * P + at + m], vals[0:k, b, kc, h, :],
                                       start=(kc == 0), stop=(kc == 2))
                mm.then_inc(sem("psT_used"), 1)

            for slot in schedule():
                for block in slot:
                    for i, k in block:
                        if k == 6:
                            pe.wait_ge(sem("hits_ready"), i + 1)
                            p = bank("hits", i)
                            full(pe.matmul(p[0:1, 0:1], hits[:, i // NG, i % NG:i % NG + 1], ones_col[:], start=True, stop=True), "hits", i)
                            if i % NG == 0:
                                b = i // NG
                                for part in range(2):
                                    emptied(pe, "v", 1, b, part)
                                pe.wait_ge(sem("att_ready", *((1, b - 1) if b else (0, NB - 1))), 3)
                    for t in range(GT):
                        for i, k in block:
                            if k == 6:
                                turn_probs(i, t)
                                if t >= 2:
                                    values1(i, t - 2)
                            if k == 0:
                                scores1(i, t)
                    for i, k in block:
                        if k == 6:
                            values1(i, GT - 2)
                            values1(i, GT - 1)
                            if i % NG == NG - 1:
                                proj(1, i // NG)
            loaded(pe, "ffn1")
            for b in range(NB):
                turn(xhat, "xt", sem("xhat_ready", 3, b), 3, b)
                turned(3, b)
                p = bank("g1", b)
                for kc in range(2):
                    mm = pe.matmul(p[0:G1, 0:T], w_g1[:, kc, :], xT[:, b, kc, 0:T], start=(kc == 0), stop=(kc == 1))
                full(mm, "g1", b)
                p = bank("logits1", b)
                emptied(pe, "g1", b)
                for c in range(3):
                    pe.matmul(p[:, c * E1:(c + 1) * E1], gT[:, b, c * P:(c + 1) * P], w_l1[:], start=True, stop=False)
                    mm = pe.matmul(p[:, c * E1:(c + 1) * E1], ones_row[:], b_l1[:], start=False, stop=True)
                full(mm, "logits1", b)
            for b in range(NB):
                for e in range(E1):
                    n = b * E1 + e
                    for f in range(2):
                        p = bank("z", b, e, f)
                        for kc in range(2):
                            mm = pe.matmul(p[:, 0:T], w_z[:, e, kc, f * P:(f + 1) * P], xT[:, b, kc, 0:T], start=(kc == 0), stop=(kc == 1))
                        full(mm, "z", b, e, f)
                    for part in range(2):
                        p = bank("up1", b, e, part)
                        for f in range(2):
                            emptied(pe, "z", b, e, f)
                        for c in ((0, 1), (2,))[part]:
                            m = SIZES[c]
                            at = D * (c % 2)
                            for f in range(2):
                                mm = pe.matmul(p[0:m, at:at + D], zT[:, n % 2, f, c * P:c * P + m], w_u[:, e, f, :],
                                               start=(f == 0), stop=(f == 1))
                        full(mm, "up1", b, e, part)

        @block.vector
        def _(dve):
            steps = [0]

            def step(ins):
                steps[0] += 1
                ins.then_inc(sem("dve_step"), 1)

            def settle():
                dve.wait_ge(sem("dve_step"), steps[0])

            def out_of(ins, *key):
                ins.then_inc(free_of(*key), 1)

            dve.memset(ones_row[:], 1.0).then_inc(sem("ones_set"), 1)
            dve.memset(ones_col[:], 1.0)
            dve.memset(eps_col[:], 1e-5).then_inc(sem("eps_set"), 1)
            dve.memset(vals[:], 1.0).then_inc(sem("vals_set"), 1)
            dve.memset(att[:, :, 2, :], 0.0).then_inc(sem("att_zero"), 1)
            dve.memset(ps[:, :, T:TP], 0.0)
            dve.memset(gT[:, :, T:TP], 0.0)
            dve.memset(lg0[:], -3e38).then_inc(sem("lg0_set"), 1)
            dve.memset(qk[:, :, :, T:TP], 0.0).then_inc(sem("pads_set"), 1)

            def by_sequence(dst, src, f, done):
                dve.tensor_copy(dst.rearrange("p b (k f) -> p k b f", f=f), src.rearrange("p k (b f) -> p k b f", b=NB)).then_inc(done, 1)

            dve.wait_ge(sem("patch1_in"), 128)
            by_sequence(seq1, patch1, 12, sem("seq1_ready"))
            p = filled(dve, "t1")
            out_of(dve.tensor_copy(t1.rearrange("p b k n -> p (b k n)"), p[0:96, 0:NB * P]), "t1")
            dve.wait_ge(sem("patch2_in"), 32)
            by_sequence(seq2, patch2, 48, sem("seq2_ready"))
            p = filled(dve, "t2")
            out_of(dve.tensor_copy(t2.rearrange("p b k n -> p (b k n)"), p[0:96, 0:NB * P]), "t2")
            p = filled(dve, "o1")
            out_of(dve.tensor_copy(o1.rearrange("p b n -> p (b n)"), p[0:64, 0:NB * 64]), "o1")
            for gh in range(2):
                dve.wait_ge(sem("patch0_in", gh), 256)
                by_sequence(seq0[:, gh, :, :], patch0[:, gh, :, :], 3, sem("seq0_ready"))
                for b in range(NB):
                    p = filled(dve, "h", gh, b)
                    out_of(dve.tensor_copy(resid[:, b, gh, :], p[:, 0:D]), "h", gh, b)

            def layernorm(i, b, src, dst):
                for c in range(3):
                    step(dve.bn_stats(stats[:, b, c, :], src[:, b, c, :]))
                settle()
                for c in range(3):
                    dve.bn_aggr(moments[:, b, c, :], stats[:, b, c, :]).then_inc(sem("moments_ready", i, b), 1)
                dve.wait_ge(sem("std_ready", i, b), 1)
                step(dve.reciprocal(rstd[:, b, :], std[:, b, :]))
                settle()
                for c in range(3):
                    dve.tensor_scalar(dst[:, b, c, :], src[:, b, c, :], moments[:, b, c, 0:1], rstd[:, b, c:c + 1],
                                      ALU.subtract, ALU.mult).then_inc(sem("xhat_ready", i, b), 1)

            def turned_half(i, b):
                p = filled(dve, "xt", i, b, 1)
                out_of(dve.tensor_copy(xT[:, b, 1, :], p[0:HF, 0:TP]), "xt", i, b, 1)

            def values(i, b):
                p = filled(dve, "v", i, b, 0)
                out_of(dve.tensor_copy(vals[:, b, 0:2, :, 0:HD], p[:, 0:2 * D].rearrange("p (c h w) -> p c h w", c=2, h=NH)), "v", i, b, 0)
                p = filled(dve, "v", i, b, 1)
                out_of(dve.tensor_copy(vals[0:TXT, b, 2, :, 0:HD], p[0:TXT, 0:D].rearrange("p (h w) -> p h w", h=NH)), "v", i, b, 1)

            def normalize(i, b, last_used, eps):
                dve.wait_ge(*last_used)
                if eps:
                    step(dve.tensor_scalar(den[:, 0:2, :], y01[:, :, :, HD], eps, None, ALU.add))
                    step(dve.tensor_scalar(den[0:TXT, 2, :], y2[:, :, HD], eps, None, ALU.add))
                else:
                    step(dve.tensor_copy(den[:, 0:2, :], y01[:, :, :, HD]))
                    step(dve.tensor_copy(den[0:TXT, 2, :], y2[:, :, HD]))
                settle()
                step(dve.reciprocal(rden[:, 0:2, :], den[:, 0:2, :]))
                step(dve.reciprocal(rden[0:TXT, 2, :], den[0:TXT, 2, :]))
                settle()
                ready = sem("att_ready", i, b)
                for c in range(3):
                    m = SIZES[c]
                    src = y01[:, c, :, 0:HD] if c < 2 else y2[:, :, 0:HD]
                    dve.tensor_tensor(att[0:m, b, c, :].rearrange("p (h w) -> p h w", h=NH), src,
                                      rden[0:m, c, :].unsqueeze(2).to_broadcast([m, NH, HD]), ALU.mult).then_inc(ready, 1)

            def add_projection(i, b):
                p = filled(dve, "yt", i, b, 1)
                out_of(dve.tensor_copy(attT[:, b, 1, :], p[0:HF, 0:TP]), "yt", i, b, 1)
                add_chunks("o", i, b)

            def add_chunks(*key):
                b = key[-1]
                p = filled(dve, *key, 0)
                r = resid[:, b, 0:2, :].rearrange("p c n -> p (c n)")
                dve.tensor_tensor(r, p[:, 0:2 * D], r, ALU.add).then_inc(free_of(*key, 0), 1)
                p = filled(dve, *key, 1)
                r = resid[0:TXT, b, 2, :]
                dve.tensor_tensor(r, p[0:TXT, 0:D], r, ALU.add).then_inc(free_of(*key, 1), 1)
                for n in range(2):
                    emptied(dve, *key, n)

            for gh in range(2):
                for b in range(NB):
                    emptied(dve, "h", gh, b)
            dve.wait_ge(sem("text_in"), 32)
            for b in range(NB):
                layernorm(0, b, resid, xhat)
            for b in range(NB):
                turned_half(0, b)
            dve.wait_ge(sem("vals_set"), 1)
            loaded(dve, "att0")
            for b in range(NB):
                for j in range(1, 2 * NG, 2):
                    p = filled(dve, "qk", 0, b, j)
                    out_of(dve.tensor_copy(qk[:, b, j, 0:T], p[:, 0:T]), "qk", 0, b, j)
                values(0, b)
                for h in range(NH):
                    n = b * NH + h
                    emptied(dve, "s0", b, h)
                    if n >= PMR:
                        dve.wait_ge(sem("pm_used"), n - PMR + 1)
                    dve.scalar_tensor_tensor(pm[:, n % PMR, :], sq[:, n % PMR, :], 1.0, mask[:], ALU.add, ALU.mult).then_inc(sem("pm_ready"), 1)
                normalize(0, b, (sem("pm_used"), (b + 1) * NH), 2e-12)
                add_projection(0, b)
            for b in range(NB):
                layernorm(1, b, resid, xhat)
            dve.wait_ge(sem("lg0_set"), 1)
            for b in range(NB):
                turned_half(1, b)
                p = filled(dve, "xsum", 1, b)
                out_of(dve.tensor_scalar(xmean[:, b, :], p[0:HF, 0:2], 1.0 / T, None, ALU.mult), "xsum", 1, b)
                p = filled(dve, "logits0", b)
                out_of(dve.tensor_copy(lg0[:, b, 0:E0], p[0:1, 0:E0]), "logits0", b)
                emptied(dve, "logits0", b)
                step(dve.max(top0[:, b, :], lg0[:, b, :]))
                settle()
                step(dve.max_index(arg0[:, b, :], top0[:, b, :], lg0[:, b, :]))
                settle()
                dve.tensor_scalar(neg0[:, b:b + 1], top0[:, b, 0:1], -1.0, None, ALU.mult).then_inc(sem("expert_known", b), 1)
            for b in range(NB):
                dve.wait_ge(sem("sum0_ready", b), 1)
                dve.reciprocal(wt0[:, b:b + 1], sum0[:, b:b + 1]).then_inc(sem("wt0_ready", b), 1)
                p = filled(dve, "gate0", b)
                out_of(dve.tensor_copy(wcol0[:, b:b + 1], p[:, 0:1]), "gate0", b)
            for b in range(NB):
                emptied(dve, "gate0", b)
                for part in range(2):
                    m = SIZES[2 * part]
                    p = filled(dve, "down0", b, part)
                    r = resid[0:m, b, 0:2, :] if part == 0 else resid[0:m, b, 2:3, :]
                    r = r.rearrange("p c n -> p (c n)")
                    out_of(dve.scalar_tensor_tensor(r, p[0:m, 0:D * (2 - part)], wcol0[0:m, b:b + 1], r, ALU.mult, ALU.add), "down0", b, part)
                for part in range(2):
                    emptied(dve, "down0", b, part)
            loaded(dve, "att1")
            step(dve.tensor_scalar(count_of[:], iota8[:], -1.0, HITS, ALU.mult, ALU.add))
            dve.tensor_scalar(b_q[:], b_qk[:, 0:NG], 0.25 * TINY, None, ALU.mult).then_inc(sem("b_q_ready"), 1)
            for b in range(NB):
                layernorm(2, b, resid, xhat)
            for b in range(NB):
                turned_half(2, b)
                p = filled(dve, "xsum", 2, b)
                emptied(dve, "xt", 2, b, 0)
                emptied(dve, "xt", 2, b, 1)
                dve.tensor_scalar(xT[:, b, :, T], p[0:HF, 0:2], 1.0 / T, None, ALU.mult).then_inc(free_of("xsum", 2, b), 1)
                for j in range(NG, 2 * NG):
                    p = filled(dve, "qk", 1, b, j)
                    out_of(dve.tensor_scalar(qk[:, b, j, 0:T + 1], p[:, 0:T + 1], b_qk[:, j:j + 1], None, ALU.add), "qk", 1, b, j)
                values(1, b)

            def pick_exactly(b, g):
                rounds = (TOPK + 7) // 8
                with dve.Fori(0, GT) as t:
                    dve.sem_clear(sem("pick_step"))
                    dve.tensor_copy(work[:, 0, :], scores[:, b, g * GT:(g + 1) * GT, 0:T][:, bass.ds(t, 1), :].rearrange("p a n -> p (a n)")).then_inc(sem("pick_step"), 1)
                    n = 1
                    for r in range(rounds):
                        dve.wait_ge(sem("pick_step"), n)
                        dve.max(top8[:], work[:, r % 2, :]).then_inc(sem("pick_step"), 1)
                        n += 1
                        dve.wait_ge(sem("pick_step"), n)
                        if r < rounds - 1:
                            dve.match_replace(work[:, (r + 1) % 2, :], top8[:], work[:, r % 2, :], -3e38).then_inc(sem("pick_step"), 1)
                            n += 1
                    at = (TOPK - 1) % 8
                    dve.tensor_copy(thr[:, b, g * GT:(g + 1) * GT][:, bass.ds(t, 1)], top8[:, at:at + 1]).then_inc(sem("pick_step"), 1)
                    dve.wait_ge(sem("pick_step"), n + 1)

            def tile_row(i, t):
                return scores[:, i // NG, (i % NG) * GT + t, 0:T]

            def row_max(i, t):
                b, at = divmod(i * GT + t, TILES)
                p = filled(dve, "s1", b, at)
                out_of(dve.tensor_scalar(scores[:, b, at, 0:T + 1], p[:, 0:T + 1], 1.0, None, ALU.mult, ALU.max,
                                         accum_out=smax[:, b, at:at + 1]), "s1", b, at)

            def next_guess(i, r):
                b, g = divmod(i, NG)
                cs = slice(g * GT, (g + 1) * GT)
                dve.wait_ge(sem("bracket_ready", i), r)
                q = diff[:, b, 1, 0, cs]
                step(dve.reciprocal(q, diff[:, b, 0, 1, cs]))
                settle()
                step(dve.tensor_tensor(q, bracket[:, b, 1, 1, cs], q, ALU.mult))
                settle()
                step(dve.tensor_tensor(q, q, diff[:, b, 0, 0, cs], ALU.mult))
                settle()
                dve.tensor_tensor(bracket[:, b, 0, 0, cs], bracket[:, b, 1, 0, cs], q, ALU.subtract).then_inc(sem("guess_ready", i), 1)

            def count_into(marks, i, t):
                b, at = divmod(i * GT + t, TILES)
                return dve.tensor_scalar(marks, tile_row(i, t), bracket[:, b, 0, 0, at:at + 1], -AIM,
                                         ALU.is_ge, ALU.add, accum_out=bracket[:, b, 0, 1, at:at + 1])

            def mark(i, t):
                n = i * GT + t
                if n >= WORK:
                    settle()
                count_into(work[:, n % WORK, :], i, t).then_inc(sem("marked"), 1)

            def sub(i, t):
                n = i * GT + t
                dve.wait_ge(sem("marked"), n + 1)
                w = work[:, n % WORK, :]
                dve.tensor_tensor(w, tile_row(i, t), w, ALU.subtract).then_inc(sem("dve_subs"), 1)

            def next8(i, t):
                n = i * GT + t
                if t in POOL_SUBS:
                    dve.wait_ge(sem("pool_subs"), i * len(POOL_SUBS) + POOL_SUBS.index(t) + 1)
                else:
                    dve.wait_ge(sem("dve_subs"), n + 1 - i * len(POOL_SUBS) - len([k for k in POOL_SUBS if k < t]))
                step(dve.max(below8[:, (i % NG) * GT + t, :], work[:, n % WORK, :]))

            def pick(i):
                b, g = divmod(i, NG)
                cs = slice(g * GT, (g + 1) * GT)
                dve.wait_ge(sem("marked"), (i + 1) * GT)
                step(dve.tensor_tensor(hit8[:], count_of[:].unsqueeze(1).to_broadcast([P, GT, 8]),
                                       bracket[:, b, 0, 1, cs].unsqueeze(2).to_broadcast([P, GT, 8]), ALU.is_equal))
                settle()
                dve.tensor_reduce(hits[:, b, g:g + 1], hit8[:].rearrange("p t k -> p (t k)"), AX.X, ALU.add).then_inc(sem("hits_ready"), 1)
                step(dve.tensor_tensor(below8[:, cs, :], below8[:, cs, :], hit8[:], ALU.mult))
                settle()
                step(dve.tensor_reduce(thr[:, b, cs], below8[:, cs, :], AX.X, ALU.add))

            def check(i):
                p = filled(dve, "hits", i)
                out_of(dve.tensor_copy(all_hits[:], p[0:1, 0:1]), "hits", i)
                emptied(dve, "hits", i)
                settle()
                found = dve.value_load(all_hits[0:1, 0:1], min_val=0, max_val=P * GT)
                with dve.If(found < P * GT):
                    pick_exactly(*divmod(i, NG))

            def mask_tile(i, t):
                n = i * GT + t
                at = n % TILES
                dve.wait_ge(sem("es_ready"), n + 1)
                if n >= PMR:
                    filled(dve, "pt", *divmod(n - PMR, TILES))
                dve.scalar_tensor_tensor(ps[:, n % PMR, 0:T], tile_row(i, t), thr[:, i // NG, at:at + 1], es[:, n % PMR, :],
                                         ALU.is_ge, ALU.mult).then_inc(sem("ps_ready"), 1)

            mark_count = 0
            for slot in schedule():
                for block in slot:
                    for i, k in block:
                        if k >= 2 and k <= 5:
                            next_guess(i, k - 1)
                    for i, k in block:
                        if k >= 1 and k <= 5:
                            dve.wait_ge(sem("guess_ready", i), k)
                        if k == 6:
                            check(i)
                    for t in range(GT + 2):
                        for i, k in block:
                            if k == 5:
                                if t >= 2:
                                    next8(i, t - 2)
                                if t >= 1 and t <= GT and t - 1 not in POOL_SUBS:
                                    sub(i, t - 1)
                                if t < GT:
                                    mark(i, t)
                            elif t < GT and k in ACT_COUNTS and t >= ACT_COUNTS[k]:
                                if mark_count >= 2:
                                    dve.wait_ge(sem("dve_counted"), mark_count - 1)
                                count_into(marks[:, mark_count % 2, :], i, t).then_inc(sem("dve_counted"), 1)
                                mark_count += 1
                            elif t < GT and k == 6:
                                mask_tile(i, t)
                            elif t < GT and k == 0:
                                row_max(i, t)
                    for i, k in block:
                        if k == 5:
                            pick(i)
                        if k == 6 and i % NG == NG - 1:
                            b = i // NG
                            normalize(1, b, (sem("psT_used"), (b + 1) * TILES), 0.0)
                            add_projection(1, b)
            for b in range(NB):
                layernorm(3, b, resid, xhat)
            loaded(dve, "ffn1")
            for b in range(NB):
                turned_half(3, b)
            for b in range(NB):
                p = filled(dve, "logits1", b)
                pl = p[:, 0:3 * E1].rearrange("p (c e) -> p c e", c=3)
                step(dve.tensor_reduce(max1[:, b, :], pl, AX.X, ALU.max))
                settle()
                dve.tensor_tensor(lg1[:, b, :, :], pl, max1[:, b, :].unsqueeze(2).to_broadcast([P, 3, E1]), ALU.subtract).then_inc(free_of("logits1", b), 1)
                emptied(dve, "logits1", b)
                for c in range(3):
                    step(dve.max(top1[:, b, c, :], lg1[:, b, c, :]))
                settle()
                for c in range(3):
                    step(dve.max_index(arg1[:, b, c, :], top1[:, b, c, :], lg1[:, b, c, :]))
                settle()
                step(dve.tensor_copy(arg1f[:, b, :, :], arg1[:, b, :, 0:2]))
                settle()
                for k in range(2):
                    step(dve.tensor_tensor(hit[:, b, k, :, :], iota8[:].unsqueeze(1).to_broadcast([P, 3, E1]),
                                           arg1f[:, b, :, k:k + 1].to_broadcast([P, 3, E1]), ALU.is_equal))
                settle()
                step(dve.tensor_tensor(hit[:, b, 0, :, :], hit[:, b, 0, :, :], hit[:, b, 1, :, :], ALU.add))
                settle()
                dve.wait_ge(sem("e1_ready", b), 1)
                step(dve.tensor_tensor(w1[:, b, :, :], e1[:, b, :, :], hit[:, b, 0, :, :], ALU.mult))
                step(dve.tensor_reduce(z1[:, b, :], e1[:, b, :, :], AX.X, ALU.add))
                settle()
                step(dve.tensor_reduce(s1[:, b, :], w1[:, b, :, :], AX.X, ALU.add))
                settle()
                step(dve.scalar_tensor_tensor(s1[:, b, :], z1[:, b, :], 1e-8, s1[:, b, :], ALU.mult, ALU.add))
                settle()
                step(dve.reciprocal(s1[:, b, :], s1[:, b, :]))
                settle()
                step(dve.tensor_tensor(w1[:, b, :, :], w1[:, b, :, :], s1[:, b, :].unsqueeze(2).to_broadcast([P, 3, E1]), ALU.mult))
                settle()
            for b in range(NB):
                for e in range(E1):
                    if e:
                        emptied(dve, "up1", b, e - 1, 0)
                        emptied(dve, "up1", b, e - 1, 1)

                    def add_expert(c, p):
                        m, at = SIZES[c], D * (c % 2)
                        return dve.scalar_tensor_tensor(acc[0:m, b, c, :], p[0:m, at:at + D], w1[0:m, b, c, e:e + 1],
                                                        acc[0:m, b, c, :], ALU.mult, ALU.add)

                    p = filled(dve, "up1", b, e, 0)
                    add_expert(0, p)
                    out_of(add_expert(1, p), "up1", b, e, 0)
                    p = filled(dve, "up1", b, e, 1)
                    out_of(add_expert(2, p), "up1", b, e, 1)
            for b in range(NB):
                for part in range(2):
                    emptied(dve, "up1", b, E1 - 1, part)
                layernorm(4, b, acc, fin)
                dve.wait_ge(sem("xhat_ready", 4, b), 3)
                f, r = fin[:, b, :, :], resid[:, b, :, :]
                step(dve.tensor_tensor(f, f, gamma[:].unsqueeze(1).to_broadcast([P, 3, D]), ALU.mult))
                step(dve.tensor_tensor(r, r, beta[:].unsqueeze(1).to_broadcast([P, 3, D]), ALU.add))
                settle()
                dve.tensor_tensor(f, f, r, ALU.add).then_inc(sem("fin_ready", b), 1)


def kernel(x, txt, L0_tok_W0, L0_tok_b0, L0_tok_W1, L0_tok_b1, L0_tok_W2, L0_tok_b2, L0_tok_Wf, L0_tok_bf,
           L0_tok_idx0, L0_tok_idx1, L0_tok_idx2, L0_attn_Wq, L0_attn_Wk, L0_attn_Wv, L0_attn_Wo,
           L0_ffn_Wg, L0_ffn_W1, L0_ffn_b1, L0_ffn_W2, L0_ffn_b2, L1_attn_W_qkv, L1_attn_b_qkv,
           L1_attn_W_proj, L1_attn_b_proj, L1_ffn_w1, L1_ffn_b1, L1_ffn_w2, L1_ffn_b2, L1_ffn_down_w,
           L1_ffn_down_b, L1_ffn_up_w, L1_ffn_gamma, L1_ffn_beta):
    import numpy as np
    import concourse.bacc as bacc
    from concourse.bass_utils import run_bass_kernel_spmd as run

    def patches(p):
        h = 64 // p
        return x.reshape(NB, 3, h, p, h, p).transpose(2, 4, 0, 3, 5, 1).reshape(h * h, NB * p * p * 3)

    def halves(w):
        return w.reshape(2, HF, -1).transpose(1, 0, 2)

    def heads(w):
        o = np.zeros(w.shape[:-1] + (NH, 32), w.dtype)
        o[..., 0:HD] = w.reshape(w.shape[:-1] + (NH, HD))
        return o.reshape(w.shape[:-1] + (NH * 32,))

    def interp(n):
        pos = np.clip((np.arange(IMG, dtype=np.float32) + 0.5) * (n / IMG) - 0.5, 0.0, n - 1)
        i0 = np.floor(pos).astype(np.int32)
        i1 = np.minimum(i0 + 1, n - 1)
        w = (pos - i0).astype(np.float32)
        m = np.zeros((n, IMG), np.float32)
        m[i0, np.arange(IMG)] += 1.0 - w
        m[i1, np.arange(IMG)] += w
        return m

    def qk_weights(wq, wk):
        return np.concatenate([halves(heads(wq)), halves(heads(wk))], axis=2).reshape(HF, 2, 2 * NG, P)

    tri = (np.arange(T)[None, :] >= np.arange(P)[:, None]).astype(np.float32)
    qkv_w, qkv_b = L1_attn_W_qkv, L1_attn_b_qkv
    arrays = {
        "x0": patches(1), "x1": patches(2), "x2": patches(4), "txt": txt,
        "idx": np.concatenate([
            L0_tok_idx0.reshape(2, P, 16).transpose(1, 0, 2).reshape(P, 32),
            L0_tok_idx1.reshape(64, 2, 8).transpose(1, 0, 2).reshape(P, 8),
            L0_tok_idx2.reshape(16, 8, 2).transpose(1, 0, 2).reshape(P, 2)], axis=1),
        "w_tok0": L0_tok_W0.T, "w_tok1": L0_tok_W1.T.reshape(2, 96, 64).transpose(1, 0, 2),
        "w_tok2": L0_tok_W2.T.reshape(8, 96, 64).transpose(1, 0, 2),
        "b_tok01": np.concatenate([L0_tok_b0, L0_tok_b1])[:, None], "b_tok2": L0_tok_b2[:, None],
        "wf_a": L0_tok_Wf.T[0:P], "wf_b": L0_tok_Wf.T[P:D], "bf_row": L0_tok_bf[None, :],
        "interp1": interp(64), "interp2": interp(16),
        "mask": np.concatenate([tri[:, 0:w] for w in KEYW], axis=1),
        "iota8": np.tile(np.arange(E1, dtype=np.float32), (P, 1)),
        "w_qk0": qk_weights(L0_attn_Wq.T, L0_attn_Wk.T), "w_v0": halves(L0_attn_Wv.T), "w_o0": halves(L0_attn_Wo.T),
        "w_qk1": qk_weights(qkv_w[:, 0:D], qkv_w[:, D:2 * D]), "w_v1": halves(qkv_w[:, 2 * D:]),
        "w_o1": halves(L1_attn_W_proj),
        "b_qk": np.concatenate([heads(qkv_b[0:D]), heads(qkv_b[D:2 * D])]).reshape(2 * NG, P).T,
        "b_v": qkv_b[None, 2 * D:], "b_o": L1_attn_b_proj[None, :],
        "w_g0": halves(L0_ffn_Wg.T),
        "w_up0": L0_ffn_W1.reshape(E0, 2, HF, F0).transpose(0, 2, 1, 3),
        "b_up0": L0_ffn_b1.reshape(E0, NF, P).transpose(0, 2, 1),
        "w_dn0": L0_ffn_W2.reshape(E0, NF, P, D).transpose(0, 2, 1, 3), "b_dn0": L0_ffn_b2,
        "w_g1": halves(L1_ffn_w1), "b_g1": L1_ffn_b1[:, None], "w_l1": L1_ffn_w2, "b_l1": L1_ffn_b2[None, :],
        "w_z": L1_ffn_down_w.reshape(E1, 2, HF, D1).transpose(2, 0, 1, 3),
        "b_z": L1_ffn_down_b.reshape(E1, 2, P).transpose(2, 0, 1),
        "w_u": L1_ffn_up_w.reshape(E1, 2, P, D).transpose(2, 0, 1, 3),
        "gamma": np.broadcast_to(L1_ffn_gamma, (P, D)), "beta": np.broadcast_to(L1_ffn_beta, (P, D)),
    }
    nc = bacc.Bacc("TRN2", target_bir_lowering=False, num_devices=1)
    arrays = {f"in_{k}": np.ascontiguousarray(v) for k, v in arrays.items()}
    aps = {k[3:]: nc.dram_tensor(k, v.shape, mybir.dt.from_np(v.dtype), kind="ExternalInput").ap() for k, v in arrays.items()}
    out = nc.dram_tensor("out_0", (NB, T, D), F32, kind="ExternalOutput").ap()
    fusion_program(nc, aps, out)
    r = run(nc, [arrays], core_ids=[0])
    return r.results[0]["out_0"]
```

```python
from contextlib import ExitStack

import concourse.bass as bass
from concourse import mybir

F32 = mybir.dt.float32
BF16 = mybir.dt.bfloat16
I32 = mybir.dt.int32
U32 = mybir.dt.uint32
ALU = mybir.AluOpType
ACT = mybir.ActivationFunctionType
AX = mybir.AxisListType

NB = 2
P = 128
IMG, TXT = 256, 32
T = IMG + TXT
TP = 3 * P
SIZES = (P, P, TXT)
D = 192
HF = D // 2
NH, HD = 12, 16
HPG = 4
NG = NH // HPG
VW = 32
F0 = 768
NF = F0 // P
E0 = 3
E1, D1 = 8, 256
G1 = 96
TOPK = 115
KEYW = (T, T - P, TXT)
KEYAT = (0, T, 2 * T - P)
CAUSAL = sum(KEYW)
TILES = 2 * NH + NG
SW = T + 2
GROUP = 16
LO = 32
PIX = NB * 3
PICKS = (7, 3)
EARLY = 7
HALFWAY = 7
TINY = 2.0 ** -40
RING = 5
PMR = 3
PR = 4
LAG = 3

GT = TILES // NG
BATCHES = NB * NG
STAGES = 7
BEGIN = (0, 12, 24, 39, 52, 64, 77)
PERIOD = 18
FOUND = 1
ACT_COUNTS = {1: 6, 2: 9, 3: 4, 4: 7}
POOL_SUBS = (0, 1, 3, 4, 6, 7)
AIM = TOPK - 4.5
HITS = 3.5
SPREAD = 1 / 2.75
START = 0.28
REACH = 120
SLOPE = 111
WORK = 3


def attention1():
    out = []
    for i in range(BATCHES):
        for k in range(STAGES):
            start = i * PERIOD + BEGIN[k]
            out.append((start, -k, 0, ("enter", i, k)))
            out += [(start + t, -k, 1, ("tile", i, k, t)) for t in range(GT)]
            if 0 < k < 5:
                out.append((start + GT - 1, -k, 2, ("leave", i, k)))
        for t in range(GT - 2, GT):
            out.append((i * PERIOD + BEGIN[5] + t + 2, -5, 2, ("next8", i, t)))
        out.append((i * PERIOD + BEGIN[5] + GT + 1, -5, 3, ("pick", i)))
        out.append((i * PERIOD + BEGIN[5] + GT + 1 + FOUND, -5, 4, ("found", i)))
        out.append((i * PERIOD + BEGIN[5] + GT + 2 + FOUND, -5, 5, ("hits", i)))
        for t in range(GT, GT + LAG):
            out.append((i * PERIOD + BEGIN[6] + t, -6, 2, ("drain", i, t)))
        out.append((i * PERIOD + GT, 0, 2, ("leave", i, 0)))
        out.append((i * PERIOD + BEGIN[6] + GT - 1 + LAG, -6, 3, ("leave", i, 6)))
    out.sort()
    return [(time, step) for time, _, _, step in out]


def norm(i, b):
    return [("stats", i, b), ("norm", i, b), ("turn", i, b)]


def qkv(i, b):
    return [("qk", i, b, j) for j in range(2 * NG)] + [("v", i, b)]


def att_end(i, b):
    return [("turn_att", i, b), ("proj", i, b)]


def heads0(b):
    out = []
    for h in range(NH + 3):
        out.append(("head0", b, h))
        g, last = divmod(h - 3 - (HPG - 1), HPG)
        if g >= 0 and last == 0:
            out.append(("y_copy", 0, b, g))
        if g >= 0 and last == (1 if g < NG - 1 else 0):
            out.append(("y_norm", 0, b, g))
    return out


def layer0(b):
    return (norm(0, b) + qkv(0, b) + heads0(b) + att_end(0, b)
            + norm(1, b) + [("token_sum", 1, b), ("route0", b), ("gate0", b)]
            + [("up0", b, f) for f in range(NF)] + [("down0", b, c) for c in range(3)] + [("add0", b)])


def layer1_in(b):
    return norm(2, b) + [("token_sum", 2, b)] + qkv(1, b)


def weave(a, b):
    out, placed = [], 0
    for n, x in enumerate(a):
        due = (n + 1) * len(b) // len(a)
        out += [x] + b[placed:due]
        placed = due
    return out


UPFRONT = 27
DURING_LOAD = 21
ZG = 4
STRETCH = 1.3
Y_COPY = 1
Y_NORM = 6


def experts1(b):
    out = norm(3, b) + [("gate1", b)]
    for e in range(0, E1, ZG):
        out += [("z", b, e + n) for n in range(ZG)]
        if e == 0:
            out += [("logits1", b), ("route1", b)]
        for n in range(ZG):
            out += [("up1", b, e + n), ("add1", b, e + n)]
    return out


def order():
    beside = layer0(1) + layer1_in(1)
    first = layer0(0) + layer1_in(0)
    split = first.index(("turn_att", 0, 0))
    ahead = beside.index(("head0", 1, 0))
    load = first.index(("up0", 0, 0))
    out = [("image",)] + weave(first[0:split], beside[0:ahead]) + weave(first[split:load], beside[ahead:ahead + DURING_LOAD])
    out += weave(first[load:], beside[ahead + DURING_LOAD:ahead + UPFRONT])
    beside = beside[ahead + UPFRONT:]
    steps = attention1()
    placed, turning, later, copies = 0, False, [], []
    room = len([n for n, (s, _) in enumerate(steps) if s < NG * PERIOD + BEGIN[0]])
    begun = 0
    for n, (s, step) in enumerate(steps):
        out.append(step)
        if step[0] in ("enter", "leave") and step[2] == STAGES - 1:
            turning = step[0] == "enter"
        due = (n + 1 - begun) * len(beside) // room
        while placed < min(due, len(beside)) and not (turning and beside[placed][0] in ("up0", "gate1", "z")):
            out.append(beside[placed])
            placed += 1
            while beside[placed - 1][0] in ("gate1", "z") and placed < len(beside) and beside[placed][0] == "z":
                out.append(beside[placed])
                placed += 1
        if step[0] == "leave" and step[2] == STAGES - 1:
            copies.append((s + (Y_COPY if step[1] < BATCHES - 1 else 0), step[1]))
            later.append((s + (Y_NORM if step[1] < BATCHES - 1 else 0), step[1]))
        if copies and s >= copies[0][0]:
            out.append(("y_copy", 1, *divmod(copies.pop(0)[1], NG)))
        if later and s >= later[0][0]:
            b, g = divmod(later.pop(0)[1], NG)
            out.append(("y_norm", 1, b, g))
            if g == NG - 1:
                out += att_end(1, b)
                if b == 0:
                    assert placed == len(beside)
                    beside, placed, begun, room = experts1(0), 0, n, int((len(steps) - n) * STRETCH)
    rest = beside[placed:]
    second = experts1(1)
    lead = second.index(("gate1", 1))
    return out + weave(second[0:lead], rest) + [("finish", 0)] + second[lead:] + [("finish", 1)]


ORDER = order()


def counted_by():
    out, act, dve = {}, 0, 0
    for name, *args in ORDER:
        if name == "tile" and args[1] in ACT_COUNTS:
            i, k, t = args
            act += t < ACT_COUNTS[k]
            dve += t >= ACT_COUNTS[k]
            out[i, k] = (act, dve)
    return out


def tile_heads():
    out = []
    for g in range(NG):
        for hh in range(HPG):
            out += [(g, hh, 0), (g, hh, 1)]
        out.append((g, None, 2))
    return out


def plan_banks():
    keys = []
    for name, *args in ORDER:
        if name == "image":
            keys += [("pair", 0, j) for j in range(EARLY)] + [("t1",), ("t2",)]
            keys += [("pair", 0, j) for j in range(EARLY, PICKS[0])] + [("o1",), ("o2",), ("t0", 0)]
            keys += [("pair", 1, j) for j in range(PICKS[1])]
            keys += [("y", 0, b) for b in range(NB)] + [("t0", 1)] + [("h", 0, b) for b in range(NB)]
            keys += [(name, 1, b) for name in ("y", "h") for b in range(NB)]
        elif name in ("turn", "turn_att", "v", "proj", "z"):
            keys += [(name, *args, part) for part in range(2)]
        elif name == "down0":
            if args[0] == 0 and args[1] != 1:
                keys += [("down0", 0, args[1] // 2)]
        elif (name, args[0]) == ("up1", 1):
            keys += [(name, *args, part) for part in range(2)]
        elif name in ("up0", "qk", "token_sum", "y_norm", "found", "gate0", "gate1", "logits1", "route0"):
            keys += [(name, *args)]
        elif name == "head0" and args[1] < NH:
            keys += [("s0", *args)]
        elif name == "tile" and args[1] == 6 and args[2] > 0:
            keys += [("pt", args[0], args[2] - 1)]
        elif name == "drain" and args[1] == GT:
            keys += [("pt", args[0], GT - 1)]
        elif name == "tile" and args[1] == 0:
            keys += [("s1", args[0], args[2])]
    return {key: (n % RING, n // RING) for n, key in enumerate(keys)}


def fusion_program(nc, a, out):
    USES = plan_banks()
    COUNTED = counted_by()
    ctx = ExitStack()
    with ctx:
        def sb(name, shape, dt=F32):
            return ctx.enter_context(nc.sbuf_tensor(name, shape, dt))

        sems = {}

        def sem(*name):
            if name not in sems:
                sems[name] = ctx.enter_context(nc.semaphore("_".join(map(str, name))))
            return sems[name]

        ident = sb("ident", [P, P])
        ones_row = sb("ones_row", [1, P])
        ones_col = sb("ones_col", [P, 1])
        mask = sb("mask", [P, CAUSAL])
        iota8 = sb("iota8", [P, E1])
        idx = sb("idx", [P, 42], I32)
        pixels = sb("pixels", [P, PIX, LO])
        iota_lo = sb("iota_lo", [P, LO])
        mid = sb("mid", [P, 1])
        w_tok0 = sb("w_tok0", [48, 64])
        b_tok01 = sb("b_tok01", [P, 1])
        b_tok2 = sb("b_tok2", [64, 1])
        b_f = sb("b_f", [P, D])
        w_qk = [sb(f"w_qk{i}", [HF, 2, 2 * NG, P]) for i in range(2)]
        w_v = [sb(f"w_v{i}", [HF, 2, D]) for i in range(2)]
        w_o = [sb(f"w_o{i}", [HF, 2, D]) for i in range(2)]
        b_qk = sb("b_qk", [P, 2 * NG])
        b_q = sb("b_q", [P, NG])
        b_v = sb("b_v", [P, D])
        b_o = sb("b_o", [P, D])
        w_g0 = sb("w_g0", [HF, 2, E0])
        b_up0 = sb("b_up0", [P, NB, NF])
        b_dn0 = sb("b_dn0", [1, NB, D])
        w_g1 = sb("w_g1", [HF, 2, G1])
        b_g1 = sb("b_g1", [G1, 1])
        w_l1 = sb("w_l1", [G1, E1])
        b_l1 = sb("b_l1", [1, E1])
        b_z = sb("b_z", [P, E1, 2])
        gamma = sb("gamma", [P, D])
        beta = sb("beta", [P, D])

        pool_sb = sb("score_store", [P, NB, TILES * SW])
        scores = pool_sb[:].rearrange("p b (t n) -> p b t n", t=TILES)
        used = [0, 0]

        def share(b, parts, *shape):
            n = 1
            for k in shape:
                n *= k
            at = used[b]
            used[b] += n
            assert used[b] <= TILES * SW
            letters = "abcd"[0:len(shape)]
            return pool_sb[0:parts, b, at:at + n].rearrange(
                f"p ({' '.join(letters)}) -> p {' '.join(letters)}", **dict(zip(letters, shape)))

        picks = sum(PICKS)
        rows = share(1, P, picks, 2 * P).bitcast(I32)
        near = share(1, P, picks, 2 * P)
        chosen = near
        low = share(1, P, 2 * GROUP).bitcast(I32)
        low_is = share(1, P, 2 * GROUP, LO)
        picked = sb("picked", [P, 3, 2, PIX, LO])
        used[1] = 0
        w_up0 = share(1, HF, 2, F0)
        hid0 = share(1, P, NF, T)
        w_dn0 = share(1, P, NF, D)
        sq = share(1, P, PMR, CAUSAL)
        pm = share(1, P, PMR, CAUSAL)
        patch0 = share(0, P, 2, 16, NB * 3)
        patch1 = share(0, P, 8, NB * 12)
        patch2 = share(0, P, 2, NB * 48)
        seq0 = share(0, P, 2, NB, 48)
        seq1 = share(0, P, NB, 96)
        seq2 = share(0, P, NB, 96)
        t0 = share(0, 48, 2, NB, P)
        t1 = share(0, 96, NB, 2, 64)
        t2 = share(0, 96, NB, 8, 16)
        o1 = share(0, 64, NB, 64)
        o2 = share(0, 16, NB, 64)
        y_a = share(0, P, 2, NB, P)
        y_b = share(0, 64, 2, NB, P)
        w_tok1 = share(0, 96, 2, 64)
        w_tok2 = share(0, 96, 8, 64)
        wf_a = share(0, P, D)
        wf_b = share(0, 64, D)
        interp1 = share(0, 64, IMG)
        interp2 = share(0, 16, IMG)
        zT = sb("zT", [P, ZG, 2, T])
        used[0] = 0
        w_z = share(0, HF, E1, 2, D1)
        w_u = share(0, P, E1, 2, D)
        resid = sb("resid", [P, NB, 3, D])
        stats = sb("stats", [P, NB, 3, 6])
        moments = sb("moments", [P, NB, 3, 2])
        var = sb("var", [P, NB, 3])
        std = sb("std", [P, NB, 3])
        half = sb("half", [P, 3])
        rstd = sb("rstd", [P, NB, 3])
        xhat = sb("xhat", [P, NB, 3, D])
        xT = sb("xT", [HF, NB, 2, TP])
        headed = sb("headed", [P, NB, NH * T + TP - T])
        grouped = sb("grouped", [P, NB, NG, T + 2])
        vals = sb("vals", [P, NB, 3, NH, VW])
        y_sb = sb("y_sb", [P, 2, TP])
        den = sb("den", [P, 2, 3, HPG])
        rden = sb("rden", [P, 2, 3, HPG])
        att = sb("att", [P, NB, 3, D])
        attT = sb("attT", [HF, NB, 2, TP])
        lg0 = sb("lg0", [1, NB, 8])
        top0 = sb("top0", [1, NB, 8])
        arg0 = sb("arg0", [1, NB, 8], U32)
        neg0 = sb("neg0", [1, NB])
        exp0 = sb("exp0", [1, NB, E0])
        sum0 = sb("sum0", [1, NB])
        wt0 = sb("wt0", [1, NB])
        wcol0 = sb("wcol0", [P, NB])
        xmean = sb("xmean", [HF, NB, 2])
        smax = sb("smax", [P, NB, TILES])
        nbias = sb("nbias", [P, NB, TILES])
        thr = sb("thr", [P, NB, TILES])
        bracket = sb("bracket", [P, NB, 3, 2, TILES])
        side = sb("side", [P, 2, TILES])
        diff = sb("diff", [P, NB, 2, 2, TILES])
        factor = sb("factor", [P, 3])
        spread = sb("spread", [P, TILES])
        signs = sb("signs", [P, 2, T], BF16)
        marks = sb("marks", [P, 2, T], BF16)
        work = sb("work", [P, WORK, T])
        below8 = sb("below8", [P, TILES, 8])
        count_of = sb("count_of", [P, 8])
        hit8 = sb("hit8", [P, GT, 8])
        hits = sb("hits", [P, NB, NG])
        all_hits = sb("all_hits", [1, 1], I32)
        top8 = sb("top8", [P, 8])
        es = sb("es", [P, PR, T])
        ps = sb("ps", [P, PR, TP])
        psT = sb("psT", [P, PR, TP])
        gT = sb("gT", [G1, NB, TP])
        lg1 = sb("lg1", [P, NB, 3, E1])
        max1 = sb("max1", [P, NB, 3])
        e1 = sb("e1", [P, NB, 3, E1])
        z1 = sb("z1", [P, NB, 3])
        top1 = sb("top1", [P, NB, 3, 8])
        arg1 = sb("arg1", [P, NB, 3, 8], U32)
        arg1f = sb("arg1f", [P, NB, 3, 2])
        hit = sb("hit", [P, NB, 2, 3, E1])
        w1 = sb("w1", [P, NB, 3, E1])
        s1 = sb("s1", [P, NB, 3])
        acc = xhat
        fin = xhat

        banks = ctx.enter_context(nc.psum_tensor("banks", [P, 8, 512], F32))
        y_bank = [banks[:, 5 + i, 0:T] for i in range(2)]
        token_out = [banks[:, 7, 0:2 * D], banks[0:TXT, 5, 0:D]]
        bank_full = [sem("bank_full", k) for k in range(RING)]
        bank_free = [sem("bank_free", k) for k in range(RING)]

        def filled(eng, *key):
            k, n = USES[key]
            eng.wait_ge(bank_full[k], n + 1)
            return banks[:, k, :]

        def emptied(eng, *key):
            k, n = USES[key]
            eng.wait_ge(bank_free[k], n + 1)

        def free_of(*key):
            return bank_free[USES[key][0]]

        def outputs_made(eng, n):
            b, e = divmod(n, E1)
            if b == 0:
                eng.wait_ge(sem("out1_ready"), 2 * (e + 1))
            else:
                filled(eng, "up1", b, e, 1)

        block = ctx.enter_context(nc.Block())

        row_parts = ((0, 2), (2, HALFWAY), (HALFWAY, picks))
        LOADS = [
            ("idx", [(idx, "idx")]),
            ("rows0", [(mid, "mid"), (rows[:, 0:2], a["rows"][:, 0:2])]),
            ("pixels", [(iota_lo, "iota_lo"), (pixels, "pixels")]),
            ("rows1", [(rows[:, 2:HALFWAY], a["rows"][:, 2:HALFWAY])]),
            ("rows2", [(rows[:, HALFWAY:picks], a["rows"][:, HALFWAY:picks])]),
            ("tok", [(w_tok1, "w_tok1"), (w_tok2, "w_tok2"), (w_tok0, "w_tok0"), (interp1, "interp1"),
                     (interp2, "interp2"), (b_tok01, "b_tok01"), (b_tok2, "b_tok2"), (wf_a, "wf_a"),
                     (wf_b, "wf_b"), (b_f, "b_f")]),
            ("att0", [(w_qk[0], "w_qk0"), (w_v[0], "w_v0"), (w_o[0], "w_o0"), (mask, "mask")]),
            ("ffn0", [(w_g0, "w_g0")]),
            ("att1", [(w_qk[1], "w_qk1"), (w_v[1], "w_v1"), (w_o[1], "w_o1"), (b_qk, "b_qk"),
                      (b_v, "b_v"), (b_o, "b_o"), (iota8, "iota8")]),
            ("ffn1", [(w_g1, "w_g1"), (b_g1, "b_g1"), (w_l1, "w_l1"), (b_l1, "b_l1"), (b_z, "b_z"),
                      (gamma, "gamma"), (beta, "beta")]),
        ]
        N_LOADS = {k: 16 * len(v) for k, v in LOADS}

        def loaded(eng, group):
            eng.wait_ge(sem("loaded", group), N_LOADS[group])

        @block.sync
        def _(sp):
            for group, items in LOADS:
                for dst, name in items:
                    sp.dma_start(dst[:], a[name] if isinstance(name, str) else name).then_inc(sem("loaded", group), 16)
                if group == "pixels":
                    sp.wait_ge(sem("resid_zero"), 1)
                    for b in range(NB):
                        sp.dma_start(resid[0:TXT, b, 2, :], a["txt"][b]).then_inc(sem("text_in"), 16)
            for b in range(NB):
                sp.wait_ge(sem("expert_known", b), 1)
                e = sp.value_load(arg0[0:1, b, 0:1], min_val=0, max_val=E0 - 1)
                one = bass.ds(e, 1)
                done = sem("expert_in", b)
                if b:
                    filled(sp, "down0", b - 1, 1)
                sp.dma_start(w_up0, a["w_up0"][one, :, :, :].rearrange("e p c n -> (e p) c n")).then_inc(done, 16)
                sp.dma_start(b_up0[:, b, :], a["b_up0"][one, :, :].rearrange("e p n -> (e p) n")).then_inc(done, 16)
                sp.dma_start(w_dn0, a["w_dn0"][one, :, :, :].rearrange("e p c n -> (e p) c n")).then_inc(done, 16)
                sp.dma_start(b_dn0[:, b, :], a["b_dn0"][one, :]).then_inc(done, 16)
            sp.wait_ge(sem("ps_ready"), TILES)
            for e in range(E1):
                sp.dma_start(w_z[:, e], a["w_z"][:, e]).then_inc(sem("experts_in", e), 16)
                sp.dma_start(w_u[:, e], a["w_u"][:, e]).then_inc(sem("experts_in", e), 16)
            for b in range(NB):
                sp.wait_ge(sem("fin_ready", b), 3)
                sp.dma_start(out[b, 0:IMG, :].rearrange("(c p) d -> p c d", p=P), fin[:, b, 0:2, :]).then_inc(sem("stored"), 16)
                sp.dma_start(out[b, IMG:T, :], fin[0:TXT, b, 2, :]).then_inc(sem("stored"), 16)
            sp.wait_ge(sem("stored"), 64)

        @block.gpsimd
        def _(pool):
            pool.memset(resid[:, :, 2, :], 0.0).then_inc(sem("resid_zero"), 1)
            pool.memset(ident[:], 0.0).then_inc(sem("ident"), 1)
            pool.wait_ge(sem("ident"), 1)
            pool.affine_select(out=ident[:], in_=ident[:], compare_op=ALU.not_equal, fill=1.0, base=0,
                               pattern=[[-1, P]], channel_multiplier=1).then_inc(sem("ident"), 1)
            loaded(pool, "idx")

            def gather(dst, src, col, done):
                pool.indirect_dma_start(out=dst, out_offset=None, in_=src,
                                        in_offset=bass.IndirectOffsetOnAxis(ap=idx[:, col:col + 1], axis=0)).then_inc(done, 16)

            for k in range(8):
                gather(patch1[:, k, :], a["x1"], 32 + k, sem("patch1_in"))
            for k in range(2):
                gather(patch2[:, k, :], a["x2"], 40 + k, sem("patch2_in"))
            for gh in range(2):
                for s in range(2 * PICKS[gh], GROUP):
                    gather(patch0[:, gh, s, :], a["x0"], 16 * gh + s, sem("patch0_in", gh))

            pool_steps = [0]

            def step(ins):
                pool_steps[0] += 1
                ins.then_inc(sem("pool_step"), 1)

            def settle():
                pool.wait_ge(sem("pool_step"), pool_steps[0])

            step(pool.memset(half[:], 0.5))
            for n, z in enumerate((0.0, -REACH / SLOPE, REACH / SLOPE)):
                step(pool.memset(factor[:, n:n + 1], (START + z) * SPREAD))
            step(pool.memset(bracket[:, :, 1, 1, :], float(REACH)))
            step(pool.memset(bracket[:, :, 2, 1, :], -float(REACH)))
            settle()

            def first_guess(i):
                b, g = divmod(i, NG)
                cs = slice(g * GT, (g + 1) * GT)
                emptied(pool, "s1", i, GT - 1)
                mean = scores[:, b, cs, T]
                step(pool.tensor_tensor(spread[:, cs], smax[:, b, cs], mean, ALU.subtract))
                pool.tensor_scalar(nbias[:, b, cs], smax[:, b, cs], -1.0 / TINY, None, ALU.mult).then_inc(sem("nbias_ready", i), 1)
                settle()
                w = bracket[:, b, :, 0, cs]
                step(pool.tensor_tensor(w, spread[:, cs].unsqueeze(1).to_broadcast([P, 3, GT]),
                                        factor[:].unsqueeze(2).to_broadcast([P, 3, GT]), ALU.mult))
                settle()
                pool.tensor_tensor(w, w, mean.unsqueeze(1).to_broadcast([P, 3, GT]), ALU.add).then_inc(sem("guess_ready", i), 1)

            def draw_in(i, r):
                b, g = divmod(i, NG)
                cs = slice(g * GT, (g + 1) * GT)
                by_act, by_dve = COUNTED[i, r + 1]
                if by_act:
                    pool.wait_ge(sem("act_counted"), by_act)
                if by_dve:
                    pool.wait_ge(sem("dve_counted"), by_dve)
                n = ACT_COUNTS[r + 1]
                if n:
                    c = bracket[:, b, 0, 1, g * GT:g * GT + n]
                    step(pool.tensor_scalar(c, c, -0.5, T / 2 - AIM, ALU.mult, ALU.add))
                    settle()
                now = bracket[:, b, 0, :, cs]
                step(pool.tensor_scalar(side[:, 0, cs], now[:, 1, :], 0.0, None, ALU.is_gt))
                step(pool.tensor_scalar(side[:, 1, cs], now[:, 1, :], 0.0, None, ALU.is_le))
                ends = bracket[:, b, 1:3, :, cs]
                move = diff[:, b, :, :, cs]
                step(pool.tensor_tensor(move, now.unsqueeze(1).to_broadcast([P, 2, 2, GT]), ends, ALU.subtract))
                settle()
                step(pool.tensor_tensor(move, move, side[:, :, cs].unsqueeze(2).to_broadcast([P, 2, 2, GT]), ALU.mult))
                settle()
                step(pool.tensor_tensor(ends, move, ends, ALU.add))
                settle()
                step(pool.tensor_tensor(diff[:, b, 0, :, cs], bracket[:, b, 1, :, cs], bracket[:, b, 2, :, cs], ALU.subtract))
                settle()
                pool.tensor_tensor(diff[:, b, 1, 1, cs], bracket[:, b, 1, 1, cs], diff[:, b, 0, 0, cs], ALU.mult).then_inc(sem("bracket_ready", i), 1)

            def deviation(i, b):
                pool.wait_ge(sem("moments_ready", i, b), 3)
                step(pool.tensor_scalar(var[:, b, :], moments[:, b, :, 1], 1e-5, None, ALU.add))
                settle()
                pool.tensor_tensor(std[:, b, :], var[:, b, :], half[:], ALU.pow).then_inc(sem("std_ready", i, b), 1)

            def sub(i, t):
                n = i * GT + t
                pool.wait_ge(sem("marked"), n + 1)
                w = work[:, n % WORK, :]
                pool.tensor_tensor(w, scores[:, i // NG, (i % NG) * GT + t, 0:T], w, ALU.subtract).then_inc(sem("pool_subs"), 1)

            def add_to_residual(row, i, b):
                pool.wait_ge(sem("xhat_ready", i, b), 3)
                r = resid[:, b, :, :]
                pool.tensor_tensor(r, r, row[:].unsqueeze(1).to_broadcast([P, 3, D]), ALU.add).then_inc(sem("resid_plus", i, b), 1)

            for name, *args in ORDER:
                if name == "stats":
                    deviation(*args)
                elif name == "v":
                    i, b = args
                    if i == 1:
                        loaded(pool, "att1")
                        add_to_residual(b_o, 2, b)
                elif name == "gate1":
                    b, = args
                    loaded(pool, "ffn1")
                    add_to_residual(beta, 3, b)
                elif name == "tile":
                    i, k, t = args
                    if k == 5 and t in POOL_SUBS:
                        sub(i, t)
                elif name == "leave":
                    i, k = args
                    if k == 0:
                        first_guess(i)
                    elif k in ACT_COUNTS:
                        draw_in(i, k - 1)
                elif name == "finish":
                    deviation(4, *args)

        @block.scalar
        def _(act):
            def out_of(ins, *key):
                ins.then_inc(free_of(*key), 1)

            def zero_headed(b):
                act.activation(headed[:, b, :], ones_col[:].to_broadcast([P, NH * T + TP - T]), ACT.Copy, scale=0.0).then_inc(sem("pads_set"), 1)

            def image():
                act.wait_ge(sem("ones_set"), 1)
                zero_headed(1)
                for n, (start, stop) in enumerate(row_parts):
                    loaded(act, f"rows{n}")
                    act.activation(near[:, start:stop], rows[:, start:stop], ACT.Square, bias=mid[:]).then_inc(sem("near_ready"), 1)
                zero_headed(0)
                p = filled(act, "o2")
                out_of(act.activation(o2.rearrange("p b n -> p (b n)"), p[0:16, 0:NB * 64], ACT.Copy), "o2")
                for gh in range(2):
                    pt = filled(act, "t0", gh)
                    out_of(act.activation(t0[:, gh, :, :].rearrange("p b n -> p (b n)"), pt[0:48, 0:NB * P], ACT.Copy), "t0", gh)
                    for b in range(NB):
                        py = filled(act, "y", gh, b)
                        act.activation(y_a[:, gh, b, :], py[:, 0:P], ACT.Identity, bias=b_tok01[:, 0:1]).then_inc(sem("y_a_ready"), 1)
                        out_of(act.activation(y_b[:, gh, b, :], py[0:64, P:2 * P], ACT.Identity, bias=b_tok2[:, 0:1]), "y", gh, b)

            def half_out(dst, name, i, b):
                p = filled(act, name, i, b, 0)
                out_of(act.activation(dst[:, b, 0, :], p[0:HF, 0:TP], ACT.Copy), name, i, b, 0)

            def qk_out(i, b, j):
                if j // NG == i or j % NG == 1:
                    return
                if i == 1:
                    act.wait_ge(sem("b_q_ready"), 1)
                p = filled(act, "qk", i, b, j)
                for hh in range(HPG):
                    rows = slice(32 * hh, 32 * hh + 32)
                    h = j % NG * HPG + hh
                    if i == 0:
                        ins = act.activation(headed[rows, b, h * T:(h + 1) * T], p[rows, 0:T], ACT.Copy)
                    else:
                        ins = act.activation(headed[rows, b, h * T:(h + 1) * T], p[rows, 0:T], ACT.Identity, scale=0.25 * TINY,
                                             bias=b_q[rows, j:j + 1])
                out_of(ins, "qk", i, b, j)

            def square(b, h):
                n = b * NH + h
                p = filled(act, "s0", b, h)
                if n >= PMR:
                    act.wait_ge(sem("pm_ready"), n - PMR + 1)
                out_of(act.activation(sq[:, n % PMR, :], p[:, 0:CAUSAL], ACT.Square, scale=0.25, bias=ones_col[:, 0:1]), "s0", b, h)

            def expert_weight(b):
                act.wait_ge(sem("expert_known", b), 1)
                act.activation(exp0[:, b, :], lg0[:, b, 0:E0], ACT.Exp, bias=neg0[:, b:b + 1],
                               accum_out=sum0[:, b:b + 1]).then_inc(sem("sum0_ready", b), 1)

            def hidden0(b, f):
                if f == 0:
                    act.wait_ge(sem("expert_in", b), 64)
                    if b:
                        filled(act, "down0", b - 1, 1)
                p = filled(act, "up0", b, f)
                out_of(act.activation(hid0[:, f, :], p[:, 0:T], ACT.Gelu, bias=b_up0[:, b, f:f + 1]), "up0", b, f)

            def exp_tile(i, t):
                b, n = i // NG, i * GT + t
                if n >= PR:
                    act.wait_ge(sem("ps_ready"), n - PR + 1)
                at = (i % NG) * GT + t
                act.activation(es[:, n % PR, :], scores[:, b, at, 0:T], ACT.Exp, scale=1.0 / TINY,
                               bias=nbias[:, b, at:at + 1]).then_inc(sem("es_ready"), 1)

            def turn_tile(i, t):
                n = i * GT + t
                p = filled(act, "pt", i, t)
                if n >= PR:
                    act.wait_ge(sem("psT_used"), n - PR + 1)
                out_of(act.activation(psT[:, n % PR, :], p[:, 0:TP], ACT.Copy), "pt", i, t)

            def y_copy(i, b, g):
                n = b * NG + g
                if i == 0:
                    act.wait_ge(sem("pm_used"), (n + 1) * HPG)
                else:
                    act.wait_ge(sem("psT_used"), (n + 1) * GT)
                if n:
                    filled(act, "y_norm", i, *divmod(n - 1, NG))
                act.activation(y_sb[:, i, 0:T], y_bank[i], ACT.Copy).then_inc(sem("y_copied", i), 1)

            signs_made = [0]

            def sign_tile(i, t):
                n, b, at = signs_made[0], i // NG, (i % NG) * GT + t
                if n >= 2:
                    act.wait_ge(sem("act_counted"), n - 1)
                act.activation(signs[:, n % 2, :], scores[:, b, at, 0:T], ACT.Sign, scale=-1.0, bias=bracket[:, b, 0, 0, at:at + 1],
                               accum_out=bracket[:, b, 0, 1, at:at + 1]).then_inc(sem("act_counted"), 1)
                signs_made[0] += 1

            def gate1(b):
                p = filled(act, "gate1", b)
                out_of(act.activation(gT[:, b, 0:T], p[0:G1, 0:T], ACT.Gelu, bias=b_g1[:, 0:1]), "gate1", b)

            def exp_logits(b):
                emptied(act, "logits1", b)
                act.activation(e1[:, b, :, :], lg1[:, b, :, :], ACT.Exp).then_inc(sem("e1_ready", b), 1)

            def hidden1(b, e):
                n = b * E1 + e
                for c in range(2):
                    p = filled(act, "z", b, e, c)
                    if n >= ZG:
                        outputs_made(act, n - ZG)
                    out_of(act.activation(zT[:, n % ZG, c, :], p[:, 0:T], ACT.Gelu, bias=b_z[:, e, c:c + 1]), "z", b, e, c)

            for name, *args in ORDER:
                if name == "image":
                    image()
                elif name == "turn":
                    half_out(xT, "turn", *args)
                elif name == "qk":
                    qk_out(*args)
                elif name == "head0":
                    b, h = args
                    if h < NH:
                        square(b, h)
                elif name == "y_copy":
                    y_copy(*args)
                elif name == "turn_att":
                    half_out(attT, "turn_att", *args)
                elif name == "route0":
                    expert_weight(*args)
                elif name == "up0":
                    hidden0(*args)
                elif name == "enter":
                    i, k = args
                    if k == 6:
                        act.wait_ge(sem("nbias_ready", i), 1)
                    elif k in ACT_COUNTS and ACT_COUNTS[k]:
                        act.wait_ge(sem("guess_ready", i), k)
                elif name == "tile":
                    i, k, t = args
                    if k == 6:
                        exp_tile(i, t)
                        if t >= 2:
                            turn_tile(i, t - 2)
                    elif k in ACT_COUNTS and t < ACT_COUNTS[k]:
                        sign_tile(i, t)
                elif name == "drain":
                    i, t = args
                    if t - 2 < GT:
                        turn_tile(i, t - 2)
                elif name == "gate1":
                    gate1(*args)
                elif name == "route1":
                    exp_logits(*args)
                elif name == "z":
                    hidden1(*args)

        @block.tensor
        def _(pe):
            def bank(*key):
                k, n = USES[key]
                if n:
                    pe.wait_ge(bank_free[k], n)
                return banks[:, k, :]

            def full(mm, *key):
                mm.then_inc(bank_full[USES[key][0]], 1)

            def pick_pixels(gh, start, stop):
                for j in range(start, stop):
                    n = gh * PICKS[0] + j
                    pe.wait_ge(sem("chosen_ready"), 1 + (n >= 2) + (n >= HALFWAY))
                    p = bank("pair", gh, j)
                    for k in range(2):
                        mm = pe.matmul(p[:, k * PIX * LO:(k + 1) * PIX * LO], chosen[:, n, k * P:(k + 1) * P], pixels.rearrange("p f l -> p (f l)"),
                                       start=True, stop=True)
                    full(mm, "pair", gh, j)

            def image():
                pick_pixels(0, 0, EARLY)
                pe.wait_ge(sem("ident"), 2)
                pe.wait_ge(sem("seq1_ready"), 1)
                p = bank("t1")
                for b in range(NB):
                    mm = pe.transpose(p[0:96, b * P:(b + 1) * P], seq1[:, b, :], ident[:])
                full(mm, "t1")
                pe.wait_ge(sem("seq2_ready"), 1)
                p = bank("t2")
                for b in range(NB):
                    mm = pe.transpose(p[0:96, b * P:(b + 1) * P], seq2[:, b, :], ident[:])
                full(mm, "t2")
                pick_pixels(0, EARLY, PICKS[0])
                loaded(pe, "tok")
                emptied(pe, "t1")
                p = bank("o1")
                for b in range(NB):
                    for k in range(2):
                        mm = pe.matmul(p[0:64, b * 64:b * 64 + 64], t1[:, b, k, :], w_tok1[:, k, :], start=(k == 0), stop=(k == 1))
                full(mm, "o1")
                emptied(pe, "t2")
                p = bank("o2")
                for b in range(NB):
                    for k in range(8):
                        mm = pe.matmul(p[0:16, b * 64:b * 64 + 64], t2[:, b, k, :], w_tok2[:, k, :], start=(k == 0), stop=(k == 7))
                full(mm, "o2")
                turn_pixels(0)
                pick_pixels(1, 0, PICKS[1])
                emptied(pe, "o1")
                emptied(pe, "o2")
                levels(0)
                turn_pixels(1)
                fuse(0)
                levels(1)
                fuse(1)

            def turn_pixels(gh):
                pe.wait_ge(sem("seq0_ready"), gh + 1)
                p = bank("t0", gh)
                for b in range(NB):
                    mm = pe.transpose(p[0:48, b * P:(b + 1) * P], seq0[:, gh, b, :], ident[:])
                full(mm, "t0", gh)

            def levels(gh):
                half = slice(gh * P, gh * P + P)
                emptied(pe, "t0", gh)
                for b in range(NB):
                    p = bank("y", gh, b)
                    pe.matmul(p[0:64, 0:P], w_tok0[:], t0[:, gh, b, :], start=True, stop=True)
                    pe.matmul(p[64:128, 0:P], o1[:, b, :], interp1[:, half], start=True, stop=True)
                    full(pe.matmul(p[0:64, P:2 * P], o2[:, b, :], interp2[:, half], start=True, stop=True), "y", gh, b)

            def fuse(gh):
                for b in range(NB):
                    p = bank("h", gh, b)
                    emptied(pe, "y", gh, b)
                    pe.matmul(p[:, 0:D], y_a[:, gh, b, :], wf_a[:], start=True, stop=False)
                    full(pe.matmul(p[:, 0:D], y_b[:, gh, b, :], wf_b[:], start=False, stop=True), "h", gh, b)

            def turn(src, name, i, b):
                for kc in range(2):
                    p = bank(name, i, b, kc)
                    for c in range(3):
                        mm = pe.transpose(p[0:HF, c * P:(c + 1) * P], src[:, b, c, kc * HF:(kc + 1) * HF], ident[:])
                    full(mm, name, i, b, kc)

            def turned(i, b):
                for part in range(2):
                    emptied(pe, "turn", i, b, part)

            def token_sum(i, b):
                p = bank("token_sum", i, b)
                for kc in range(2):
                    for c in range(3):
                        n = SIZES[c]
                        mm = pe.matmul(p[0:HF, kc:kc + 1], xhat[0:n, b, c, kc * HF:(kc + 1) * HF], ones_col[0:n, :],
                                       start=(c == 0), stop=(c == 2))
                full(mm, "token_sum", i, b)

            def qk_step(i, b, j):
                loaded(pe, f"att{i}")
                turned(2 * i, b)
                if i and j == NG:
                    emptied(pe, "token_sum", 2, b)
                w = T + 1 if i and j >= NG else T
                p = bank("qk", i, b, j)
                for kc in range(2):
                    mm = pe.matmul(p[:, 0:w], w_qk[i][:, kc, j, :], xT[:, b, kc, 0:w], start=(kc == 0), stop=(kc == 1))
                full(mm, "qk", i, b, j)

            def tokens_by(name, i, b, srcT, weights):
                for part in range(2):
                    p = bank(name, i, b, part)
                    for c in ((0, 1), (2,))[part]:
                        m = SIZES[c]
                        at = D * (c % 2)
                        for kc in range(2):
                            mm = pe.matmul(p[0:m, at:at + D], srcT[:, b, kc, c * P:c * P + m], weights[i][:, kc, :],
                                           start=(kc == 0), stop=(kc == 1))
                    full(mm, name, i, b, part)

            def proj(i, b):
                for kc in range(2):
                    emptied(pe, "turn_att", i, b, kc)
                tokens_by("proj", i, b, attT, w_o)

            def scores0(b, h):
                if h == 0:
                    pe.wait_ge(sem("pads_set"), 2)
                    for j in range(2 * NG):
                        emptied(pe, "qk", 0, b, j)
                p = bank("s0", b, h)
                for c in range(3):
                    at = h * T + c * P
                    mm = pe.matmul(p[:, KEYAT[c]:KEYAT[c] + KEYW[c]], headed[:, b, at:at + P], grouped[:, b, h // HPG, c * P:T],
                                   start=True, stop=True)
                full(mm, "s0", b, h)

            def values0(b, h):
                if h == 0:
                    for part in range(2):
                        emptied(pe, "v", 0, b, part)
                    pe.wait_ge(sem("pads_set"), 2)
                n = b * NH + h
                if n and n % HPG == 0:
                    pe.wait_ge(sem("y_copied", 0), n // HPG)
                pe.wait_ge(sem("pm_ready"), n + 1)
                w = pm[:, n % PMR, :]
                r = VW * (h % HPG)
                for kc in range(3):
                    k = SIZES[kc]
                    mm = pe.matmul(y_bank[0][r:r + VW, kc * P:T], vals[0:k, b, kc, h, :], w[0:k, KEYAT[kc]:KEYAT[kc] + KEYW[kc]],
                                   start=(kc == 0), stop=(kc == 2), tile_position=(0, r))
                mm.then_inc(sem("pm_used"), 1)

            def turn_group(i, b, g):
                pe.wait_ge(sem("y_copied", i), b * NG + g + 1)
                p = bank("y_norm", i, b, g)
                for c in range(3):
                    mm = pe.transpose(p[:, c * P:(c + 1) * P], y_sb[:, i, c * P:(c + 1) * P], ident[:])
                full(mm, "y_norm", i, b, g)

            def route0(b):
                loaded(pe, "ffn0")
                emptied(pe, "token_sum", 1, b)
                p = bank("route0", b)
                for kc in range(2):
                    mm = pe.matmul(p[0:1, 0:E0], xmean[:, b, kc:kc + 1], w_g0[:, kc, :], start=(kc == 0), stop=(kc == 1))
                full(mm, "route0", b)

            def gate0(b):
                p = bank("gate0", b)
                pe.wait_ge(sem("wt0_ready", b), 1)
                full(pe.matmul(p[:, 0:1], ones_row[:], wt0[:, b:b + 1], start=True, stop=True), "gate0", b)

            def up0(b, f):
                if f == 0:
                    turned(1, b)
                    pe.wait_ge(sem("expert_in", b), 64)
                p = bank("up0", b, f)
                for kc in range(2):
                    mm = pe.matmul(p[:, 0:T], w_up0[:, kc, f * P:(f + 1) * P], xT[:, b, kc, 0:T], start=(kc == 0), stop=(kc == 1))
                full(mm, "up0", b, f)

            def down0(b, c):
                if c == 0:
                    for f in range(NF):
                        emptied(pe, "up0", b, f)
                    if b:
                        pe.wait_ge(sem("y_copied", 0), NB * NG)
                part, m, at = c // 2, SIZES[c], D * (c % 2)
                p = token_out[part] if b else bank("down0", b, part)
                for f in range(NF):
                    pe.matmul(p[0:m, at:at + D], hid0[:, f, c * P:c * P + m], w_dn0[:, f, :], start=(f == 0), stop=False)
                mm = pe.matmul(p[0:m, at:at + D], ones_row[:, 0:m], b_dn0[:, b, :], start=False, stop=True)
                if c == 0:
                    return
                if b:
                    mm.then_inc(sem("down_ready"), 1)
                else:
                    full(mm, "down0", b, part)

            def scores1(i, t):
                b, at = divmod(i * GT + t, TILES)
                if at == 0:
                    for j in range(2 * NG):
                        emptied(pe, "qk", 1, b, j)
                g, hh, c = tile_heads()[at]
                p = bank("s1", i, t)
                for one in ([hh] if hh is not None else range(HPG)):
                    m = SIZES[c]
                    to = 0 if hh is not None else 32 * one
                    start = (g * HPG + one) * T + c * P
                    mm = pe.matmul(p[to:to + m, 0:T + 1], headed[:, b, start:start + m], grouped[:, b, g, 0:T + 1],
                                   start=True, stop=True, tile_position=(0, to))
                full(mm, "s1", i, t)

            def turn_probs(i, t):
                n = i * GT + t
                pe.wait_ge(sem("ps_ready"), n + 1)
                p = bank("pt", i, t)
                for kc in range(3):
                    mm = pe.transpose(p[:, kc * P:(kc + 1) * P], ps[:, n % PR, kc * P:(kc + 1) * P], ident[:])
                full(mm, "pt", i, t)

            def values1(i, t):
                n = i * GT + t
                b, at = divmod(n, TILES)
                if at == 0:
                    for part in range(2):
                        emptied(pe, "v", 1, b, part)
                if t == 0 and i:
                    pe.wait_ge(sem("y_copied", 1), i)
                g, hh, c = tile_heads()[at]
                emptied(pe, "pt", i, t)
                m = SIZES[c]
                for one in ([hh] if hh is not None else range(HPG)):
                    h = g * HPG + one
                    col = 0 if hh is not None else 32 * one
                    r = VW * one
                    for kc in range(3):
                        k = SIZES[kc]
                        mm = pe.matmul(y_bank[1][r:r + VW, c * P:c * P + m], vals[0:k, b, kc, h, :],
                                       psT[0:k, n % PR, kc * P + col:kc * P + col + m],
                                       start=(kc == 0), stop=(kc == 2), tile_position=(0, r))
                mm.then_inc(sem("psT_used"), 1)

            def sum_hits(i):
                pe.wait_ge(sem("hits_ready"), i + 1)
                p = bank("found", i)
                full(pe.matmul(p[0:1, 0:1], hits[:, i // NG, i % NG:i % NG + 1], ones_col[:], start=True, stop=True), "found", i)

            def gate1(b):
                loaded(pe, "ffn1")
                turned(3, b)
                p = bank("gate1", b)
                for kc in range(2):
                    mm = pe.matmul(p[0:G1, 0:T], w_g1[:, kc, :], xT[:, b, kc, 0:T], start=(kc == 0), stop=(kc == 1))
                full(mm, "gate1", b)

            def logits1(b):
                p = bank("logits1", b)
                emptied(pe, "gate1", b)
                for c in range(3):
                    pe.matmul(p[:, c * E1:(c + 1) * E1], gT[:, b, c * P:(c + 1) * P], w_l1[:], start=True, stop=False)
                    mm = pe.matmul(p[:, c * E1:(c + 1) * E1], ones_row[:], b_l1[:], start=False, stop=True)
                full(mm, "logits1", b)

            def z_step(b, e):
                pe.wait_ge(sem("experts_in", e), 32)
                for f in range(2):
                    p = bank("z", b, e, f)
                    for kc in range(2):
                        mm = pe.matmul(p[:, 0:T], w_z[:, e, kc, f * P:(f + 1) * P], xT[:, b, kc, 0:T], start=(kc == 0), stop=(kc == 1))
                    full(mm, "z", b, e, f)

            def up1(b, e):
                n = b * E1 + e
                for f in range(2):
                    emptied(pe, "z", b, e, f)
                if b == 0:
                    pe.wait_ge(*((sem("out1_added"), 2 * e) if e else (sem("down_added"), 2)))
                for part in range(2):
                    p = bank("up1", b, e, part) if b else token_out[part]
                    for c in ((0, 1), (2,))[part]:
                        m = SIZES[c]
                        at = D * (c % 2)
                        for f in range(2):
                            mm = pe.matmul(p[0:m, at:at + D], zT[:, n % ZG, f, c * P:c * P + m], w_u[:, e, f, :],
                                           start=(f == 0), stop=(f == 1))
                    if b:
                        full(mm, "up1", b, e, part)
                    else:
                        mm.then_inc(sem("out1_ready"), 1)

            for name, *args in ORDER:
                if name == "image":
                    image()
                elif name == "turn":
                    pe.wait_ge(sem("xhat_ready", *args), 3)
                    turn(xhat, "turn", *args)
                elif name == "token_sum":
                    token_sum(*args)
                elif name == "qk":
                    qk_step(*args)
                elif name == "v":
                    tokens_by("v", *args, xT, w_v)
                elif name == "head0":
                    b, h = args
                    if h < NH:
                        scores0(b, h)
                    if h >= 3:
                        values0(b, h - 3)
                elif name == "y_norm":
                    turn_group(*args)
                elif name == "turn_att":
                    for g in range(NG):
                        emptied(pe, "y_norm", *args, g)
                    turn(att, "turn_att", *args)
                elif name == "proj":
                    proj(*args)
                elif name == "route0":
                    route0(*args)
                elif name == "gate0":
                    gate0(*args)
                elif name == "up0":
                    up0(*args)
                elif name == "down0":
                    down0(*args)
                elif name == "tile":
                    i, k, t = args
                    if k == 6:
                        if t >= 1:
                            turn_probs(i, t - 1)
                        if t >= LAG:
                            values1(i, t - LAG)
                    elif k == 0:
                        scores1(i, t)
                elif name == "drain":
                    i, t = args
                    if t == GT:
                        turn_probs(i, t - 1)
                    values1(i, t - LAG)
                elif name == "found":
                    sum_hits(*args)
                elif name == "gate1":
                    gate1(*args)
                elif name == "logits1":
                    logits1(*args)
                elif name == "z":
                    z_step(*args)
                elif name == "up1":
                    up1(*args)

        @block.vector
        def _(dve):
            steps = [0]

            def step(ins):
                steps[0] += 1
                ins.then_inc(sem("dve_step"), 1)

            def settle():
                dve.wait_ge(sem("dve_step"), steps[0])

            def out_of(ins, *key):
                ins.then_inc(free_of(*key), 1)

            dve.memset(ones_row[:], 1.0)
            dve.memset(ones_col[:], 1.0).then_inc(sem("ones_set"), 1)
            dve.memset(vals[:], 1.0).then_inc(sem("vals_set"), 1)
            dve.memset(y_sb[:, :, T:TP], 1.0)
            dve.memset(ps[:, :, T:TP], 0.0)
            dve.memset(gT[:, :, T:TP], 0.0)
            dve.memset(lg0[:], -3e38).then_inc(sem("lg0_set"), 1)

            def by_sequence(dst, src, f, done):
                dve.tensor_copy(dst.rearrange("p b (k f) -> p k b f", f=f), src.rearrange("p k (b f) -> p k b f", b=NB)).then_inc(done, 1)

            def sum_pixels(gh, start, stop):
                for j in range(start, stop + 1):
                    if j < stop:
                        p = filled(dve, "pair", gh, j)
                        if j < start + 3:
                            settle()
                        else:
                            dve.wait_ge(sem("dve_step"), steps[0] - 1)
                        out_of(dve.tensor_tensor(picked[:, j % 3], p[:, 0:2 * PIX * LO].rearrange("p (k f l) -> p k f l", k=2, f=PIX),
                                                 low_is[:, gh * GROUP + 2 * j:gh * GROUP + 2 * j + 2].unsqueeze(2).to_broadcast([P, 2, PIX, LO]),
                                                 ALU.mult), "pair", gh, j)
                    if j > start:
                        emptied(dve, "pair", gh, j - 1)
                        step(dve.tensor_reduce(patch0[:, gh, 2 * j - 2:2 * j, :], picked[:, (j - 1) % 3], AX.X, ALU.add))

            def image():
                loaded(dve, "pixels")
                loaded(dve, "idx")
                step(dve.tensor_scalar(low, idx[:, 0:2 * GROUP], LO - 1, None, ALU.bitwise_and))
                settle()
                step(dve.tensor_tensor(low_is, low.unsqueeze(2).to_broadcast([P, 2 * GROUP, LO]),
                                       iota_lo[:].unsqueeze(1).to_broadcast([P, 2 * GROUP, LO]), ALU.is_equal))
                choose(0)
                choose(1)
                sum_pixels(0, 0, EARLY)
                choose(2)
                dve.wait_ge(sem("patch1_in"), 128)
                by_sequence(seq1, patch1, 12, sem("seq1_ready"))
                dve.wait_ge(sem("patch2_in"), 32)
                by_sequence(seq2, patch2, 48, sem("seq2_ready"))
                p = filled(dve, "t1")
                out_of(dve.tensor_copy(t1.rearrange("p b k n -> p (b k n)"), p[0:96, 0:NB * P]), "t1")
                p = filled(dve, "t2")
                out_of(dve.tensor_copy(t2.rearrange("p b k n -> p (b k n)"), p[0:96, 0:NB * P]), "t2")
                sum_pixels(0, EARLY, PICKS[0])
                order_pixels(0)
                p = filled(dve, "o1")
                out_of(dve.tensor_copy(o1.rearrange("p b n -> p (b n)"), p[0:64, 0:NB * 64]), "o1")
                sum_pixels(1, 0, PICKS[1])
                order_pixels(1)
                for b in range(NB):
                    tokens_out(0, b)

            def tokens_out(gh, b):
                p = filled(dve, "h", gh, b)
                out_of(dve.tensor_tensor(resid[:, b, gh, :], p[:, 0:D], b_f[:], ALU.add), "h", gh, b)

            def choose(n):
                start, stop = row_parts[n]
                dve.wait_ge(sem("near_ready"), n + 1)
                dve.tensor_scalar(chosen[:, start:stop], near[:, start:stop], (LO / 2) ** 2, None, ALU.is_lt).then_inc(sem("chosen_ready"), 1)

            def order_pixels(gh):
                if PICKS[gh] < GROUP // 2:
                    dve.wait_ge(sem("patch0_in", gh), 16 * (GROUP - 2 * PICKS[gh]))
                settle()
                by_sequence(seq0[:, gh, :, :], patch0[:, gh, :, :], 3, sem("seq0_ready"))

            def moments_of(i, b):
                settle()
                for c in range(3):
                    dve.bn_aggr(moments[:, b, c, :], stats[:, b, c, :]).then_inc(sem("moments_ready", i, b), 1)

            def stats_step(i, b):
                if i == 0:
                    dve.wait_ge(sem("text_in"), 32)
                    emptied(dve, "h", 0, b)
                    for c in (2, 0):
                        step(dve.bn_stats(stats[:, b, c, :], resid[:, b, c, :]))
                    tokens_out(1, b)
                    emptied(dve, "h", 1, b)
                    step(dve.bn_stats(stats[:, b, 1, :], resid[:, b, 1, :]))
                else:
                    if i == 2 and b:
                        dve.wait_ge(sem("down_added"), 2)
                    else:
                        for part in range(2):
                            emptied(dve, *(("proj", 0, b), ("down0", b), ("proj", 1, b))[i - 1], part)
                    for c in range(3):
                        step(dve.bn_stats(stats[:, b, c, :], resid[:, b, c, :]))
                moments_of(i, b)

            def normed(i, b, src, dst):
                dve.wait_ge(sem("std_ready", i, b), 1)
                step(dve.reciprocal(rstd[:, b, :], std[:, b, :]))
                settle()
                for c in range(3):
                    dve.tensor_scalar(dst[:, b, c, :], src[:, b, c, :], moments[:, b, c, 0:1], rstd[:, b, c:c + 1],
                                      ALU.subtract, ALU.mult).then_inc(sem("xhat_ready", i, b), 1)

            def half_out(dst, name, i, b):
                p = filled(dve, name, i, b, 1)
                out_of(dve.tensor_copy(dst[:, b, 1, :], p[0:HF, 0:TP]), name, i, b, 1)

            def means(i, b):
                p = filled(dve, "token_sum", i, b)
                if i == 1:
                    out_of(dve.tensor_scalar(xmean[:, b, :], p[0:HF, 0:2], 1.0 / T, None, ALU.mult), "token_sum", i, b)
                else:
                    emptied(dve, "turn", 2, b, 0)
                    emptied(dve, "turn", 2, b, 1)
                    out_of(dve.tensor_scalar(xT[:, b, :, T], p[0:HF, 0:2], 1.0 / T, None, ALU.mult), "token_sum", i, b)

            def qk_out(i, b, j):
                if j // NG == i:
                    p = filled(dve, "qk", i, b, j)
                    if i == 0:
                        ins = dve.tensor_copy(grouped[:, b, j % NG, 0:T], p[:, 0:T])
                    else:
                        ins = dve.tensor_scalar(grouped[:, b, j % NG, 0:T + 1], p[:, 0:T + 1], b_qk[:, j:j + 1], None, ALU.add)
                    out_of(ins, "qk", i, b, j)
                elif j % NG == 1:
                    dve.wait_ge(sem("pads_set"), 2)
                    p = filled(dve, "qk", i, b, j)
                    for hh in range(HPG):
                        rows = slice(32 * hh, 32 * hh + 32)
                        h = j % NG * HPG + hh
                        dst = headed[rows, b, h * T:(h + 1) * T]
                        if i == 0:
                            ins = dve.tensor_copy(dst, p[rows, 0:T])
                        else:
                            ins = dve.tensor_scalar(dst, p[rows, 0:T], 0.25 * TINY, b_q[rows, j:j + 1], ALU.mult, ALU.add)
                    out_of(ins, "qk", i, b, j)

            def weigh(b, h):
                n = b * NH + h
                emptied(dve, "s0", b, h)
                if n >= PMR:
                    dve.wait_ge(sem("pm_used"), n - PMR + 1)
                dve.scalar_tensor_tensor(pm[:, n % PMR, :], sq[:, n % PMR, :], 1.0, mask[:], ALU.add, ALU.mult).then_inc(sem("pm_ready"), 1)

            def values(i, b):
                p = filled(dve, "v", i, b, 0)
                v = vals[:, b, 0:2, :, 0:HD]
                y = p[:, 0:2 * D].rearrange("p (c h w) -> p c h w", c=2, h=NH)
                bias = b_v[:].rearrange("p (h w) -> p h w", h=NH)
                if i == 0:
                    out_of(dve.tensor_copy(v, y), "v", i, b, 0)
                else:
                    dve.tensor_tensor(v[:, 0], y[:, 0], bias, ALU.add)
                    out_of(dve.tensor_tensor(v[:, 1], y[:, 1], bias, ALU.add), "v", i, b, 0)
                p = filled(dve, "v", i, b, 1)
                v = vals[0:TXT, b, 2, :, 0:HD]
                y = p[0:TXT, 0:D].rearrange("p (h w) -> p h w", h=NH)
                if i == 0:
                    out_of(dve.tensor_copy(v, y), "v", i, b, 1)
                else:
                    out_of(dve.tensor_tensor(v, y, bias[0:TXT], ALU.add), "v", i, b, 1)

            def normalize(i, b, g):
                p = filled(dve, "y_norm", i, b, g)
                y = p[:, 0:TP].rearrange("p (c h w) -> p c h w", c=3, h=HPG)
                step(dve.tensor_scalar(den[:, i, :, :], y[:, :, :, HD], (2e-12, 0.0)[i], None, ALU.add))
                settle()
                step(dve.reciprocal(rden[:, i, :, :], den[:, i, :, :]))
                settle()
                ins = dve.tensor_tensor(att[:, b, :, g * HPG * HD:(g + 1) * HPG * HD].rearrange("p c (h w) -> p c h w", h=HPG),
                                        y[:, :, :, 0:HD], rden[:, i, :, :].unsqueeze(3).to_broadcast([P, 3, HPG, HD]), ALU.mult)
                out_of(ins, "y_norm", i, b, g)

            def add_projection(i, b):
                if i == 1:
                    dve.wait_ge(sem("resid_plus", 2, b), 1)
                p = filled(dve, "proj", i, b, 0)
                r = resid[:, b, 0:2, :].rearrange("p c n -> p (c n)")
                out_of(dve.tensor_tensor(r, p[:, 0:2 * D], r, ALU.add), "proj", i, b, 0)
                p = filled(dve, "proj", i, b, 1)
                r = resid[0:TXT, b, 2, :]
                out_of(dve.tensor_tensor(r, p[0:TXT, 0:D], r, ALU.add), "proj", i, b, 1)

            def route0(b):
                p = filled(dve, "route0", b)
                out_of(dve.tensor_copy(lg0[:, b, 0:E0], p[0:1, 0:E0]), "route0", b)
                emptied(dve, "route0", b)
                step(dve.max(top0[:, b, :], lg0[:, b, :]))
                settle()
                step(dve.max_index(arg0[:, b, :], top0[:, b, :], lg0[:, b, :]))
                settle()
                dve.tensor_scalar(neg0[:, b:b + 1], top0[:, b, 0:1], -1.0, None, ALU.mult).then_inc(sem("expert_known", b), 1)

            def gate0(b):
                dve.wait_ge(sem("sum0_ready", b), 1)
                dve.reciprocal(wt0[:, b:b + 1], sum0[:, b:b + 1]).then_inc(sem("wt0_ready", b), 1)
                p = filled(dve, "gate0", b)
                out_of(dve.tensor_copy(wcol0[:, b:b + 1], p[:, 0:1]), "gate0", b)

            def add_expert0(b):
                emptied(dve, "gate0", b)
                for part in range(2):
                    m = SIZES[2 * part]
                    if b:
                        dve.wait_ge(sem("down_ready"), part + 1)
                        p = token_out[part]
                    else:
                        p = filled(dve, "down0", b, part)
                    r = resid[0:m, b, 0:2, :] if part == 0 else resid[0:m, b, 2:3, :]
                    r = r.rearrange("p c n -> p (c n)")
                    ins = dve.scalar_tensor_tensor(r, p[0:m, 0:D * (2 - part)], wcol0[0:m, b:b + 1], r, ALU.mult, ALU.add)
                    if b:
                        ins.then_inc(sem("down_added"), 1)
                    else:
                        out_of(ins, "down0", b, part)

            def pick_exactly(b, g):
                rounds = (TOPK + 7) // 8
                with dve.Fori(0, GT) as t:
                    dve.sem_clear(sem("pick_step"))
                    dve.tensor_copy(work[:, 0, :], scores[:, b, g * GT:(g + 1) * GT, 0:T][:, bass.ds(t, 1), :].rearrange("p a n -> p (a n)")).then_inc(sem("pick_step"), 1)
                    n = 1
                    for r in range(rounds):
                        dve.wait_ge(sem("pick_step"), n)
                        dve.max(top8[:], work[:, r % 2, :]).then_inc(sem("pick_step"), 1)
                        n += 1
                        dve.wait_ge(sem("pick_step"), n)
                        if r < rounds - 1:
                            dve.match_replace(work[:, (r + 1) % 2, :], top8[:], work[:, r % 2, :], -3e38).then_inc(sem("pick_step"), 1)
                            n += 1
                    at = (TOPK - 1) % 8
                    dve.tensor_copy(thr[:, b, g * GT:(g + 1) * GT][:, bass.ds(t, 1)], top8[:, at:at + 1]).then_inc(sem("pick_step"), 1)
                    dve.wait_ge(sem("pick_step"), n + 1)

            def tile_row(i, t):
                return scores[:, i // NG, (i % NG) * GT + t, 0:T]

            def row_max(i, t):
                b, at = divmod(i * GT + t, TILES)
                p = filled(dve, "s1", i, t)
                out_of(dve.tensor_scalar(scores[:, b, at, 0:T + 1], p[:, 0:T + 1], 1.0, None, ALU.mult, ALU.max,
                                         accum_out=smax[:, b, at:at + 1]), "s1", i, t)

            def next_guess(i, r):
                b, g = divmod(i, NG)
                cs = slice(g * GT, (g + 1) * GT)
                dve.wait_ge(sem("bracket_ready", i), r)
                q = diff[:, b, 1, 0, cs]
                step(dve.reciprocal(q, diff[:, b, 0, 1, cs]))
                settle()
                step(dve.tensor_tensor(q, q, diff[:, b, 1, 1, cs], ALU.mult))
                settle()
                dve.tensor_tensor(bracket[:, b, 0, 0, cs], bracket[:, b, 1, 0, cs], q, ALU.subtract).then_inc(sem("guess_ready", i), 1)

            def count_into(marks, i, t):
                b, at = divmod(i * GT + t, TILES)
                return dve.tensor_scalar(marks, tile_row(i, t), bracket[:, b, 0, 0, at:at + 1], -AIM,
                                         ALU.is_ge, ALU.add, accum_out=bracket[:, b, 0, 1, at:at + 1])

            def mark(i, t):
                n = i * GT + t
                if n >= WORK:
                    settle()
                count_into(work[:, n % WORK, :], i, t).then_inc(sem("marked"), 1)

            def sub(i, t):
                n = i * GT + t
                dve.wait_ge(sem("marked"), n + 1)
                w = work[:, n % WORK, :]
                dve.tensor_tensor(w, tile_row(i, t), w, ALU.subtract).then_inc(sem("dve_subs"), 1)

            def next8(i, t):
                n = i * GT + t
                if t in POOL_SUBS:
                    dve.wait_ge(sem("pool_subs"), i * len(POOL_SUBS) + POOL_SUBS.index(t) + 1)
                else:
                    dve.wait_ge(sem("dve_subs"), n + 1 - i * len(POOL_SUBS) - len([k for k in POOL_SUBS if k < t]))
                step(dve.max(below8[:, (i % NG) * GT + t, :], work[:, n % WORK, :]))

            def pick(i):
                b, g = divmod(i, NG)
                cs = slice(g * GT, (g + 1) * GT)
                dve.wait_ge(sem("marked"), (i + 1) * GT)
                step(dve.tensor_tensor(hit8[:], count_of[:].unsqueeze(1).to_broadcast([P, GT, 8]),
                                       bracket[:, b, 0, 1, cs].unsqueeze(2).to_broadcast([P, GT, 8]), ALU.is_equal))
                settle()
                dve.tensor_reduce(hits[:, b, g:g + 1], hit8[:].rearrange("p t k -> p (t k)"), AX.X, ALU.add).then_inc(sem("hits_ready"), 1)
                step(dve.tensor_tensor(below8[:, cs, :], below8[:, cs, :], hit8[:], ALU.mult))
                settle()
                step(dve.tensor_reduce(thr[:, b, cs], below8[:, cs, :], AX.X, ALU.add))

            def copy_hits(i):
                p = filled(dve, "found", i)
                out_of(dve.tensor_copy(all_hits[:], p[0:1, 0:1]), "found", i)

            def check(i):
                emptied(dve, "found", i)
                hit_rows = dve.value_load(all_hits[0:1, 0:1], min_val=0, max_val=P * GT)
                with dve.If(hit_rows < P * GT):
                    pick_exactly(*divmod(i, NG))

            def mask_tile(i, t):
                n = i * GT + t
                at = n % TILES
                dve.wait_ge(sem("es_ready"), n + 1)
                if n >= PR:
                    filled(dve, "pt", *divmod(n - PR, GT))
                dve.scalar_tensor_tensor(ps[:, n % PR, 0:T], tile_row(i, t), thr[:, i // NG, at:at + 1], es[:, n % PR, :],
                                         ALU.is_ge, ALU.mult).then_inc(sem("ps_ready"), 1)

            marks_made = [0]

            def count(i, t):
                n = marks_made[0]
                if n >= 2:
                    dve.wait_ge(sem("dve_counted"), n - 1)
                count_into(marks[:, n % 2, :], i, t).then_inc(sem("dve_counted"), 1)
                marks_made[0] += 1

            def logits1(b):
                p = filled(dve, "logits1", b)
                pl = p[:, 0:3 * E1].rearrange("p (c e) -> p c e", c=3)
                step(dve.tensor_reduce(max1[:, b, :], pl, AX.X, ALU.max))
                settle()
                out_of(dve.tensor_tensor(lg1[:, b, :, :], pl, max1[:, b, :].unsqueeze(2).to_broadcast([P, 3, E1]), ALU.subtract), "logits1", b)
                emptied(dve, "logits1", b)
                for c in range(3):
                    step(dve.max(top1[:, b, c, :], lg1[:, b, c, :]))
                settle()
                for c in range(3):
                    step(dve.max_index(arg1[:, b, c, :], top1[:, b, c, :], lg1[:, b, c, :]))
                settle()
                step(dve.tensor_copy(arg1f[:, b, :, :], arg1[:, b, :, 0:2]))
                settle()
                for k in range(2):
                    step(dve.tensor_tensor(hit[:, b, k, :, :], iota8[:].unsqueeze(1).to_broadcast([P, 3, E1]),
                                           arg1f[:, b, :, k:k + 1].to_broadcast([P, 3, E1]), ALU.is_equal))
                settle()
                step(dve.tensor_tensor(hit[:, b, 0, :, :], hit[:, b, 0, :, :], hit[:, b, 1, :, :], ALU.add))
                settle()

            def weights1(b):
                dve.wait_ge(sem("e1_ready", b), 1)
                step(dve.tensor_tensor(w1[:, b, :, :], e1[:, b, :, :], hit[:, b, 0, :, :], ALU.mult))
                step(dve.tensor_reduce(z1[:, b, :], e1[:, b, :, :], AX.X, ALU.add))
                settle()
                step(dve.tensor_reduce(s1[:, b, :], w1[:, b, :, :], AX.X, ALU.add))
                settle()
                step(dve.scalar_tensor_tensor(s1[:, b, :], z1[:, b, :], 1e-8, s1[:, b, :], ALU.mult, ALU.add))
                settle()
                step(dve.reciprocal(s1[:, b, :], s1[:, b, :]))
                settle()
                step(dve.tensor_tensor(w1[:, b, :, :], w1[:, b, :, :], s1[:, b, :].unsqueeze(2).to_broadcast([P, 3, E1]), ALU.mult))
                settle()

            def add_expert1(b, e):
                if e:
                    sums_there(b, e - 1)

                def add(c, p):
                    m, at = SIZES[c], D * (c % 2)
                    return dve.scalar_tensor_tensor(acc[0:m, b, c, :], p[0:m, at:at + D], w1[0:m, b, c, e:e + 1],
                                                    acc[0:m, b, c, :], ALU.mult, ALU.add)

                for part in range(2):
                    if b:
                        p = filled(dve, "up1", b, e, part)
                    else:
                        dve.wait_ge(sem("out1_ready"), 2 * e + part + 1)
                        p = token_out[part]
                    if part == 0:
                        add(0, p)
                    ins = add(1 + part, p)
                    if b:
                        out_of(ins, "up1", b, e, part)
                    else:
                        ins.then_inc(sem("out1_added"), 1)

            def sums_there(b, e):
                if b:
                    emptied(dve, "up1", b, e, 0)
                    emptied(dve, "up1", b, e, 1)
                else:
                    dve.wait_ge(sem("out1_added"), 2 * (e + 1))

            def finish(b):
                sums_there(b, E1 - 1)
                for c in range(3):
                    step(dve.bn_stats(stats[:, b, c, :], acc[:, b, c, :]))
                moments_of(4, b)
                dve.wait_ge(sem("moments_ready", 4, b), 3)
                for c in range(3):
                    step(dve.scalar_tensor_tensor(fin[:, b, c, :], acc[:, b, c, :], moments[:, b, c, 0:1], gamma[:], ALU.subtract, ALU.mult))
                dve.wait_ge(sem("std_ready", 4, b), 1)
                step(dve.reciprocal(rstd[:, b, :], std[:, b, :]))
                settle()
                dve.wait_ge(sem("resid_plus", 3, b), 1)
                for c in range(3):
                    dve.scalar_tensor_tensor(fin[:, b, c, :], fin[:, b, c, :], rstd[:, b, c:c + 1], resid[:, b, c, :],
                                             ALU.mult, ALU.add).then_inc(sem("fin_ready", b), 1)

            for name, *args in ORDER:
                if name == "image":
                    image()
                    dve.wait_ge(sem("vals_set"), 1)
                    dve.wait_ge(sem("lg0_set"), 1)
                    loaded(dve, "att0")
                    loaded(dve, "att1")
                    dve.tensor_scalar(b_q[:], b_qk[:, 0:NG], 0.25 * TINY, None, ALU.mult).then_inc(sem("b_q_ready"), 1)
                    step(dve.tensor_scalar(count_of[:], iota8[:], -1.0, HITS, ALU.mult, ALU.add))
                elif name == "stats":
                    stats_step(*args)
                elif name == "norm":
                    normed(*args, resid, xhat)
                elif name == "turn":
                    half_out(xT, "turn", *args)
                elif name == "token_sum":
                    means(*args)
                elif name == "qk":
                    qk_out(*args)
                elif name == "v":
                    values(*args)
                elif name == "head0":
                    b, h = args
                    if 1 <= h <= NH:
                        weigh(b, h - 1)
                elif name == "y_norm":
                    normalize(*args)
                elif name == "turn_att":
                    half_out(attT, "turn_att", *args)
                elif name == "proj":
                    add_projection(*args)
                elif name == "route0":
                    route0(*args)
                elif name == "gate0":
                    gate0(*args)
                elif name == "add0":
                    add_expert0(*args)
                elif name == "enter":
                    i, k = args
                    if 2 <= k <= 5:
                        next_guess(i, k - 1)
                    if 1 <= k <= 5:
                        dve.wait_ge(sem("guess_ready", i), k)
                    if k == 6:
                        check(i)
                elif name == "tile":
                    i, k, t = args
                    if k == 0 and t:
                        row_max(i, t - 1)
                    elif k in ACT_COUNTS and t >= ACT_COUNTS[k]:
                        count(i, t)
                    elif k == 5:
                        if t >= 2:
                            next8(i, t - 2)
                        if t >= 1 and t - 1 not in POOL_SUBS:
                            sub(i, t - 1)
                        mark(i, t)
                    elif k == 6:
                        mask_tile(i, t)
                elif name == "next8":
                    i, t = args
                    if t == GT - 2 and GT - 1 not in POOL_SUBS:
                        sub(i, GT - 1)
                    next8(i, t)
                elif name == "leave":
                    i, k = args
                    if k == 0:
                        row_max(i, GT - 1)
                elif name == "hits":
                    copy_hits(*args)
                elif name == "pick":
                    pick(*args)
                elif name == "route1":
                    if args[0] == 0:
                        loaded(dve, "ffn1")
                    logits1(*args)
                    weights1(*args)
                elif name == "add1":
                    add_expert1(*args)
                elif name == "finish":
                    finish(*args)


def kernel(x, txt, L0_tok_W0, L0_tok_b0, L0_tok_W1, L0_tok_b1, L0_tok_W2, L0_tok_b2, L0_tok_Wf, L0_tok_bf,
           L0_tok_idx0, L0_tok_idx1, L0_tok_idx2, L0_attn_Wq, L0_attn_Wk, L0_attn_Wv, L0_attn_Wo,
           L0_ffn_Wg, L0_ffn_W1, L0_ffn_b1, L0_ffn_W2, L0_ffn_b2, L1_attn_W_qkv, L1_attn_b_qkv,
           L1_attn_W_proj, L1_attn_b_proj, L1_ffn_w1, L1_ffn_b1, L1_ffn_w2, L1_ffn_b2, L1_ffn_down_w,
           L1_ffn_down_b, L1_ffn_up_w, L1_ffn_gamma, L1_ffn_beta):
    import numpy as np
    import concourse.bacc as bacc
    from concourse.bass_utils import run_bass_kernel_spmd as run

    def patches(p):
        h = 64 // p
        return x.reshape(NB, 3, h, p, h, p).transpose(2, 4, 0, 3, 5, 1).reshape(h * h, NB * p * p * 3)

    def halves(w):
        return w.reshape(2, HF, -1).transpose(1, 0, 2)

    def heads(w):
        o = np.zeros(w.shape[:-1] + (NH, 32), w.dtype)
        o[..., 0:HD] = w.reshape(w.shape[:-1] + (NH, HD))
        return o.reshape(w.shape[:-1] + (NH * 32,))

    def interp(n):
        pos = np.clip((np.arange(IMG, dtype=np.float32) + 0.5) * (n / IMG) - 0.5, 0.0, n - 1)
        i0 = np.floor(pos).astype(np.int32)
        i1 = np.minimum(i0 + 1, n - 1)
        w = (pos - i0).astype(np.float32)
        m = np.zeros((n, IMG), np.float32)
        m[i0, np.arange(IMG)] += 1.0 - w
        m[i1, np.arange(IMG)] += w
        return m

    def qk_weights(wq, wk):
        return np.concatenate([halves(heads(wq)), halves(heads(wk))], axis=2).reshape(HF, 2, 2 * NG, P)

    tri = (np.arange(T)[None, :] >= np.arange(P)[:, None]).astype(np.float32)
    qkv_w, qkv_b = L1_attn_W_qkv, L1_attn_b_qkv
    arrays = {
        "x0": patches(1), "x1": patches(2), "x2": patches(4), "txt": txt,
        "idx": np.concatenate([
            L0_tok_idx0.reshape(2, P, 16).transpose(1, 0, 2).reshape(P, 32),
            L0_tok_idx1.reshape(64, 2, 8).transpose(1, 0, 2).reshape(P, 8),
            L0_tok_idx2.reshape(16, 8, 2).transpose(1, 0, 2).reshape(P, 2)], axis=1),
        "rows": np.broadcast_to(np.concatenate([
            L0_tok_idx0.reshape(2, P, GROUP)[gh, :, 0:2 * PICKS[gh]].T.reshape(PICKS[gh], 2 * P) for gh in range(2)]), (P, sum(PICKS), 2 * P)),
        "pixels": x.reshape(PIX, P, LO).transpose(1, 0, 2),
        "mid": -(LO * np.arange(P, dtype=np.float32) + (LO - 1) / 2)[:, None].astype(np.float32),
        "iota_lo": np.tile(np.arange(LO, dtype=np.float32), (P, 1)),
        "w_tok0": L0_tok_W0.T, "w_tok1": L0_tok_W1.T.reshape(2, 96, 64).transpose(1, 0, 2),
        "w_tok2": L0_tok_W2.T.reshape(8, 96, 64).transpose(1, 0, 2),
        "b_tok01": np.concatenate([L0_tok_b0, L0_tok_b1])[:, None], "b_tok2": L0_tok_b2[:, None],
        "wf_a": L0_tok_Wf.T[0:P], "wf_b": L0_tok_Wf.T[P:D], "b_f": np.broadcast_to(L0_tok_bf, (P, D)),
        "interp1": interp(64), "interp2": interp(16),
        "mask": np.concatenate([tri[:, 0:w] for w in KEYW], axis=1),
        "iota8": np.tile(np.arange(E1, dtype=np.float32), (P, 1)),
        "w_qk0": qk_weights(L0_attn_Wq.T, L0_attn_Wk.T), "w_v0": halves(L0_attn_Wv.T), "w_o0": halves(L0_attn_Wo.T),
        "w_qk1": qk_weights(qkv_w[:, 0:D], qkv_w[:, D:2 * D]), "w_v1": halves(qkv_w[:, 2 * D:]),
        "w_o1": halves(L1_attn_W_proj),
        "b_qk": np.concatenate([heads(qkv_b[0:D]), heads(qkv_b[D:2 * D])]).reshape(2 * NG, P).T,
        "b_v": np.broadcast_to(qkv_b[2 * D:], (P, D)), "b_o": np.broadcast_to(L1_attn_b_proj, (P, D)),
        "w_g0": halves(L0_ffn_Wg.T),
        "w_up0": L0_ffn_W1.reshape(E0, 2, HF, F0).transpose(0, 2, 1, 3),
        "b_up0": L0_ffn_b1.reshape(E0, NF, P).transpose(0, 2, 1),
        "w_dn0": L0_ffn_W2.reshape(E0, NF, P, D).transpose(0, 2, 1, 3), "b_dn0": L0_ffn_b2,
        "w_g1": halves(L1_ffn_w1), "b_g1": L1_ffn_b1[:, None], "w_l1": L1_ffn_w2, "b_l1": L1_ffn_b2[None, :],
        "w_z": L1_ffn_down_w.reshape(E1, 2, HF, D1).transpose(2, 0, 1, 3),
        "b_z": L1_ffn_down_b.reshape(E1, 2, P).transpose(2, 0, 1),
        "w_u": L1_ffn_up_w.reshape(E1, 2, P, D).transpose(2, 0, 1, 3),
        "gamma": np.broadcast_to(L1_ffn_gamma, (P, D)), "beta": np.broadcast_to(L1_ffn_beta, (P, D)),
    }
    nc = bacc.Bacc("TRN2", target_bir_lowering=False, num_devices=1)
    arrays = {f"in_{k}": np.ascontiguousarray(v) for k, v in arrays.items()}
    aps = {k[3:]: nc.dram_tensor(k, v.shape, mybir.dt.from_np(v.dtype), kind="ExternalInput").ap() for k, v in arrays.items()}
    out = nc.dram_tensor("out_0", (NB, T, D), F32, kind="ExternalOutput").ap()
    fusion_program(nc, aps, out)
    r = run(nc, [arrays], core_ids=[0])
    return r.results[0]["out_0"]
```
